# Optimizing a Trainium2 kernel written in Bass

```python
import numpy as np
import jax
import jax.numpy as jnp

def _softmax(x, axis=-1):
    return jax.nn.softmax(x, axis=axis)

def _gelu(x):
    return jax.nn.gelu(x, approximate=True)

def _silu(x):
    return jax.nn.silu(x)

def _sigmoid(x):
    return jax.nn.sigmoid(x)

def _layernorm(x, axis=-1, eps=1e-05):
    m = jnp.mean(x, axis=axis, keepdims=True)
    v = jnp.var(x, axis=axis, keepdims=True)
    return (x - m) / jnp.sqrt(v + eps)

def _scatter_add(tgt, idx, src, axis=0):
    return tgt.at[idx].add(src)

def _segment_sum(src, seg, n):
    return jax.ops.segment_sum(src, seg, n)
kernel_name = 'mk_decoder_postln_d1_seqx_r8_15dea4'

def setup_inputs(seed: int=0):
    np.random.seed(seed)
    _w = jnp.asarray

    def _rec_inputs():
        import jax
        import jax.numpy as jnp
        _rk = jax.random.key(seed)
        x = 7.22e-05 + 1 * jax.random.normal(jax.random.fold_in(_rk, 1), (32, 56, 128), jnp.float32)
        _lenS = 56 - jax.random.randint(jax.random.fold_in(_rk, 7), (32,), 0, max(1, 56 // 4) + 1, jnp.int32)
        _lenS2 = 1500 - jax.random.randint(jax.random.fold_in(_rk, 8), (32,), 0, max(1, 1500 // 4) + 1, jnp.int32)
        _ctx_1024P = jax.random.normal(jax.random.fold_in(_rk, 11), (32, 16, 128), jnp.float32)
        _ctx_1024c = jax.random.dirichlet(jax.random.fold_in(_rk, 511), 0.3 * jnp.ones((16,), jnp.float32), (32, 1500))
        _ctx_1024t = jnp.einsum('bsk,bkd->bsd', _ctx_1024c, _ctx_1024P)
        _ctx_1024t = _ctx_1024t * jax.lax.rsqrt(jnp.mean(jnp.square(_ctx_1024t)) + 1e-12) * 0.953939
        ctx_1024 = -0.000514642 + 1.00011 * (_ctx_1024t + 0.3 * jax.random.normal(jax.random.fold_in(_rk, 611), (32, 1500, 128), jnp.float32))
        return (x, ctx_1024)
    x, ctx_1024 = _rec_inputs()

    def _L0_attn_setup():
        import jax, jax.numpy as jnp
        import numpy as np
        import math
        EPS = 1e-06
        H = 16

        def favorplus_features(x, proj, eps=EPS):
            xw = jnp.einsum('bhtd,hmd->bhtm', x, proj)
            xw = xw - jnp.max(xw, axis=-1, keepdims=True)
            exp_part = jnp.exp(xw)
            x_norm_sq = jnp.sum(x * x, axis=-1, keepdims=True)
            base = jnp.exp(-0.5 * x_norm_sq)
            return exp_part * base + eps
        key = jax.random.key(seed)
        ks = jax.random.split(key, 7)
        B, T, d = (4, 512, 128)
        h, m = (H, 32)
        dk = d // h
        s = 1.0 / math.sqrt(d)
        return {'x': jax.random.normal(ks[0], (B, T, d), jnp.float32), 'Wq': jax.random.normal(ks[1], (d, d), jnp.float32) * s, 'Wk': jax.random.normal(ks[2], (d, d), jnp.float32) * s, 'Wv': jax.random.normal(ks[3], (d, d), jnp.float32) * s, 'Wo': jax.random.normal(ks[4], (d, d), jnp.float32) * s, 'bo': jnp.zeros((d,), jnp.float32), 'proj': jax.random.normal(ks[5], (h, m, dk), jnp.float32)}
    _L0_attn_all = _L0_attn_setup()
    _L0_attn_in = {k: v for k, v in _L0_attn_all.items() if k in ('Wq', 'Wk', 'Wv', 'Wo', 'bo', 'proj')}
    del _L0_attn_all

    def _L0_xattn_setup():
        import jax, jax.numpy as jnp
        import numpy as np
        B, L_ENC, L_DEC, D = (16, 64, 128, 128)
        key = jax.random.key(seed)
        k1, k2, k3, k4, k5, k6 = jax.random.split(key, 6)
        encoder_hc = jax.random.normal(k1, (B, L_ENC, D), dtype=jnp.float32)
        decoder_hq = jax.random.normal(k2, (B, L_DEC, D), dtype=jnp.float32)
        w_sim = jax.random.normal(k3, (3 * D,), dtype=jnp.float32) * 0.02
        b_sim = jax.random.normal(k4, (1,), dtype=jnp.float32) * 0.02
        W_qv = jax.random.normal(k5, (4 * D, D), dtype=jnp.float32) * 0.02
        b_qv = jax.random.normal(k6, (D,), dtype=jnp.float32) * 0.02
        return {'encoder_hc': encoder_hc, 'decoder_hq': decoder_hq, 'w_sim': w_sim, 'b_sim': b_sim, 'W_qv': W_qv, 'b_qv': b_qv}
    _L0_xattn_all = _L0_xattn_setup()
    _L0_xattn_in = {k: v for k, v in _L0_xattn_all.items() if k in ('w_sim', 'b_sim', 'W_qv', 'b_qv')}
    del _L0_xattn_all

    def _L0_ffn_setup():
        import jax, jax.numpy as jnp
        import numpy as np
        SQRT_2_PI = 0.7978845608028654
        GELU_COEF = 0.044715
        LN_EPS = 1e-06
        TOP_K = 2

        def gelu_kernel(x):
            inner = SQRT_2_PI * (x + GELU_COEF * x ** 3)
            return 0.5 * x * (1.0 + jnp.tanh(inner))
        key = jax.random.key(seed)
        ks = jax.random.split(key, 8)
        B, S, D, F, E = (2, 256, 128, 512, 8)
        s = lambda d: 1.0 / np.sqrt(d)
        return {'x': jax.random.normal(ks[0], (B, S, D), jnp.float32), 'Wr1': jax.random.normal(ks[1], (D, D // 2), jnp.float32) * s(D), 'br1': jnp.zeros((D // 2,), jnp.float32), 'ln_scale': jnp.ones((D // 2,), jnp.float32), 'ln_bias': jnp.zeros((D // 2,), jnp.float32), 'Wr2': jax.random.normal(ks[2], (D // 2, E), jnp.float32) * s(D // 2), 'br2': jnp.zeros((E,), jnp.float32), 'W1': jax.random.normal(ks[3], (E, D, 2 * F), jnp.float32) * s(D), 'b1': jnp.zeros((E, 2 * F), jnp.float32), 'W2': jax.random.normal(ks[4], (E, F, D), jnp.float32) * s(F), 'b2': jnp.zeros((E, D), jnp.float32)}
    _L0_ffn_all = _L0_ffn_setup()
    _L0_ffn_in = {k: v for k, v in _L0_ffn_all.items() if k in ('Wr1', 'br1', 'ln_scale', 'ln_bias', 'Wr2', 'br2', 'W1', 'b1', 'W2', 'b2')}
    del _L0_ffn_all
    return {'x': x, 'ctx_1024': ctx_1024, 'L0_attn_Wq': _L0_attn_in['Wq'], 'L0_attn_Wk': _L0_attn_in['Wk'], 'L0_attn_Wv': _L0_attn_in['Wv'], 'L0_attn_Wo': _L0_attn_in['Wo'], 'L0_attn_bo': _L0_attn_in['bo'], 'L0_attn_proj': _L0_attn_in['proj'], 'L0_xattn_w_sim': _L0_xattn_in['w_sim'], 'L0_xattn_b_sim': _L0_xattn_in['b_sim'], 'L0_xattn_W_qv': _L0_xattn_in['W_qv'], 'L0_xattn_b_qv': _L0_xattn_in['b_qv'], 'L0_ffn_Wr1': _L0_ffn_in['Wr1'], 'L0_ffn_br1': _L0_ffn_in['br1'], 'L0_ffn_ln_scale': _L0_ffn_in['ln_scale'], 'L0_ffn_ln_bias': _L0_ffn_in['ln_bias'], 'L0_ffn_Wr2': _L0_ffn_in['Wr2'], 'L0_ffn_br2': _L0_ffn_in['br2'], 'L0_ffn_W1': _L0_ffn_in['W1'], 'L0_ffn_b1': _L0_ffn_in['b1'], 'L0_ffn_W2': _L0_ffn_in['W2'], 'L0_ffn_b2': _L0_ffn_in['b2']}

def reference(x, ctx_1024, L0_attn_Wq, L0_attn_Wk, L0_attn_Wv, L0_attn_Wo, L0_attn_bo, L0_attn_proj, L0_xattn_w_sim, L0_xattn_b_sim, L0_xattn_W_qv, L0_xattn_b_qv, L0_ffn_Wr1, L0_ffn_br1, L0_ffn_ln_scale, L0_ffn_ln_bias, L0_ffn_Wr2, L0_ffn_br2, L0_ffn_W1, L0_ffn_b1, L0_ffn_W2, L0_ffn_b2):
    import jax
    import jax.numpy as jnp

    def _L0_attn_ref(x, Wq, Wk, Wv, Wo, bo, proj):
        import jax, jax.numpy as jnp
        import numpy as np
        import math
        EPS = 1e-06
        H = 16

        def favorplus_features(x, proj, eps=EPS):
            xw = jnp.einsum('bhtd,hmd->bhtm', x, proj)
            xw = xw - jnp.max(xw, axis=-1, keepdims=True)
            exp_part = jnp.exp(xw)
            x_norm_sq = jnp.sum(x * x, axis=-1, keepdims=True)
            base = jnp.exp(-0.5 * x_norm_sq)
            return exp_part * base + eps
        B, T, d = x.shape
        h = H
        dk = d // h
        m = proj.shape[1]

        def heads(W):
            return (x @ W.T).reshape(B, T, h, dk).transpose(0, 2, 1, 3)
        Q, K, V = (heads(Wq), heads(Wk), heads(Wv))
        scale = 1.0 / math.sqrt(dk)
        phiQ = favorplus_features(Q * scale, proj) / math.sqrt(m)
        phiK = favorplus_features(K * scale, proj) / math.sqrt(m)
        KV = jnp.einsum('bhtm,bhtd->bhmd', phiK, V)
        Ksum = jnp.sum(phiK, axis=2)
        num = jnp.einsum('bhtm,bhmd->bhtd', phiQ, KV)
        den = jnp.einsum('bhtm,bhm->bht', phiQ, Ksum)[..., None] + EPS
        out_heads = num / den
        merged = out_heads.transpose(0, 2, 1, 3).reshape(B, T, h * dk)
        return merged @ Wo.T + bo

    def _L0_xattn_ref(encoder_hc, decoder_hq, w_sim, b_sim, W_qv, b_qv):
        import jax, jax.numpy as jnp
        import numpy as np
        B, L_ENC, L_DEC, D = (16, 64, 128, 128)
        d = encoder_hc.shape[-1]
        w1, w2, w3 = (w_sim[:d], w_sim[d:2 * d], w_sim[2 * d:])
        Sim = (encoder_hc @ w1)[:, :, None] + (decoder_hq @ w2)[:, None, :] + jnp.einsum('bid,bjd->bij', encoder_hc * w3, decoder_hq) + b_sim[0]
        A = jax.nn.softmax(Sim, axis=2)
        hq_hat = jnp.einsum('bij,bjd->bid', A, decoder_hq)
        Batt = jax.nn.softmax(jnp.max(Sim, axis=2), axis=1)
        hc_bar = jnp.einsum('bi,bid->bd', Batt, encoder_hc)[:, None, :]
        hc_hat = jnp.broadcast_to(hc_bar, encoder_hc.shape)
        feats = jnp.concatenate([encoder_hc, hq_hat, encoder_hc * hq_hat, encoder_hc * hc_hat], axis=-1)
        hcq = feats @ W_qv + b_qv
        return hcq

    def _L0_ffn_ref(x, Wr1, br1, ln_scale, ln_bias, Wr2, br2, W1, b1, W2, b2):
        import jax, jax.numpy as jnp
        import numpy as np
        SQRT_2_PI = 0.7978845608028654
        GELU_COEF = 0.044715
        LN_EPS = 1e-06
        TOP_K = 2

        def gelu_kernel(x):
            inner = SQRT_2_PI * (x + GELU_COEF * x ** 3)
            return 0.5 * x * (1.0 + jnp.tanh(inner))
        E = W1.shape[0]
        h = jnp.einsum('bsd,dk->bsk', x, Wr1) + br1
        mu = jnp.mean(h, axis=-1, keepdims=True)
        var = jnp.mean((h - mu) ** 2, axis=-1, keepdims=True)
        h = (h - mu) * jax.lax.rsqrt(var + LN_EPS) * ln_scale + ln_bias
        h = gelu_kernel(h)
        router_logits = jnp.einsum('bsk,ke->bse', h, Wr2) + br2
        routing_probs = jax.nn.softmax(router_logits, axis=-1)
        top_k_probs, top_k_indices = jax.lax.top_k(routing_probs, TOP_K)
        top_k_probs = top_k_probs / jnp.sum(top_k_probs, axis=-1, keepdims=True)
        expert_mask = jnp.sum(jax.nn.one_hot(top_k_indices, E, dtype=x.dtype) * top_k_probs[..., None], axis=-2)
        output = jnp.zeros_like(x)
        for e in range(E):
            x12 = jnp.einsum('bsd,df->bsf', x, W1[e]) + b1[e]
            x1, x2 = jnp.split(x12, 2, axis=-1)
            g = x1 * gelu_kernel(x2)
            y = jnp.einsum('bsf,fd->bsd', g, W2[e]) + b2[e]
            output = output + y * expert_mask[:, :, e][:, :, None]
        return output
    x = _layernorm(x + _L0_attn_ref(x, L0_attn_Wq, L0_attn_Wk, L0_attn_Wv, L0_attn_Wo, L0_attn_bo, L0_attn_proj), axis=-1)
    x = _layernorm(x + _L0_xattn_ref(x, ctx_1024, L0_xattn_w_sim, L0_xattn_b_sim, L0_xattn_W_qv, L0_xattn_b_qv), axis=-1)
    x = _layernorm(x + _L0_ffn_ref(x, L0_ffn_Wr1, L0_ffn_br1, L0_ffn_ln_scale, L0_ffn_ln_bias, L0_ffn_Wr2, L0_ffn_br2, L0_ffn_W1, L0_ffn_b1, L0_ffn_W2, L0_ffn_b2), axis=-1)
    return x

_drawn_inputs = setup_inputs


def setup_inputs(seed=0):
    import zlib

    import numpy as np

    out = dict(_drawn_inputs(seed))
    spreads = {'L0_attn_bo': (0.0, 0.1),
     'L0_ffn_br1': (0.0, 0.1),
     'L0_ffn_ln_scale': (1.0, 0.2),
     'L0_ffn_ln_bias': (0.0, 0.1),
     'L0_ffn_br2': (0.0, 0.1),
     'L0_ffn_b1': (0.0, 0.1),
     'L0_ffn_b2': (0.0, 0.1)}
    factors = {}
    for name, (base, spread) in spreads.items():
        noise = np.random.default_rng([zlib.crc32(name.encode()), seed]).standard_normal(out[name].shape)
        drawn = base * np.exp(spread * noise) if base else spread * noise
        out[name] = jnp.asarray(drawn.astype(out[name].dtype))
    for name, factor in factors.items():
        out[name] = (out[name] * factor).astype(out[name].dtype)
    return out
```

```python
from contextlib import ExitStack

import concourse.bass as bass
from concourse import mybir

F32 = mybir.dt.float32
BF16 = mybir.dt.bfloat16
U32 = mybir.dt.uint32
ALU = mybir.AluOpType
ACT = mybir.ActivationFunctionType
AX = mybir.AxisListType

P = 128
HALF = 64


def tiles(eng, count, ring, body, head=4):
    for t in range(head):
        body(t, t % ring)
    with eng.Fori(head, count - 2 * ring + 1, ring) as t0:
        for k in range(ring):
            body(t0 + k, k)
    for t in range(count - ring, count):
        body(t, t % ring)


def before(t, n):
    return isinstance(t, int) and t < n


def build(nc, a, out):
    B, T, D = a["x"].shape
    J = a["ctx_1024"].shape[1]
    H, DK, M = 16, 8, 32
    HM = H * M
    PAIRS = B // 2
    CH = 12
    JP = J // CH
    CG = 4
    NG = CH // CG
    E = 8
    R1 = D // 2
    F = a["L0_ffn_W2"].shape[1]
    FT = F // P
    NCK = PAIRS * P // 512
    CR = 4
    assert (D, T, J, JP * CH) == (P, 56, 1500, J) and JP <= P and PAIRS % 2 == 0

    with ExitStack() as ctx:
        def sb(name, shape, dt=F32):
            return ctx.enter_context(nc.sbuf_tensor(name, shape, dt))

        def sem(name):
            return ctx.enter_context(nc.semaphore(name))

        PS = ctx.enter_context(nc.psum_tensor("PS", [P, 8, 512], F32))

        ident = sb("ident", [P, P])
        ones = sb("ones", [P, P])
        ones_bf = sb("ones_bf", [P, P], BF16)
        headmask = sb("headmask", [P, H])
        kvmask = sb("kvmask", [P, 4, 4, DK + 1])
        iota_e = sb("iota_e", [P, E])
        eps5 = sb("eps5", [P, 1])
        eps6 = sb("eps6", [P, 1])
        wqkvT = sb("wqkvT", [P, 3, P])
        wqk = sb("wqk", [P, 2, P])
        woT = sb("woT", [P, P])
        projT = sb("projT", [P, M])
        pblk = sb("pblk", [P, H, M])
        wfeat = sb("wfeat", [P, 2, HM])
        bo_b = sb("bo_b", [P, D])
        wsim = sb("wsim", [P, 3])
        w1_b = sb("w1_b", [P, D])
        bsim = sb("bsim", [PAIRS, 1])
        wqv = sb("wqv", [P, 4, P])
        bqv = sb("bqv", [P, 1])
        wr1 = sb("wr1", [P, R1])
        wr2 = sb("wr2", [P, 2, E])
        br1_b = sb("br1_b", [P, R1])
        lns_b = sb("lns_b", [P, R1])
        lnb_b = sb("lnb_b", [P, R1])
        br2_b = sb("br2_b", [P, E])
        b1s = sb("b1s", [P, 2, 2 * FT])
        b2r = sb("b2r", [P, D])

        xT = sb("xT", [P, 2, P])
        xn_in = sb("xn_in", [P, 2, P])
        sq = sb("sq", [P, 2, 2 * P])
        mx = sb("mx", [P, 2, 2 * H])
        nr = sb("nr", [P, 2, 2 * H])
        cc = sb("cc", [P, 2, 2 * H])
        phi = sb("phi", [P, 2, 2 * HM])
        vv = sb("vv", [P, 2, H, DK + 1])
        phT = sb("phT", [P, 2, HM])
        kvs = sb("kvs", [P, 2, 2, H * (DK + 1)])
        den = sb("den", [P, 2, H])
        rden = sb("rden", [P, 2, H])
        mg = sb("mg", [P, 2, P])
        mgT = sb("mgT", [P, 2, P])
        xb = sb("xb", [P, 2, P])
        res = sb("res", [P, PAIRS, P])
        st = sb("st", [P, PAIRS, 6])
        mv = sb("mv", [P, PAIRS, 2])
        rstd = sb("rstd", [P, PAIRS])
        xn = sb("xn", [P, 2, P])
        tmpr = sb("tmpr", [P, 2, P])
        rcol = sb("rcol", [P, PAIRS])

        cx = sb("cx", [P, CR, CH, P])
        cxT = sb("cxT", [P, 2, CH, JP])
        xnT = sb("xnT", [P, PAIRS, P])
        xw = sb("xw", [P, PAIRS, P])
        hqT = sb("hqT", [P, PAIRS, P])
        x3 = sb("x3", [P, PAIRS, P])
        x4 = sb("x4", [P, PAIRS, P])
        cm = sb("cm", [P, 2, P])
        nm = sb("nm", [P, 2, 1])
        nm_all = sb("nm_all", [P, B])
        dh = sb("dh", [P, 2, T], BF16)
        dl = sb("dl", [P, 2, T], BF16)
        ex = sb("ex", [P, 2, CH, T])
        e1 = sb("e1", [P, CH // 2, T])
        e2 = sb("e2", [P, CH // 4, T])
        e3 = sb("e3", [P, T])
        es = sb("es", [P, 2, T])
        rz = sb("rz", [P, T])
        rT = sb("rT", [PAIRS, 2, HALF])
        ba = sb("ba", [PAIRS, 2, HALF])
        bmx = sb("bmx", [PAIRS, 2, 1])
        hcb = sb("hcb", [P, B])
        zT = sb("zT", [P, 2, P])

        x2T = xw
        x2s = sb("x2s", [P, 2, P])
        acc = sb("acc", [P, PAIRS, P])
        rt0, rt1 = (x3[:, h * PAIRS // 2:(h + 1) * PAIRS // 2, :].rearrange("p t (a n) -> p (t a) n", a=2) for h in range(2))
        rt2 = x4[:, 0:PAIRS // 2, :].rearrange("p t (a n) -> p (t a) n", a=2)
        rstat = sb("rstat", [P, 4, PAIRS])
        hrT = sb("hrT", [P, PAIRS // 2, P])
        lg = sb("lg", [P, PAIRS, E])
        top = sb("top", [P, PAIRS, 8])
        topi = sb("topi", [P, PAIRS, 8], U32)
        topf = sb("topf", [P, PAIRS, 8])
        pw = sb("pw", [P, 4, PAIRS])
        oh = sb("oh", [P, 2, PAIRS, E])
        gate = sb("gate", [P, PAIRS, E])
        gateT = sb("gateT", [P, P])
        w1s = sb("w1s", [P, 2, 2 * F])
        w2s = sb("w2s", [P, 2, FT, P])
        g2 = sb("g2", [P, 2, 512])
        gT = sb("gT", [P, 2, FT, 512])

        consts_loaded = sem("consts_loaded")
        late_loaded = sem("late_loaded")
        pool_consts = sem("pool_consts")
        dve_consts = sem("dve_consts")
        composite = sem("composite")
        composite_sb = sem("composite_sb")
        xT_loaded = [sem(f"xT_loaded{i}") for i in range(2)]
        x_loaded = [sem(f"x_loaded{i}") for i in range(2)]
        ctx_loaded = [sem(f"ctx_loaded{i}") for i in range(CR)]
        w_loaded = [sem(f"w_loaded{i}") for i in range(2)]
        (a_qkv, a_feat, a_kv, a_phT, a_num, a_mT, a_wo, a_sq, a_exp, a_v, a_phTs, a_mTs, a_max, a_nrm, a_c, a_sub,
         a_kvm, a_dn, a_rc, a_mg, a_res, a_st, a_phi, a_xb) = (sem("a_" + n) for n in (
             "qkv feat kv phT num mT wo sq exp v phTs mTs max nrm c sub kvm dn rc mg res st phi xb").split())
        ln_ag, ln_sd, ln_rs = sem("ln_ag"), sem("ln_sd"), sem("ln_rs")
        p_xn, p_T, p_cp, p_xw, p_tmp, p_r = (sem("p_" + n) for n in "xn T cp xw tmp r".split())
        (b_T, b_evA, b_evD, b_S, b_cm, b_cmT, b_nm, b_dh, b_dl, b_nma, b_sub, b_exp, b_e1, b_e2, b_e3, b_es, b_pv,
         b_z, b_rz, b_hq) = (sem("b_" + n) for n in (
             "T evA evD S cm cmT nm dh dl nma sub exp e1 e2 e3 es pv z rz hq").split())
        h_tr, h_cp, h_ex, h_R, h_bc, h_x3, h_x4, h_pad = (sem("h_" + n) for n in "tr cp ex R bc x3 x4 pad".split())
        c_mm, c_z, c_T, c_cp, c_st = (sem("c_" + n) for n in "mm z T cp st".split())
        d_xn, d_T, d_cp, d_x2s, d_acc, d_h = (sem("d_" + n) for n in "xn T cp x2s acc h".split())
        (r_hc, r_sq, r_vs, r_sd, r_ln, r_ge, r_T, r_Tc, r_lg, r_dif, r_exp, r_gate, r_gT, r_gTc, r_b2, r_acc) = (
            sem("r_" + n) for n in "hc sq vs sd ln ge T Tc lg dif exp gate gT gTc b2 acc".split())
        f_b2b = sem("f_b2b")
        f_x, f_g, f_gT, f_y, f_acc = (sem("f_" + n) for n in "x g gT y acc".split())
        o_st, o_y, o_done = sem("o_st"), sem("o_y"), sem("o_done")
        chain = sem("chain")

        block = ctx.enter_context(nc.Block())

        psF = PS[:, 0:2, :].rearrange("p a b -> p (a b)")
        psQ = PS[:, 2, :]
        psT = PS[:, 3, :]
        psKV = PS[:, 4:6, 0:H * (DK + 1)]
        psN = PS[:, 6, :]
        psW = PS[:, 7, :]
        num = psN[:, 0:H * (DK + 1)].rearrange("p (h c) -> p h c", h=H)
        psC = PS[:, 0:NG, :]
        psS = [PS[:, 3 + 2 * i:5 + 2 * i, 0:CH // 2 * T] for i in range(2)]
        cmT = [PS[:, 3 + 2 * i, CH // 2 * T:CH // 2 * T + JP] for i in range(2)]
        psM = PS[:, 7, :]

        CONSTS = [
            (wqkvT[:, 0, :], a["wqT"]), (wqkvT[:, 1, :], a["wkT"]), (wqkvT[:, 2, :], a["wvT"]),
            (wqk[:, 0, :], a["L0_attn_Wq"]), (wqk[:, 1, :], a["L0_attn_Wk"]), (projT[:, :], a["projT"]),
            (woT[:, :], a["woT"]), (bo_b[:, :], a["L0_attn_bo"].partition_broadcast(P)),
        ]
        LATE = [
            (wsim[:, :], a["wsimT"]), (w1_b[:, :], a["L0_xattn_w_sim"][0:D].partition_broadcast(P)),
            (bsim[:, :], a["L0_xattn_b_sim"].partition_broadcast(PAIRS)),
            (wqv[:, :, :], a["L0_xattn_W_qv"].rearrange("(k p) n -> p k n", p=P)),
            (bqv[:, :], a["L0_xattn_b_qv"].rearrange("(p a) -> p a", a=1)),
            (wr1[:, :], a["L0_ffn_Wr1"]),
            (wr2[0:R1, 0, :], a["L0_ffn_Wr2"]), (wr2[R1:P, 1, :], a["L0_ffn_Wr2"]),
            (br1_b[:, :], a["L0_ffn_br1"].partition_broadcast(P)),
            (lns_b[:, :], a["L0_ffn_ln_scale"].partition_broadcast(P)),
            (lnb_b[:, :], a["L0_ffn_ln_bias"].partition_broadcast(P)),
            (br2_b[:, :], a["L0_ffn_br2"].partition_broadcast(P)),
        ] + [(b2r[p * E:(p + 1) * E, :], a["L0_ffn_b2"]) for p in range(PAIRS)]

        @block.sync
        def _(sp):
            for dst, src in CONSTS:
                sp.dma_start(dst, src).then_inc(consts_loaded, 16)

            def load_x(t, k):
                if not before(t, 2):
                    sp.wait_ge(a_feat, t - 1)
                    sp.wait_ge(a_xb, t - 1)
                sp.dma_start(xT[:, k, :].rearrange("p (b i) -> p b i", b=2)[:, :, 0:T],
                             a["xT"][:, t, :, :]).then_inc(xT_loaded[k], 16)
                for b in range(2):
                    sp.dma_start(xn_in[b * HALF:b * HALF + T, k, :], a["x"][2 * t + b]).then_inc(x_loaded[k], 16)

            def load_ctx(b, k):
                if not before(b, CR):
                    sp.wait_ge(b_pv, b - CR + 1)
                src = a["ctx_1024"][b].rearrange("(p c) d -> p c d", c=CH)
                cut = JP // 16 * 16
                sp.dma_start(cx[0:cut, k], src[0:cut]).then_inc(ctx_loaded[k], 16)
                sp.dma_start(cx[cut:JP, k], src[cut:JP]).then_inc(ctx_loaded[k], 16)

            sp.wait_ge(pool_consts, 3)
            load_x(0, 0)
            load_x(1, 1)
            for b in range(CR):
                load_ctx(b, b)
            with sp.Fori(2, PAIRS - 1, 2) as t0:
                for k in range(2):
                    load_x(t0 + k, k)
            with sp.Fori(CR, B - CR + 1, CR) as b0:
                for k in range(CR):
                    load_ctx(b0 + k, k)

            def load_w(e, k):
                if not before(e, 2):
                    sp.wait_ge(f_y, NCK * (e - 1))
                sp.dma_start(w1s[:, k, :], a["L0_ffn_W1"][e]).then_inc(w_loaded[k], 16)
                sp.dma_start(b1s[:, k, :], a["b1c"][:, e, :]).then_inc(w_loaded[k], 16)
                sp.dma_start(w2s[:, k, :, :], a["L0_ffn_W2"][e].rearrange("(f p) n -> p f n", p=P)).then_inc(w_loaded[k], 16)

            load_w(0, 0)
            load_w(1, 1)
            with sp.Fori(2, E - 1, 2) as e0:
                for k in range(2):
                    load_w(e0 + k, k)

            sp.wait_ge(o_y, 2)
            for b in range(2):
                sp.dma_start(out.rearrange("(t b) i d -> b i t d", b=2)[b],
                             res[b * HALF:b * HALF + T, :, :]).then_inc(o_done, 16)
            sp.wait_ge(o_done, 32)

        @block.gpsimd
        def _(pool):
            pool.memset(xT[:, :, :], 0.0).then_inc(pool_consts, 1)
            pool.memset(xn_in[:, :, :], 0.0).then_inc(pool_consts, 1)
            pool.memset(ident[:, :], 0.0).then_inc(pool_consts, 1)
            pool.memset(ones[:, :], 1.0).then_inc(pool_consts, 1)
            pool.memset(ones_bf[:, :], 1.0).then_inc(pool_consts, 1)
            pool.memset(headmask[:, :], 1.0).then_inc(pool_consts, 1)
            pool.memset(kvmask[:, :, :, :], 1.0).then_inc(pool_consts, 1)
            pool.memset(vv[:, :, :, :], 1.0).then_inc(pool_consts, 1)
            pool.memset(wr2[:, :, :], 0.0).then_inc(pool_consts, 1)
            pool.memset(eps5[:, :], 1e-5).then_inc(pool_consts, 1)
            pool.memset(eps6[:, :], 1e-6).then_inc(pool_consts, 1)
            pool.memset(hqT[:, :, :], 0.0).then_inc(pool_consts, 1)
            pool.memset(cm[:, :, :], 0.0).then_inc(pool_consts, 1)
            pool.memset(ba[:, :, :], 0.0).then_inc(pool_consts, 1)
            pool.iota(iota_e[:, :], [[1, E]], base=0, channel_multiplier=0,
                      allow_small_or_imprecise_dtypes=True).then_inc(pool_consts, 1)
            pool.wait_ge(pool_consts, 15)
            pool.affine_select(out=ident[:, :], in_=ident[:, :], compare_op=ALU.not_equal, fill=1.0, base=0,
                               pattern=[[-1, P]], channel_multiplier=1).then_inc(pool_consts, 1)
            pool.affine_select(out=headmask[:, :], in_=headmask[:, :], compare_op=ALU.is_ge, fill=0.0, base=0,
                               pattern=[[-DK, H]], channel_multiplier=1).then_inc(pool_consts, 1)
            pool.affine_select(out=kvmask[:, :, :, :], in_=kvmask[:, :, :, :], compare_op=ALU.is_ge, fill=0.0, base=0,
                               pattern=[[0, 4], [-M, 4], [0, DK + 1]], channel_multiplier=1).then_inc(pool_consts, 1)
            pool.wait_ge(pool_consts, 18)
            pool.affine_select(out=headmask[:, :], in_=headmask[:, :], compare_op=ALU.is_ge, fill=0.0, base=DK - 1,
                               pattern=[[DK, H]], channel_multiplier=-1).then_inc(pool_consts, 1)
            pool.affine_select(out=kvmask[:, :, :, :], in_=kvmask[:, :, :, :], compare_op=ALU.is_ge, fill=0.0,
                               base=M - 1, pattern=[[0, 4], [M, 4], [0, DK + 1]],
                               channel_multiplier=-1).then_inc(pool_consts, 1)
            for dst, src in LATE:
                pool.dma_start(dst, src).then_inc(late_loaded, 16)
            pool.wait_ge(consts_loaded, 16 * len(CONSTS))

            def attention(t, k):
                pool.wait_ge(x_loaded[k], 16 * (t - k) + 32)
                if not before(t, 2):
                    pool.wait_ge(a_res, t - 1)
                pool.tensor_tensor(xb[:, k], xn_in[:, k], bo_b[:, :], ALU.add).then_inc(a_xb, 1)
                pool.wait_ge(a_exp, t + 1)
                pool.tensor_tensor(phi[:, k], phi[:, k], eps6[:, :].broadcast_to([P, 2 * HM]), ALU.add).then_inc(a_phi, 1)

            tiles(pool, PAIRS, 2, attention)
            pool.wait_ge(late_loaded, 16 * len(LATE))

            def w1_product(t, k):
                pool.wait_ge(p_xn, t + 1)
                if not before(t, 2):
                    pool.wait_ge(p_r, t - 1)
                pool.tensor_tensor(tmpr[:, k], xn[:, k], w1_b[:, :], ALU.mult).then_inc(p_tmp, 1)

            tiles(pool, PAIRS, 2, w1_product)

            def sum_chunks(b, k):
                u = k % 2
                pool.wait_ge(b_nm, b + 1)
                pool.tensor_copy(nm_all[0:T, bass.ds(b, 1)], nm[0:T, u]).then_inc(b_nma, 1)
                pool.wait_ge(b_exp, b + 1)
                if not before(b, 1):
                    pool.wait_ge(b_es, b)
                pool.tensor_tensor(e1[0:JP], ex[0:JP, u, 0:6], ex[0:JP, u, 6:12], ALU.add).then_inc(b_e1, 1)
                pool.wait_ge(b_e1, b + 1)
                pool.tensor_tensor(e2[0:JP], e1[0:JP, 0:3], e1[0:JP, 3:6], ALU.add).then_inc(b_e2, 1)
                pool.wait_ge(b_e2, b + 1)
                pool.tensor_tensor(e3[0:JP], e2[0:JP, 0], e2[0:JP, 1], ALU.add).then_inc(b_e3, 1)
                pool.wait_ge(b_e3, b + 1)
                if not before(b, 2):
                    pool.wait_ge(b_z, b - 1)
                pool.tensor_tensor(es[0:JP, u], e3[0:JP], e2[0:JP, 2], ALU.add).then_inc(b_es, 1)

            tiles(pool, B, CR, sum_chunks)
            pool.wait_ge(b_hq, B)
            pool.tensor_tensor(x3[:, :, :], xnT[:, :, :], hqT[:, :, :], ALU.mult).then_inc(h_x3, 1)

            def keep_x(t, k):
                pool.wait_ge(d_xn, t + 1)
                pool.tensor_copy(acc[:, t], xn[:, k]).then_inc(d_acc, 1)

            tiles(pool, PAIRS, 2, keep_x)

        @block.scalar
        def _(act):
            act.wait_ge(composite, 2)
            act.activation(wfeat[:, :, :], psF.rearrange("p (a b) -> p a b", a=2), ACT.Copy,
                           scale=float(DK) ** -0.5).then_inc(composite_sb, 1)

            def phT_copy(t, k):
                act.wait_ge(a_phT, t + 1)
                if not before(t, 2):
                    act.wait_ge(a_num, t - 1)
                act.activation(phT[:, k], psT, ACT.Copy).then_inc(a_phTs, 1)

            def mT_copy(t, k):
                act.wait_ge(a_mT, t + 1)
                if not before(t, 2):
                    act.wait_ge(a_wo, t - 1)
                act.activation(mgT[:, k], psT[:, 0:P], ACT.Copy).then_inc(a_mTs, 1)

            def attention(t, k):
                if not before(t, 1):
                    phT_copy(t - 1, 1 - k)
                if not before(t, 2):
                    mT_copy(t - 2, k)
                act.wait_ge(a_qkv, t + 1)
                if not before(t, 2):
                    act.wait_ge(a_nrm, t - 1)
                act.activation(sq[:, k], psQ[:, 0:2 * P], ACT.Square, scale=0.5 * float(DK // 2) ** -0.5).then_inc(a_sq, 1)
                if not before(t, 2):
                    act.wait_ge(a_kv, t - 1)
                act.activation(vv[:, k, :, 0:DK], psQ[:, 2 * P:3 * P].rearrange("p (h d) -> p h d", h=H),
                               ACT.Copy).then_inc(a_v, 1)
                act.wait_ge(a_sub, t + 1)
                act.activation(phi[:, k], phi[:, k], ACT.Exp).then_inc(a_exp, 1)

            act.wait_ge(pool_consts, 20)
            tiles(act, PAIRS, 2, attention)
            phT_copy(PAIRS - 1, 1)
            mT_copy(PAIRS - 2, 0)
            mT_copy(PAIRS - 1, 1)

            act.wait_ge(ln_ag, 1)
            act.activation(rstd[:, :], mv[:, :, 1], ACT.Sqrt, bias=eps5[:, :]).then_inc(ln_sd, 1)

            def x_transposed(t, k):
                act.wait_ge(p_T, t + 1)
                act.activation(xnT[:, t], PS[:, k, 0:P], ACT.Copy).then_inc(p_cp, 1)

            tiles(act, PAIRS, 2, x_transposed)

            def exp_sim(b, u):
                act.wait_ge(b_sub, b + 1)
                if not before(b, 2):
                    act.wait_ge(b_pv, b - 1)
                    act.wait_ge(b_es, b - 1)
                act.activation(ex[0:JP, u].rearrange("p (h c) i -> p h (c i)", h=2), psS[u][0:JP],
                               ACT.Exp).then_inc(b_exp, 1)

            def cross(b, k):
                u = k % 2
                for g in range(2):
                    act.wait_ge(b_T, NG * b + g + 1)
                    if g == 0 and not before(b, 2):
                        act.wait_ge(b_S, b - 1)
                    act.activation(cxT[:, u, g * CG:(g + 1) * CG], psC[:, g, 0:CG * JP].rearrange(
                        "p (c j) -> p c j", c=CG), ACT.Copy).then_inc(b_evA, 1)
                if not before(b, 1):
                    exp_sim(b - 1, 1 - u)

            tiles(act, B, CR, cross)
            exp_sim(B - 1, 1)

            act.wait_ge(h_tr, 3)
            act.activation(rT[:, :, :], psM[0:PAIRS, 0:P].rearrange("p (u i) -> p u i", u=2), ACT.Copy).then_inc(h_cp, 1)
            act.wait_ge(h_pad, 1)
            act.activation(ba[:, :, 0:T], rT[:, :, 0:T], ACT.Exp).then_inc(h_ex, 1)

            def z_rows(t, k):
                act.wait_ge(c_T, t + 1)
                act.activation(res[:, t], PS[:, 6 + k, 0:P], ACT.Copy).then_inc(c_cp, 1)

            tiles(act, PAIRS, 2, z_rows)
            act.wait_ge(ln_ag, 2)
            act.activation(rstd[:, :], mv[:, :, 1], ACT.Sqrt, bias=eps5[:, :]).then_inc(ln_sd, 1)

            def x2_transposed(t, k):
                act.wait_ge(d_T, t + 1)
                act.activation(x2T[:, t], PS[:, k, 0:P], ACT.Copy).then_inc(d_cp, 1)

            tiles(act, PAIRS, 2, x2_transposed)

            act.wait_ge(r_hc, 1)
            act.activation(rt1, rt0, ACT.Square).then_inc(r_sq, 1)
            act.wait_ge(r_vs, 1)
            act.activation(rstat[:, 1], rstat[:, 1], ACT.Sqrt, bias=eps6[:, :], scale=1.0 / R1).then_inc(r_sd, 1)
            act.wait_ge(r_ln, 1)
            act.activation(rt1, rt0, ACT.Gelu_apprx_tanh).then_inc(r_ge, 1)
            act.wait_ge(r_T, 1)
            act.activation(hrT[:, :, :].rearrange("p (a q) n -> p a (q n)", a=2), PS[:, 4:6, :], ACT.Copy).then_inc(r_Tc, 1)
            act.wait_ge(r_dif, 1)
            act.activation(pw[:, 1], pw[:, 0], ACT.Exp).then_inc(r_exp, 1)
            act.wait_ge(r_gT, 1)
            act.activation(gateT[:, :], PS[:, 6, 0:P], ACT.Copy).then_inc(r_gTc, 1)

            def expert(e, k):
                act.wait_ge(w_loaded[k], 24 * (e - k) + 48)
                for s in range(NCK * FT):
                    v = NCK * FT * e + s
                    f = s % FT
                    act.wait_ge(f_x, v + 1)
                    if not before(v, 2):
                        act.wait_ge(f_gT, v - 1)
                    act.activation(g2[:, s % 2], PS[:, 2 + s % 2], ACT.Gelu_apprx_tanh,
                                   bias=b1s[:, k, FT + f:FT + f + 1]).then_inc(f_g, 1)

            tiles(act, E, 2, expert, head=2)
            act.wait_ge(ln_ag, 3)
            act.activation(rstd[:, :], mv[:, :, 1], ACT.Sqrt, bias=eps5[:, :]).then_inc(ln_sd, 1)

        @block.tensor
        def _(pe):
            pe.wait_ge(consts_loaded, 16 * len(CONSTS))
            pe.wait_ge(dve_consts, 1)
            for i in range(2):
                pe.matmul(psF[:, i * HM:(i + 1) * HM], wqk[:, i, :], pblk[:, :, :].rearrange("p h m -> p (h m)"),
                          start=True, stop=True).then_inc(composite, 1)
            pe.wait_ge(composite_sb, 1)

            def kv_and_turn(t, k):
                pe.wait_ge(a_phi, t + 1)
                if not before(t, 2):
                    pe.wait_ge(a_mTs, t - 1)
                for g in range(4):
                    last = pe.transpose(psT[:, g * P:(g + 1) * P], phi[:, k, g * P:(g + 1) * P], ident[:, :])
                last.then_inc(a_phT, 1)
                pe.wait_ge(a_v, t + 1)
                if not before(t, 1):
                    pe.wait_ge(a_kvm, t)
                for b in range(2):
                    r = slice(b * HALF, b * HALF + T)
                    for g in range(4):
                        last = pe.matmul(psKV[:, b, g * 36:g * 36 + 36], phi[r, k, HM + g * P:HM + (g + 1) * P],
                                         vv[r, k, 4 * g:4 * g + 4, :].rearrange("p h c -> p (h c)"), start=True, stop=True)
                last.then_inc(a_kv, 1)

            def numerators(t, k):
                pe.wait_ge(a_phTs, t + 1)
                pe.wait_ge(a_kvm, t + 1)
                if not before(t, 1):
                    pe.wait_ge(a_mg, t)
                for b in range(2):
                    for g in range(4):
                        last = pe.matmul(psN[b * HALF:(b + 1) * HALF, g * 36:g * 36 + 36],
                                         phT[:, k, g * P + b * HALF:g * P + (b + 1) * HALF],
                                         kvs[:, k, b, g * 36:g * 36 + 36], start=True, stop=True)
                last.then_inc(a_num, 1)

            def turn_merged(t, k):
                pe.wait_ge(a_mg, t + 1)
                pe.wait_ge(a_phTs, min(t + 2, PAIRS) if isinstance(t, int) else t + 2)
                pe.transpose(psT[:, 0:P], mg[:, k], ident[:, :]).then_inc(a_mT, 1)

            def out_projection(t, k):
                pe.wait_ge(a_mTs, t + 1)
                if not before(t, 1):
                    pe.wait_ge(a_res, t)
                pe.matmul(psW[:, 0:P], mgT[:, k], woT[:, :], start=True, stop=True).then_inc(a_wo, 1)

            def attention(t, k):
                if not before(t, 1):
                    kv_and_turn(t - 1, 1 - k)
                if not before(t, 2):
                    turn_merged(t - 2, k)
                pe.wait_ge(xT_loaded[k], 8 * (t - k) + 16)
                if not before(t, 1):
                    pe.wait_ge(a_sq, t)
                    pe.wait_ge(a_v, t)
                pe.matmul(psQ[:, 0:3 * P], xT[:, k], wqkvT[:, :, :].rearrange("p a b -> p (a b)"),
                          start=True, stop=True).then_inc(a_qkv, 1)
                if not before(t, 2):
                    out_projection(t - 2, k)
                if not before(t, 1):
                    pe.wait_ge(a_sub, t)
                for i in range(2):
                    last = pe.matmul(psF[:, i * HM:(i + 1) * HM], xT[:, k], wfeat[:, i, :], start=True, stop=True)
                last.then_inc(a_feat, 1)
                if not before(t, 1):
                    numerators(t - 1, 1 - k)

            tiles(pe, PAIRS, 2, attention)
            kv_and_turn(PAIRS - 1, 1)
            turn_merged(PAIRS - 2, 0)
            out_projection(PAIRS - 2, 0)
            numerators(PAIRS - 1, 1)
            turn_merged(PAIRS - 1, 1)
            out_projection(PAIRS - 1, 1)

            def turn_x(t, k):
                pe.wait_ge(p_xn, t + 1)
                if not before(t, 2):
                    pe.wait_ge(p_cp, t - 1)
                pe.transpose(PS[:, k, 0:P], xn[:, k], ident[:, :]).then_inc(p_T, 1)

            tiles(pe, PAIRS, 2, turn_x)

            def less_maximum(b, u):
                pe.wait_ge(b_dl, b + 1)
                for h in range(2):
                    for d in (dh, dl):
                        last = pe.matmul(psS[u][0:JP, h].rearrange("p (c i) -> p c i", c=CH // 2),
                                         ones_bf[0:T, 0:JP],
                                         d[0:T, u].unsqueeze(1).broadcast_to([T, CH // 2, T]),
                                         start=False, stop=True, skip_group_check=True)
                last.then_inc(b_sub, 1)

            def values(b, k):
                u = k % 2
                pe.wait_ge(b_exp, b + 1)
                if not before(b, 1):
                    pe.wait_ge(b_hq, b)
                for c in range(CH):
                    last = pe.matmul(psM[:, 0:T], cx[0:JP, k, c], ex[0:JP, u, c], start=(c == 0), stop=(c == CH - 1))
                last.then_inc(b_pv, 1)
                pe.wait_ge(b_es, b + 1)
                pe.matmul(psM[:, 64:64 + T], ones[0:JP, :], es[0:JP, u], start=True, stop=True).then_inc(b_z, 1)

            def cross(b, k):
                u = k % 2
                pe.wait_ge(ctx_loaded[k], 8 * (b - k) + 32)
                for g in range(NG):
                    if not before(b, 1):
                        pe.wait_ge(b_evA, 2 * (b - 1) + g + 1) if g < 2 else pe.wait_ge(b_evD, b)
                    for c in range(CG):
                        last = pe.transpose(psC[:, g, c * JP:(c + 1) * JP], cx[0:JP, k, g * CG + c], ident[0:JP, 0:JP])
                    last.then_inc(b_T, 1)
                if not before(b, 1):
                    less_maximum(b - 1, 1 - u)
                if not before(b, 2):
                    pe.wait_ge(b_exp, b - 1)
                for c in range(CH):
                    if c == 0:
                        pe.wait_ge(b_evA, 2 * b + 1)
                    if c == CG:
                        pe.wait_ge(b_evA, 2 * b + 2)
                    if c == 2 * CG:
                        pe.wait_ge(b_evD, b + 1)
                    h, i = c // (CH // 2), c % (CH // 2)
                    last = pe.matmul(psS[u][0:JP, h, i * T:(i + 1) * T], cxT[:, u, c],
                                     xw[:, :, :].rearrange("p t (u i) -> p (t u) i", u=2)[:, b, 0:T],
                                     start=(i == 0), stop=True, skip_group_check=True)
                last.then_inc(b_S, 1)
                if not before(b, 1):
                    values(b - 1, (k - 1) % CR)
                pe.wait_ge(b_cm, b + 1)
                pe.matmul(cmT[u], cm[0:JP, u], ident[0:JP, 0:JP], is_transpose=True, start=False, stop=True,
                          skip_group_check=True).then_inc(b_cmT, 1)

            pe.wait_ge(p_xw, PAIRS)
            pe.wait_ge(p_cp, PAIRS)
            tiles(pe, B, CR, cross)
            less_maximum(B - 1, 1)
            values(B - 1, CR - 1)

            pe.wait_ge(b_hq, B)
            pe.wait_ge(b_nma, B)
            pe.wait_ge(p_r, PAIRS)
            pe.transpose(psM[0:PAIRS, 0:P], rcol[:, :], ident[:, :]).then_inc(h_tr, 1)
            for u in range(2):
                pe.transpose(psM[0:PAIRS, P + u * HALF:P + u * HALF + T],
                             nm_all[0:T, :].rearrange("p (t u) -> p u t", u=2)[:, u, :],
                             ident[0:T, 0:T]).then_inc(h_tr, 1)
            pe.wait_ge(h_R, 1)
            for n in range(NCK):
                last = pe.matmul(PS[:, n, :], ones[0:PAIRS, :],
                                 x4[0:PAIRS, :, :].rearrange("p t i -> p (t i)")[:, n * 512:(n + 1) * 512],
                                 start=True, stop=True)
            last.then_inc(h_bc, 1)

            def turn_z(t, k):
                pe.wait_ge(c_z, t + 1)
                if not before(t, 2):
                    pe.wait_ge(c_cp, t - 1)
                pe.transpose(PS[:, 6 + k, 0:P], zT[:, k], ident[:, :]).then_inc(c_T, 1)

            def features(t, k):
                if not before(t, 2):
                    pe.wait_ge(c_z, t - 1)
                for i, x in enumerate((xnT, hqT, x3, x4)):
                    last = pe.matmul(PS[:, 4 + k, 0:P], wqv[:, i], x[:, t], start=(i == 0), stop=(i == 3))
                last.then_inc(c_mm, 1)
                if not before(t, 1):
                    turn_z(t - 1, 1 - k)

            pe.wait_ge(h_x4, 1)
            pe.wait_ge(h_x3, 1)
            tiles(pe, PAIRS, 2, features)
            turn_z(PAIRS - 1, 1)

            def router(t, k):
                pe.wait_ge(d_x2s, t + 1)
                pe.matmul(PS[:, bass.ds(2 + t // 8, 1), bass.ds((t % 8) * R1, R1)] if isinstance(t, int) else
                          PS[:, 2:4, :].rearrange("p a (t n) -> p (a t) n", n=R1)[:, t, :],
                          x2s[:, k], wr1[:, :], start=True, stop=True).then_inc(d_h, 1)

            def turn_x2(t, k):
                pe.wait_ge(d_xn, t + 1)
                if not before(t, 2):
                    pe.wait_ge(d_cp, t - 1)
                pe.transpose(PS[:, k, 0:P], xn[:, k], ident[:, :]).then_inc(d_T, 1)
                if not before(t, 1):
                    router(t - 1, 1 - k)

            tiles(pe, PAIRS, 2, turn_x2)
            router(PAIRS - 1, 1)

            pe.wait_ge(r_ge, 1)
            for q in range(PAIRS // 2):
                last = pe.transpose(PS[:, 4 + q // 4, (q % 4) * P:(q % 4 + 1) * P],
                                    rt1[:, 2 * q:2 * q + 2, :].rearrange("p a n -> p (a n)"), ident[:, :])
            last.then_inc(r_T, 1)
            pe.wait_ge(r_Tc, 1)
            for q in range(PAIRS // 2):
                last = pe.matmul(PS[:, 6, 2 * q * E:(2 * q + 2) * E], hrT[:, q], wr2[:, :, :].rearrange("p a e -> p (a e)"),
                                 start=True, stop=True)
            last.then_inc(r_lg, 1)
            pe.wait_ge(r_gate, 1)
            pe.transpose(PS[:, 6, 0:P], gate[:, :, :].rearrange("p t e -> p (t e)"), ident[:, :]).then_inc(r_gT, 1)
            pe.wait_ge(r_gTc, 1)
            pe.wait_ge(f_b2b, 1)
            for n in range(NCK):
                last = pe.matmul(PS[:, n, :], gateT[:, :], x4[:, :, :].rearrange("p t i -> p (t i)")[:, n * 512:(n + 1) * 512],
                                 start=True, stop=True)
            last.then_inc(r_b2, 1)
            pe.wait_ge(r_acc, 1)

            def down(e, n, k):
                s = NCK * e + n
                pe.wait_ge(f_gT, FT * s + FT)
                if not before(s, 2):
                    pe.wait_ge(f_acc, s - 1)
                for q in range(4):
                    for f in range(FT):
                        last = pe.matmul(PS[:, 4 + n % 2, q * P:(q + 1) * P], gT[:, n % 2, f, q * P:(q + 1) * P],
                                         w2s[:, k, f], start=(f == 0), stop=(f == FT - 1))
                last.then_inc(f_y, 1)

            def expert(e, k):
                pe.wait_ge(w_loaded[k], 24 * (e - k) + 48)
                for n in range(NCK):
                    xs = x2T[:, 4 * n:4 * n + 4, :].rearrange("p t i -> p (t i)")
                    for f in range(FT):
                        s = n * FT + f
                        v = NCK * FT * e + s
                        if not before(v, 2):
                            pe.wait_ge(f_gT, v - 1)
                        pe.matmul(PS[:, 2 + s % 2], w1s[:, k, F + f * P:F + (f + 1) * P], xs, start=True, stop=True)
                        pe.matmul(PS[:, s % 2], w1s[:, k, f * P:(f + 1) * P], xs, start=True, stop=True).then_inc(f_x, 1)
                        if f == 0 and not before(NCK * e + n, 1):
                            if n:
                                down(e, n - 1, k)
                            else:
                                down(e - 1, NCK - 1, 1 - k)

            tiles(pe, E, 2, expert, head=2)
            down(E - 1, NCK - 1, 1)

        @block.vector
        def _(dve):
            steps = [0]

            def link(ins):
                steps[0] += 1
                ins.then_inc(chain, 1)
                dve.wait_ge(chain, steps[0])

            dve.wait_ge(pool_consts, 20)
            dve.wait_ge(consts_loaded, 16 * len(CONSTS))
            dve.tensor_tensor(pblk[:, :, :], projT[:, :].unsqueeze(1).broadcast_to([P, H, M]),
                              headmask[:, :].unsqueeze(2).broadcast_to([P, H, M]), ALU.mult).then_inc(dve_consts, 1)

            def keep_kv(t, k):
                dve.wait_ge(a_kv, t + 1)
                if not before(t, 2):
                    dve.wait_ge(a_num, t - 1)
                dve.tensor_tensor(kvs[:, k], psKV, kvmask[:, :, :, :].rearrange("p a b c -> p (a b c)").unsqueeze(1)
                                  .broadcast_to([P, 2, H * (DK + 1)]), ALU.mult).then_inc(a_kvm, 1)

            def merged(t, k):
                dve.wait_ge(a_num, t + 1)
                dve.tensor_scalar(den[:, k], num[:, :, DK], M * 1e-6, None, ALU.add).then_inc(a_dn, 1)
                dve.wait_ge(a_dn, t + 1)
                dve.reciprocal(rden[:, k], den[:, k]).then_inc(a_rc, 1)
                dve.wait_ge(a_rc, t + 1)
                if not before(t, 2):
                    dve.wait_ge(a_mT, t - 1)
                dve.tensor_tensor(mg[:, k].rearrange("p (h d) -> p h d", h=H), num[:, :, 0:DK],
                                  rden[:, k].unsqueeze(2).broadcast_to([P, H, DK]), ALU.mult).then_inc(a_mg, 1)

            def residual(t, k):
                dve.wait_ge(a_wo, t + 1)
                dve.wait_ge(a_xb, t + 1)
                dve.tensor_tensor(res[:, t], psW[:, 0:P], xb[:, k], ALU.add).then_inc(a_res, 1)
                dve.wait_ge(a_res, t + 1)
                dve.bn_stats(st[:, t], res[:, t]).then_inc(a_st, 1)

            def attention(t, k):
                dve.wait_ge(a_sq, t + 1)
                if not before(t, 2):
                    dve.wait_ge(a_c, t - 1)
                dve.tensor_reduce(nr[:, k], sq[:, k].rearrange("p (h d) -> p h d", d=DK), AX.X, ALU.add).then_inc(a_nrm, 1)
                dve.wait_ge(a_feat, t + 1)
                dve.tensor_reduce(mx[:, k], psF.rearrange("p (h m) -> p h m", m=M), AX.X, ALU.max).then_inc(a_max, 1)
                if not before(t, 1):
                    keep_kv(t - 1, 1 - k)
                dve.wait_ge(a_max, t + 1)
                dve.wait_ge(a_nrm, t + 1)
                dve.tensor_tensor(cc[:, k], mx[:, k], nr[:, k], ALU.add).then_inc(a_c, 1)
                dve.wait_ge(a_c, t + 1)
                if not before(t, 2):
                    dve.wait_ge(a_kv, t - 1)
                dve.tensor_tensor(phi[:, k].rearrange("p (h m) -> p h m", m=M), psF.rearrange("p (h m) -> p h m", m=M),
                                  cc[:, k].unsqueeze(2).broadcast_to([P, 2 * H, M]), ALU.subtract).then_inc(a_sub, 1)
                if not before(t, 1):
                    merged(t - 1, 1 - k)
                if not before(t, 2):
                    residual(t - 2, k)

            tiles(dve, PAIRS, 2, attention)
            keep_kv(PAIRS - 1, 1)
            residual(PAIRS - 2, 0)
            merged(PAIRS - 1, 1)
            residual(PAIRS - 1, 1)

            def norm_factors(n, stats, count):
                dve.wait_ge(stats, count)
                for t in range(PAIRS):
                    last = dve.bn_aggr(mv[:, t], st[:, t])
                last.then_inc(ln_ag, 1)
                dve.wait_ge(ln_sd, n)
                dve.reciprocal(rstd[:, :], rstd[:, :]).then_inc(ln_rs, 1)
                dve.wait_ge(ln_rs, n)

            norm_factors(1, a_st, PAIRS)
            dve.wait_ge(late_loaded, 16 * len(LATE))

            def x_parts(t, k):
                dve.wait_ge(p_cp, t + 1)
                dve.tensor_scalar(xw[:, t], xnT[:, t], wsim[:, 2:3], wsim[:, 1:2], ALU.mult, ALU.add).then_inc(p_xw, 1)
                dve.wait_ge(p_tmp, t + 1)
                dve.tensor_reduce(rcol[:, bass.ds(t, 1)], tmpr[:, k], AX.X, ALU.add).then_inc(p_r, 1)

            def norm1(t, k):
                if not before(t, 2):
                    dve.wait_ge(p_T, t - 1)
                    dve.wait_ge(p_tmp, t - 1)
                dve.tensor_scalar(xn[:, k], res[:, t], mv[:, t, 0:1], rstd[:, bass.ds(t, 1)], ALU.subtract,
                                  ALU.mult).then_inc(p_xn, 1)
                if not before(t, 1):
                    x_parts(t - 1, 1 - k)

            tiles(dve, PAIRS, 2, norm1)
            x_parts(PAIRS - 1, 1)

            def attended(b, u):
                dve.wait_ge(b_z, b + 1)
                dve.reciprocal(rz[:, :], psM[:, 64:64 + T]).then_inc(b_rz, 1)
                dve.wait_ge(b_rz, b + 1)
                dve.tensor_tensor(hqT[:, :, :].rearrange("p t (u i) -> p (t u) i", u=2)[:, b, 0:T], psM[:, 0:T], rz[:, :],
                                  ALU.mult).then_inc(b_hq, 1)

            def cross(b, k):
                u = k % 2
                dve.wait_ge(b_T, NG * b + NG)
                if not before(b, 2):
                    dve.wait_ge(b_S, b - 1)
                dve.tensor_copy(cxT[:, u, 2 * CG:3 * CG], psC[:, 2, 0:CG * JP].rearrange(
                    "p (c j) -> p c j", c=CG)).then_inc(b_evD, 1)
                dve.wait_ge(b_S, b + 1)
                if not before(b, 2):
                    dve.wait_ge(b_cmT, b - 1)
                dve.tensor_reduce(cm[0:JP, u, 0:T], psS[u][0:JP].rearrange("p h (c i) -> p i h c", i=T), AX.XY,
                                  ALU.max).then_inc(b_cm, 1)
                if not before(b, 1):
                    attended(b - 1, 1 - u)
                dve.wait_ge(b_cmT, b + 1)
                if not before(b, 2):
                    dve.wait_ge(b_nma, b - 1)
                dve.tensor_reduce(nm[0:T, u], cmT[u][0:T], AX.X, ALU.max, negate=True).then_inc(b_nm, 1)
                dve.wait_ge(b_nm, b + 1)
                if not before(b, 2):
                    dve.wait_ge(b_sub, b - 1)
                dve.tensor_scalar(dh[0:T, u], ident[0:T, 0:T], nm[0:T, u], None, ALU.mult).then_inc(b_dh, 1)
                dve.wait_ge(b_dh, b + 1)
                dve.scalar_tensor_tensor(out=dl[0:T, u], in0=ident[0:T, 0:T], scalar=nm[0:T, u], in1=dh[0:T, u],
                                         op0=ALU.mult, op1=ALU.subtract).then_inc(b_dl, 1)

            tiles(dve, B, CR, cross)
            attended(B - 1, 1)

            dve.wait_ge(h_cp, 1)
            link(dve.scalar_tensor_tensor(out=rT[:, :, 0:T], in0=rT[:, :, 0:T], scalar=bsim[:, :],
                                          in1=psM[0:PAIRS, P:2 * P].rearrange("p (u i) -> p u i", u=2)[:, :, 0:T],
                                          op0=ALU.add, op1=ALU.subtract))
            link(dve.tensor_reduce(bmx[:, :, :], rT[:, :, 0:T], AX.X, ALU.max))
            dve.tensor_tensor(rT[:, :, 0:T], rT[:, :, 0:T], bmx[:, :, :].broadcast_to([PAIRS, 2, T]),
                              ALU.subtract).then_inc(h_pad, 1)
            dve.wait_ge(h_ex, 1)
            link(dve.tensor_reduce(bmx[:, :, :], ba[:, :, 0:T], AX.X, ALU.add))
            link(dve.reciprocal(bmx[:, :, :], bmx[:, :, :]))
            link(dve.tensor_tensor(ba[:, :, 0:T], ba[:, :, 0:T], bmx[:, :, :].broadcast_to([PAIRS, 2, T]), ALU.mult))
            dve.tensor_tensor(x4[0:PAIRS, :, :], ba[:, :, :].rearrange("p u i -> p (u i)").unsqueeze(1).broadcast_to([PAIRS, PAIRS, P]),
                              ident[0:PAIRS, 0:PAIRS].unsqueeze(2).broadcast_to([PAIRS, PAIRS, P]), ALU.mult).then_inc(h_R, 1)
            dve.wait_ge(h_bc, 1)
            link(dve.tensor_tensor(x4[:, :, :].rearrange("p t i -> p (t i)"), xnT[:, :, :].rearrange("p t i -> p (t i)"),
                                   PS[:, 0:4, :].rearrange("p a b -> p (a b)"), ALU.mult))
            link(dve.tensor_reduce(hcb[:, :], x4[:, :, :].rearrange("p t (u i) -> p (t u) i", u=2), AX.X, ALU.add))
            dve.tensor_tensor(x4[:, :, :].rearrange("p t (u i) -> p (t u) i", u=2),
                              xnT[:, :, :].rearrange("p t (u i) -> p (t u) i", u=2),
                              hcb[:, :].unsqueeze(2).broadcast_to([P, B, HALF]), ALU.mult).then_inc(h_x4, 1)

            def z_stats(t, k):
                dve.wait_ge(c_cp, t + 1)
                dve.bn_stats(st[:, t], res[:, t]).then_inc(c_st, 1)

            def z_sum(t, k):
                dve.wait_ge(c_mm, t + 1)
                if not before(t, 2):
                    dve.wait_ge(c_T, t - 1)
                dve.scalar_tensor_tensor(out=zT[:, k], in0=PS[:, 4 + k, 0:P], scalar=bqv[:, :], in1=xnT[:, t],
                                         op0=ALU.add, op1=ALU.add).then_inc(c_z, 1)
                if not before(t, 1):
                    z_stats(t - 1, 1 - k)

            tiles(dve, PAIRS, 2, z_sum)
            z_stats(PAIRS - 1, 1)
            dve.wait_ge(c_cp, PAIRS)
            norm_factors(2, c_st, PAIRS)

            def x2_copy(t, k):
                dve.wait_ge(d_cp, t + 1)
                if not before(t, 2):
                    dve.wait_ge(d_h, t - 1)
                dve.tensor_copy(x2s[:, k], x2T[:, t]).then_inc(d_x2s, 1)

            def norm2(t, k):
                if not before(t, 2):
                    dve.wait_ge(d_T, t - 1)
                    dve.wait_ge(d_acc, t - 1)
                dve.tensor_scalar(xn[:, k], res[:, t], mv[:, t, 0:1], rstd[:, bass.ds(t, 1)], ALU.subtract,
                                  ALU.mult).then_inc(d_xn, 1)
                if not before(t, 1):
                    x2_copy(t - 1, 1 - k)

            tiles(dve, PAIRS, 2, norm2)
            x2_copy(PAIRS - 1, 1)

            dve.wait_ge(d_h, PAIRS)
            hps = PS[:, 2:4, :].rearrange("p a (t n) -> p (a t) n", n=R1)

            def rows(v):
                return v[:, :].unsqueeze(1).broadcast_to([P, PAIRS, R1])

            def cols(v):
                return v.unsqueeze(2).broadcast_to([P, PAIRS, R1])

            link(dve.tensor_tensor(rt2, hps, rows(br1_b), ALU.add))
            link(dve.tensor_reduce(rstat[:, 0], rt2, AX.X, ALU.add))
            link(dve.tensor_scalar(rstat[:, 0], rstat[:, 0], -1.0 / R1, None, ALU.mult))
            dve.tensor_tensor(rt0, rt2, cols(rstat[:, 0]), ALU.add).then_inc(r_hc, 1)
            dve.wait_ge(r_sq, 1)
            dve.tensor_reduce(rstat[:, 1], rt1, AX.X, ALU.add).then_inc(r_vs, 1)
            dve.wait_ge(r_sd, 1)
            link(dve.reciprocal(rstat[:, 2], rstat[:, 1]))
            link(dve.tensor_tensor(rt0, rt0, cols(rstat[:, 2]), ALU.mult))
            link(dve.tensor_tensor(rt0, rt0, rows(lns_b), ALU.mult))
            dve.tensor_tensor(rt0, rt0, rows(lnb_b), ALU.add).then_inc(r_ln, 1)
            dve.wait_ge(r_lg, 1)
            link(dve.tensor_tensor(lg[:, :, :], PS[:, 6, 0:P].rearrange("p (t e) -> p t e", e=E),
                                   br2_b[:, :].unsqueeze(1).broadcast_to([P, PAIRS, E]), ALU.add))
            for t in range(PAIRS):
                last = dve.max(top[:, t], lg[:, t])
            link(last)
            dve.tensor_tensor(pw[:, 0], top[:, :, 1], top[:, :, 0], ALU.subtract).then_inc(r_dif, 1)
            for t in range(PAIRS):
                last = dve.max_index(topi[:, t], top[:, t], lg[:, t])
            link(last)
            link(dve.tensor_copy(topf[:, :, :], topi[:, :, :]))
            for i in range(2):
                link(dve.tensor_tensor(oh[:, i], topf[:, :, i:i + 1].broadcast_to([P, PAIRS, E]),
                                       iota_e[:, :].unsqueeze(1).broadcast_to([P, PAIRS, E]), ALU.is_equal))
            dve.wait_ge(r_exp, 1)
            link(dve.tensor_scalar(pw[:, 2], pw[:, 1], 1.0, None, ALU.add))
            link(dve.reciprocal(pw[:, 2], pw[:, 2]))
            link(dve.tensor_tensor(pw[:, 3], pw[:, 1], pw[:, 2], ALU.mult))
            for i in range(2):
                link(dve.tensor_tensor(oh[:, i], oh[:, i], pw[:, 2 + i].unsqueeze(2).broadcast_to([P, PAIRS, E]), ALU.mult))
            dve.tensor_tensor(gate[:, :, :], oh[:, 0], oh[:, 1], ALU.add).then_inc(r_gate, 1)
            dve.wait_ge(r_gate, 1)
            dve.tensor_tensor(x4[:, :, :], b2r[:, :].unsqueeze(1).broadcast_to([P, PAIRS, P]),
                              headmask[:, :].unsqueeze(2).broadcast_to([P, PAIRS, P]), ALU.mult).then_inc(f_b2b, 1)
            dve.wait_ge(r_b2, 1)
            dve.wait_ge(d_acc, PAIRS)
            dve.tensor_tensor(acc[:, :, :].rearrange("p t i -> p (t i)"), acc[:, :, :].rearrange("p t i -> p (t i)"),
                              PS[:, 0:4, :].rearrange("p a b -> p (a b)"), ALU.add).then_inc(r_acc, 1)
            dve.wait_ge(r_acc, 1)

            def add_expert(e, n):
                s = NCK * e + n
                dve.wait_ge(f_y, s + 1)
                if not before(s, NCK):
                    dve.wait_ge(f_acc, s - NCK + 1)
                for q in range(4):
                    t = 4 * n + q
                    last = dve.scalar_tensor_tensor(out=acc[:, t], in0=PS[:, 4 + n % 2, q * P:(q + 1) * P],
                                                    scalar=gate[:, t, bass.ds(e, 1)], in1=acc[:, t],
                                                    op0=ALU.mult, op1=ALU.add)
                last.then_inc(f_acc, 1)

            def expert(e, k):
                dve.wait_ge(w_loaded[k], 24 * (e - k) + 48)
                for n in range(NCK):
                    for f in range(FT):
                        s = n * FT + f
                        v = NCK * FT * e + s
                        dve.wait_ge(f_g, v + 1)
                        if f == 0 and not before(NCK * e + n, 2):
                            dve.wait_ge(f_y, NCK * e + n - 1)
                        dve.scalar_tensor_tensor(out=gT[:, n % 2, f], in0=PS[:, s % 2], scalar=b1s[:, k, f:f + 1],
                                                 in1=g2[:, s % 2], op0=ALU.add, op1=ALU.mult).then_inc(f_gT, 1)
                        if f == 1 and not before(NCK * e + n, 1):
                            if n:
                                add_expert(e, n - 1)
                            else:
                                add_expert(e - 1, NCK - 1)

            tiles(dve, E, 2, expert, head=2)
            add_expert(E - 1, NCK - 1)
            dve.wait_ge(f_acc, NCK * E)
            with dve.Fori(0, PAIRS, 1) as t:
                dve.bn_stats(st[:, t], acc[:, t]).then_inc(o_st, 1)
            norm_factors(3, o_st, PAIRS)
            for i, op in enumerate((ALU.subtract, ALU.mult)):
                src = acc if i == 0 else res
                v = mv[:, :, 0:1] if i == 0 else rstd[:, :].unsqueeze(2)
                dve.tensor_tensor(res[:, :, :], src[:, :, :], v.broadcast_to([P, PAIRS, P]), op).then_inc(o_y, 1)
                dve.wait_ge(o_y, i + 1)


def kernel(**inputs):
    import numpy as np
    import concourse.bacc as bacc
    from concourse.bass_utils import run_bass_kernel_spmd

    given = {n: np.ascontiguousarray(v) for n, v in inputs.items()}
    B, T, D = given["x"].shape
    given["xT"] = given["x"].reshape(B // 2, 2, T, D).transpose(3, 0, 1, 2)
    given["wqT"] = given["L0_attn_Wq"].T
    given["wkT"] = given["L0_attn_Wk"].T
    given["wvT"] = given["L0_attn_Wv"].T
    given["woT"] = given["L0_attn_Wo"].T
    given["projT"] = given["L0_attn_proj"].transpose(0, 2, 1).reshape(D, -1)
    given["wsimT"] = given["L0_xattn_w_sim"].reshape(3, D).T
    given["b1c"] = given["L0_ffn_b1"].reshape(8, -1, D).transpose(2, 0, 1)
    for n in ("L0_attn_Wv", "L0_attn_Wo", "L0_attn_proj", "L0_ffn_b1"):
        del given[n]
    nc = bacc.Bacc("TRN2", target_bir_lowering=False, num_devices=1)
    arrays, aps = {}, {}
    for n, v in given.items():
        v = np.ascontiguousarray(v)
        arrays["in_" + n] = v
        aps[n] = nc.dram_tensor("in_" + n, v.shape, mybir.dt.from_np(v.dtype), kind="ExternalInput").ap()
    out = nc.dram_tensor("out_0", (B, T, D), mybir.dt.float32, kind="ExternalOutput").ap()
    build(nc, aps, out)
    return run_bass_kernel_spmd(nc, [arrays], core_ids=[0]).results[0]["out_0"]
```

```python
from contextlib import ExitStack

import concourse.bass as bass
from concourse import mybir

F32 = mybir.dt.float32
BF16 = mybir.dt.bfloat16
I32 = mybir.dt.int32
U32 = mybir.dt.uint32
ALU = mybir.AluOpType
ACT = mybir.ActivationFunctionType
AX = mybir.AxisListType

P = 128
HALF = 64


def tiles(eng, count, ring, body, head=4):
    turns = (count - head - ring) // ring
    for t in range(head):
        body(t, t % ring)
    if turns > 0:
        with eng.Fori(head, head + ring * (turns - 1) + 1, ring) as t0:
            for k in range(ring):
                body(t0 + k, (head + k) % ring)
    for t in range(head + ring * max(turns, 0), count):
        body(t, t % ring)


def before(t, n):
    return isinstance(t, int) and t < n


def build(nc, a, out):
    B, T, D = a["x"].shape
    J = a["ctx_1024"].shape[1]
    H, DK, M = 16, 8, 32
    HM = H * M
    PAIRS = B // 2
    CH = 12
    JP = J // CH
    CG = 4
    NG = CH // CG
    W = CG * JP
    CR = 4
    E = a["L0_ffn_W1"].shape[0]
    R1 = D // 2
    F = a["L0_ffn_W2"].shape[1]
    FT = F // P
    NT = PAIRS * P
    FULL = B * T // P
    KT = 2 * B * T // P + E - 1
    assert (D, T, J, JP * CH) == (P, 56, 1500, J) and JP <= P and B * T % P == 0

    accd = [nc.dram_tensor(f"accumulated{i}", (NT, D), F32, kind="Internal").ap() for i in range(2)]
    x2d = nc.dram_tensor("x2_rows", (NT, D), F32, kind="Internal").ap()

    with ExitStack() as ctx:
        def sb(name, shape, dt=F32):
            return ctx.enter_context(nc.sbuf_tensor(name, shape, dt))

        def sem(name):
            return ctx.enter_context(nc.semaphore(name))

        PS = ctx.enter_context(nc.psum_tensor("PS", [P, 8, 512], F32))

        ident = sb("ident", [P, P])
        ones_bf = sb("ones_bf", [P, P], BF16)
        below = sb("below", [P, P], BF16)
        ones16 = sb("ones16", [PAIRS, P])
        headmask = sb("headmask", [P, H])
        kvmask = sb("kvmask", [P, 4, 4, DK + 1])
        iota = sb("iota", [P, P])
        token_id = sb("token_id", [P, PAIRS])
        real = sb("real", [P, 1])
        eps5 = sb("eps5", [P, 1])
        eps6 = sb("eps6", [P, 1])
        zero = sb("zero", [P, P])
        wqkvT = sb("wqkvT", [P, 3, P])
        wqk = sb("wqk", [P, 2, P])
        woT = sb("woT", [P, P])
        projT = sb("projT", [P, M])
        pblk = sb("pblk", [P, H, M])
        wfeat = sb("wfeat", [P, 2, HM])
        bo_b = sb("bo_b", [P, D])
        wsim = sb("wsim", [P, 3])
        w1_b = sb("w1_b", [P, D])
        bsim = sb("bsim", [PAIRS, 1])
        wqv = sb("wqv", [P, 4, P])
        bqv = sb("bqv", [P, 1])
        wr1 = sb("wr1", [P, R1])
        wr2 = sb("wr2", [P, 2, E])
        br1_b = sb("br1_b", [P, R1])
        lns_b = sb("lns_b", [P, R1])
        lnb_b = sb("lnb_b", [P, R1])
        br2_b = sb("br2_b", [P, E])
        b2b = sb("b2b", [P, E, D])
        w1s = sb("w1s", [P, E, 2 * F])

        xT = sb("xT", [P, 2, P])
        xn_in = sb("xn_in", [P, 2, P])
        sq = sb("sq", [P, 2, 2 * P])
        mx = sb("mx", [P, 2, 2 * H])
        nr = sb("nr", [P, 2, 2 * H])
        cc = sb("cc", [P, 2, 2 * H])
        phi = sb("phi", [P, 2, 2 * HM])
        vv = sb("vv", [P, 2, H, DK + 1])
        phT = sb("phT", [P, 2, HM])
        kvs = sb("kvs", [P, 2, 2, H * (DK + 1)])
        den = sb("den", [P, 2, H])
        rden = sb("rden", [P, 2, H])
        mg = sb("mg", [P, 2, P])
        mgT = sb("mgT", [P, 2, P])
        xb = sb("xb", [P, 4, P])
        wide = sb("wide", [P, 2, PAIRS, P])
        res, hqT = wide[:, 0], wide[:, 1]
        st = sb("st", [P, PAIRS, 6])
        mv = sb("mv", [P, PAIRS, 2])
        rstd = sb("rstd", [P, PAIRS])
        xn = sb("xn", [P, 2, P])
        tmpr = sb("tmpr", [P, P])

        arena = sb("arena", [P, CR * 2 * CH * P])
        cx = arena[:, :].rearrange("p (r b c d) -> p r b c d", r=CR, b=2, c=CH)
        turned = sb("turned", [P, 2 * 2 * J])
        cxT = turned[:, :].rearrange("p (u b j) -> p u b j", u=2, b=2)
        mid = sb("mid", [P, J + NG * 4 * P])
        ex = mid[:, 0:J]
        etT = mid[:, J:].rearrange("p (g c i) -> p g c i", g=NG, c=CG)
        xnT = sb("xnT", [P, PAIRS, P])
        xw = sb("xw", [P, 2, P])
        rs = sb("rs", [P, 2, 1])
        m3 = sb("m3", [P, NG])
        nm = sb("nm", [P, 2, 1])
        s3 = sb("s3", [P, 2, NG])
        s1 = sb("s1", [P, 1])
        rz = sb("rz", [P, 2, 1])
        hq = sb("hq", [P, P])
        rm_all = sb("rm_all", [P, PAIRS])
        rT = sb("rT", [PAIRS, 2, HALF])
        ba = sb("ba", [PAIRS, 2, HALF])
        bmx = sb("bmx", [PAIRS, 2, 1])
        hcb = sb("hcb", [P, B])
        zT = sb("zT", [P, 2, P])
        x3 = turned[:, 0:NT].rearrange("p (t i) -> p t i", t=PAIRS)
        x4 = turned[:, NT:2 * NT].rearrange("p (t i) -> p t i", t=PAIRS)

        x2 = xnT
        x2s = sb("x2s", [P, 2, P])
        rt0, rt1, rt2 = (turned[:, i * PAIRS * R1:(i + 1) * PAIRS * R1].rearrange("p (t n) -> p t n", t=PAIRS)
                         for i in range(3))
        rstat = sb("rstat", [P, 3, PAIRS])
        hrT = mid[:, J:J + PAIRS // 2 * P].rearrange("p (q n) -> p q n", q=PAIRS // 2)
        lg = sb("lg", [P, PAIRS, E])
        top = sb("top", [P, PAIRS, 8])
        topi = sb("topi", [P, PAIRS, 8], U32)
        topf = sb("topf", [P, PAIRS, 8])
        pw = sb("pw", [P, 4, PAIRS])
        oh = sb("oh", [P, 2, PAIRS, E])
        chosen = sb("chosen", [P, PAIRS, E], BF16)
        scan_t = sb("scan_t", [P, 2, 8 + PAIRS, E])
        scan_e = sb("scan_e", [P, 2, 4 + E])
        full = mid[:, KT * E:KT * E + E * FULL].rearrange("p (e n) -> p e n", e=E)
        slot = sb("slot", [P, PAIRS, E])
        sel = sb("sel", [P, 2, PAIRS, E])
        slf = sb("slf", [P, 2 * PAIRS])
        slu = sb("slu", [P, 3, 2 * PAIRS], U32)
        slh = sb("slh", [P, 2, 2 * PAIRS])
        late_tile = mid[:, 0:KT * E].rearrange("p (k e) -> p k e", k=KT)
        ekf = sb("ekf", [P, KT])
        eki = sb("eki", [P, KT], I32)
        which = wide[:, :, :, :].rearrange("p a t i -> p (a t) i")
        what = turned[:, 0:2 * PAIRS * 3 * KT].rearrange("p (n c k) -> p n c k", n=2 * PAIRS, c=3)

        b1b = arena[:, 0:E * 2 * F].rearrange("p (e f) -> p e f", e=E)
        w2s = arena[:, E * 2 * F:E * 2 * F + E * FT * D].rearrange("p (e f d) -> p e f d", e=E, f=FT)
        gidx = sb("gidx", [P, KT], U32)
        sidx = sb("sidx", [P, KT], U32)
        tmpk = sb("tmpk", [P, KT])
        wk = sb("wk", [P, KT])
        gs = sb("gs", [P, 2, 1], U32)
        ss = sb("ss", [P, 2, 1], U32)
        beat = sb("beat", [P, 1])
        xg = sb("xg", [P, 2, P])
        xgT = sb("xgT", [P, 2, P])
        h1, h2, gg, gT = (turned[:, i * 2 * F:(i + 1) * 2 * F].rearrange("p (u f) -> p u f", u=2) for i in range(4))
        yb = sb("yb", [P, 2, P])
        ys = sb("ys", [P, 2, P])

        consts_loaded = sem("consts_loaded")
        late_loaded = sem("late_loaded")
        pool_consts = sem("pool_consts")
        dve_consts = sem("dve_consts")
        composite = sem("composite")
        composite_sb = sem("composite_sb")
        xT_loaded = [sem(f"xT_loaded{i}") for i in range(2)]
        x_loaded = [sem(f"x_loaded{i}") for i in range(2)]
        ctx_loaded = [sem(f"ctx_loaded{i}") for i in range(CR)]
        (a_qkv, a_feat, a_kv, a_phT, a_num, a_mT, a_wo, a_sq, a_exp, a_v, a_phTs, a_mTs, a_max, a_nrm, a_c, a_sub,
         a_kvm, a_dn, a_rc, a_mg, a_res, a_st, a_phi, a_xb) = (sem("a_" + n) for n in (
             "qkv feat kv phT num mT wo sq exp v phTs mTs max nrm c sub kvm dn rc mg res st phi xb").split())
        ln_ag, ln_sd, ln_rs = sem("ln_ag"), sem("ln_sd"), sem("ln_rs")
        (b_T, b_evA, b_evD, b_S, b_mx, b_nm, b_exp, b_ET, b_etD, b_etA, b_pv, b_hq, b_HT, b_hqT, b_xn, b_XT, b_xnT,
         b_xw, b_rs, b_rm, b_sum, b_rz) = (sem("b_" + n) for n in (
             "T evA evD S mx nm exp ET etD etA pv hq HT hqT xn XT xnT xw rs rm sum rz").split())
        h_tr, h_cp, h_sub, h_ex, h_R, h_bc, h_x3, h_x4 = (sem("h_" + n) for n in "tr cp sub ex R bc x3 x4".split())
        c_mm, c_z, c_T, c_cp, c_st = (sem("c_" + n) for n in "mm z T cp st".split())
        d_xn, d_T, d_cp, d_x2, d_h, d_rows, d_zero = (sem("d_" + n) for n in "xn T cp x2 h rows zero".split())
        (r_hc, r_sq, r_vs, r_sd, r_ln, r_ge, r_T, r_Tc, r_lg, r_dif, r_exp, r_chosen, r_rank, r_what, r_table,
         r_index, r_experts) = (sem("r_" + n) for n in (
             "hc sq vs sd ln ge T Tc lg dif exp chosen rank what table index experts").split())
        w1_loaded, w2_loaded = sem("w1_loaded"), sem("w2_loaded")
        (f_gs, f_ss, f_X, f_xT, f_H2, f_H1, f_h2, f_h1, f_ge, f_g, f_G, f_gT, f_Y, f_yb, f_ys) = (
            sem("f_" + n) for n in "gs ss X xT H2 H1 h2 h1 ge g G gT Y yb ys".split())
        gathered = [sem(f"gathered{i}") for i in range(2)]
        added = [sem(f"added{i}") for i in range(2)]
        o_in, o_sum, o_st, o_y, o_done = (sem("o_" + n) for n in "in sum st y done".split())
        chain = sem("chain")

        block = ctx.enter_context(nc.Block())

        psF = PS[:, 0:2, :].rearrange("p a b -> p (a b)")
        psQ = PS[:, 2, :]
        psT = PS[:, 3, :]
        psKV = PS[:, 4:6, 0:H * (DK + 1)]
        psN = PS[:, 6, :]
        psW = PS[:, 7, :]
        num = psN[:, 0:H * (DK + 1)].rearrange("p (h c) -> p h c", h=H)
        psS = PS[:, 0:3, 0:W]
        psC = PS[:, 3:5, 0:W]
        psE = PS[:, 5:7, :]
        psO = PS[:, 7, 0:P]
        psG = PS[:, 5, :]

        CONSTS = [
            (wqkvT[:, 0, :], a["wqT"]), (wqkvT[:, 1, :], a["wkT"]), (wqkvT[:, 2, :], a["wvT"]),
            (wqk[:, 0, :], a["L0_attn_Wq"]), (wqk[:, 1, :], a["L0_attn_Wk"]), (projT[:, :], a["projT"]),
            (woT[:, :], a["woT"]), (bo_b[:, :], a["L0_attn_bo"].partition_broadcast(P)),
        ]
        LATE = [
            (wsim[:, :], a["wsimT"]), (w1_b[:, :], a["L0_xattn_w_sim"][0:D].partition_broadcast(P)),
            (bsim[:, :], a["L0_xattn_b_sim"].partition_broadcast(PAIRS)),
            (wqv[:, :, :], a["L0_xattn_W_qv"].rearrange("(k p) n -> p k n", p=P)),
            (bqv[:, :], a["L0_xattn_b_qv"].rearrange("(p a) -> p a", a=1)),
            (wr1[:, :], a["L0_ffn_Wr1"]),
            (wr2[0:R1, 0, :], a["L0_ffn_Wr2"]), (wr2[R1:P, 1, :], a["L0_ffn_Wr2"]),
            (br1_b[:, :], a["L0_ffn_br1"].partition_broadcast(P)),
            (lns_b[:, :], a["L0_ffn_ln_scale"].partition_broadcast(P)),
            (lnb_b[:, :], a["L0_ffn_ln_bias"].partition_broadcast(P)),
            (br2_b[:, :], a["L0_ffn_br2"].partition_broadcast(P)),
            (b2b[:, :, :], a["L0_ffn_b2"].partition_broadcast(P)),
        ]
        POOL_CONSTS = 23

        @block.sync
        def _(sp):
            for dst, src in CONSTS:
                sp.dma_start(dst, src).then_inc(consts_loaded, 16)

            def load_x(t, k):
                if not before(t, 2):
                    sp.wait_ge(a_feat, t - 1)
                    sp.wait_ge(a_xb, t - 1)
                sp.dma_start(xT[:, k, :].rearrange("p (b i) -> p b i", b=2)[:, :, 0:T],
                             a["xT"][:, t, :, :]).then_inc(xT_loaded[k], 16)
                for b in range(2):
                    sp.dma_start(xn_in[b * HALF:b * HALF + T, k, :], a["x"][2 * t + b]).then_inc(x_loaded[k], 16)

            def load_ctx(p, k):
                if not before(p, CR):
                    sp.wait_ge(b_pv, p - CR + 1)
                cut = JP // 16 * 16
                for b in range(2):
                    src = a["ctx_1024"][2 * p + b].rearrange("(p c) d -> p c d", c=CH)
                    sp.dma_start(cx[0:cut, k, b], src[0:cut]).then_inc(ctx_loaded[k], 16)
                    sp.dma_start(cx[cut:JP, k, b], src[cut:JP]).then_inc(ctx_loaded[k], 16)

            sp.wait_ge(pool_consts, 2)
            load_x(0, 0)
            load_x(1, 1)
            load_ctx(0, 0)
            with sp.Fori(2, PAIRS - 1, 2) as t0:
                for k in range(2):
                    load_x(t0 + k, k)
            for p in range(1, CR):
                load_ctx(p, p)
            for e in range(E):
                sp.dma_start(w1s[:, e, :], a["L0_ffn_W1"][e]).then_inc(w1_loaded, 16)
            sp.wait_ge(pool_consts, POOL_CONSTS)
            sp.dma_start(accd[1].rearrange("(p t) d -> p t d", t=PAIRS),
                         zero[:, :].unsqueeze(1).broadcast_to([P, PAIRS, D])).then_inc(d_zero, 16)
            with sp.Fori(CR, PAIRS - CR + 1, CR) as p0:
                for k in range(CR):
                    load_ctx(p0 + k, k)
            sp.wait_ge(b_pv, PAIRS)
            for e in range(E):
                sp.dma_start(w2s[:, e], a["L0_ffn_W2"][e].rearrange("(f p) n -> p f n", p=P)).then_inc(w2_loaded, 16)
            for e in range(E):
                sp.dma_start(b1b[:, e], a["L0_ffn_b1"][e].partition_broadcast(P)).then_inc(w2_loaded, 16)
            sp.wait_ge(d_x2, PAIRS)
            for dst in (x2d, accd[0]):
                sp.dma_start(dst.rearrange("(p t) d -> p t d", t=PAIRS), x2[:, :, :]).then_inc(d_rows, 16)

            sp.wait_ge(added[0], 16 * ((KT + 1) // 2))
            sp.wait_ge(added[1], 16 * (KT // 2))
            for i in range(2):
                sp.dma_start(wide[:, i], accd[i].rearrange("(p t) d -> p t d", t=PAIRS)).then_inc(o_in, 16)
            sp.wait_ge(o_y, 2)
            for b in range(2):
                sp.dma_start(out.rearrange("(t b) i d -> b i t d", b=2)[b],
                             wide[b * HALF:b * HALF + T, 0]).then_inc(o_done, 16)
            sp.wait_ge(o_done, 32)

        @block.gpsimd
        def _(pool):
            pool.memset(xT[:, :, :], 0.0).then_inc(pool_consts, 1)
            pool.memset(xn_in[:, :, :], 0.0).then_inc(pool_consts, 1)
            pool.memset(ident[:, :], 0.0).then_inc(pool_consts, 1)
            pool.memset(headmask[:, :], 1.0).then_inc(pool_consts, 1)
            pool.memset(kvmask[:, :, :, :], 1.0).then_inc(pool_consts, 1)
            pool.memset(vv[:, :, :, :], 1.0).then_inc(pool_consts, 1)
            pool.memset(eps6[:, :], 1e-6).then_inc(pool_consts, 1)
            pool.wait_ge(pool_consts, 7)
            pool.affine_select(out=headmask[:, :], in_=headmask[:, :], compare_op=ALU.is_ge, fill=0.0, base=0,
                               pattern=[[-DK, H]], channel_multiplier=1).then_inc(pool_consts, 1)
            pool.affine_select(out=ident[:, :], in_=ident[:, :], compare_op=ALU.not_equal, fill=1.0, base=0,
                               pattern=[[-1, P]], channel_multiplier=1).then_inc(pool_consts, 1)
            pool.affine_select(out=kvmask[:, :, :, :], in_=kvmask[:, :, :, :], compare_op=ALU.is_ge, fill=0.0, base=0,
                               pattern=[[0, 4], [-M, 4], [0, DK + 1]], channel_multiplier=1).then_inc(pool_consts, 1)
            pool.wait_ge(pool_consts, 10)
            pool.affine_select(out=headmask[:, :], in_=headmask[:, :], compare_op=ALU.is_ge, fill=0.0, base=DK - 1,
                               pattern=[[DK, H]], channel_multiplier=-1).then_inc(pool_consts, 1)
            pool.affine_select(out=kvmask[:, :, :, :], in_=kvmask[:, :, :, :], compare_op=ALU.is_ge, fill=0.0,
                               base=M - 1, pattern=[[0, 4], [M, 4], [0, DK + 1]],
                               channel_multiplier=-1).then_inc(pool_consts, 1)
            pool.memset(wr2[:, :, :], 0.0).then_inc(pool_consts, 1)
            pool.memset(eps5[:, :], 1e-5).then_inc(pool_consts, 1)
            pool.memset(ba[:, :, :], 0.0).then_inc(pool_consts, 1)
            pool.memset(ones_bf[:, :], 1.0).then_inc(pool_consts, 1)
            pool.memset(ones16[:, :], 1.0).then_inc(pool_consts, 1)
            pool.memset(below[:, :], 1.0).then_inc(pool_consts, 1)
            pool.memset(zero[:, :], 0.0).then_inc(pool_consts, 1)
            pool.iota(iota[:, :], [[1, P]], base=0, channel_multiplier=0,
                      allow_small_or_imprecise_dtypes=True).then_inc(pool_consts, 1)
            pool.iota(token_id[:, :], [[1, PAIRS]], base=0, channel_multiplier=PAIRS,
                      allow_small_or_imprecise_dtypes=True).then_inc(pool_consts, 1)
            pool.wait_ge(pool_consts, 21)
            pool.affine_select(out=below[:, :], in_=below[:, :], compare_op=ALU.is_ge, fill=0.0, base=-1,
                               pattern=[[1, P]], channel_multiplier=-1).then_inc(pool_consts, 1)
            pool.memset(scan_e[:, :, :], 0.0).then_inc(pool_consts, 1)
            pool.wait_ge(pool_consts, POOL_CONSTS)
            for dst, src in LATE:
                pool.dma_start(dst, src).then_inc(late_loaded, 16)
            pool.wait_ge(consts_loaded, 16 * len(CONSTS))

            def attention(t, k):
                x = k % 2
                pool.wait_ge(x_loaded[x], 16 * (t - x) + 32)
                if not before(t, 4):
                    pool.wait_ge(a_res, t - 3)
                pool.tensor_tensor(xb[:, k], xn_in[:, x], bo_b[:, :], ALU.add).then_inc(a_xb, 1)

            tiles(pool, PAIRS, 4, attention)

            def row_sums(p, k):
                pool.wait_ge(b_nm, p + 1)
                pool.wait_ge(b_rs, p + 1)
                pool.tensor_tensor(rm_all[:, bass.ds(p, 1)], rs[:, k % 2], nm[:, k % 2], ALU.subtract).then_inc(b_rm, 1)

            tiles(pool, PAIRS, CR, row_sums)
            pool.wait_ge(b_hqT, PAIRS)
            pool.wait_ge(b_S, NG * PAIRS)
            pool.tensor_tensor(x3, xnT[:, :, :], hqT, ALU.mult).then_inc(h_x3, 1)

            def keep_rows(t, k):
                pool.wait_ge(d_xn, t + 1)
                pool.tensor_copy(x2[:, t], xn[:, k]).then_inc(d_x2, 1)

            tiles(pool, PAIRS, 2, keep_rows)

            top_row = pool.to_reg(NT - 1)

            def pass_on():
                pool.tensor_tensor(beat[:, :], zero[:, 0:1], zero[:, 0:1], ALU.add)

            def gather(k, u):
                if not before(k, 2):
                    pool.wait_ge(gathered[u], 8 * (k - u))
                    pool.wait_ge(f_X, k - 1)
                pool.tensor_copy(gs[:, u], gidx[:, bass.ds(k, 1)]).then_inc(f_gs, 1)
                pool.wait_ge(f_gs, k + 1)
                pass_on()
                pool.indirect_dma_start(xg[:, u], None, x2d, bass.IndirectOffsetOnAxis(ap=gs[:, u], axis=0),
                                        bounds_check=top_row, oob_is_err=False).then_inc(gathered[u], 16)

            def scatter(k, u):
                pool.wait_ge(f_ys, k + 1)
                if not before(k, 2):
                    pool.wait_ge(added[u], 8 * (k - u))
                pool.tensor_copy(ss[:, u], sidx[:, bass.ds(k, 1)]).then_inc(f_ss, 1)
                pool.wait_ge(f_ss, k + 1)
                pass_on()
                pool.indirect_dma_start(accd[u], bass.IndirectOffsetOnAxis(ap=ss[:, u], axis=0), ys[:, u], None,
                                        bounds_check=top_row, oob_is_err=False, compute_op=ALU.add).then_inc(added[u], 16)

            LAG = 5

            def expert_tile(k, u):
                gather(k, u)
                if not before(k, LAG):
                    scatter(k - LAG, (u - LAG) % 2)

            pool.wait_ge(r_index, 1)
            pool.wait_ge(d_rows, 32)
            pool.wait_ge(d_zero, 16)
            tiles(pool, KT, 2, expert_tile, head=LAG + 3)
            for k in range(KT - LAG, KT):
                scatter(k, k % 2)

        @block.scalar
        def _(act):
            act.wait_ge(composite, 2)
            act.activation(wfeat[:, :, :], psF.rearrange("p (a b) -> p a b", a=2), ACT.Copy,
                           scale=float(DK) ** -0.5).then_inc(composite_sb, 1)
            act.wait_ge(pool_consts, 12)

            def features(t, k):
                act.wait_ge(a_sub, t + 1)
                act.activation(phi[:, k], phi[:, k], ACT.Exp).then_inc(a_exp, 1)

            def phT_copy(t, k):
                act.wait_ge(a_phT, t + 1)
                if not before(t, 2):
                    act.wait_ge(a_num, t - 1)
                act.activation(phT[:, k], psT, ACT.Identity, bias=eps6[:, :]).then_inc(a_phTs, 1)

            def mT_copy(t, k):
                act.wait_ge(a_mT, t + 1)
                if not before(t, 2):
                    act.wait_ge(a_wo, t - 1)
                act.activation(mgT[:, k], psW[:, 0:P], ACT.Copy).then_inc(a_mTs, 1)

            def attention(t, k):
                if not before(t, 3):
                    mT_copy(t - 3, 1 - k)
                act.wait_ge(a_qkv, t + 1)
                if not before(t, 2):
                    act.wait_ge(a_nrm, t - 1)
                act.activation(sq[:, k], psQ[:, 0:2 * P], ACT.Square, scale=float(2 * DK) ** -0.5).then_inc(a_sq, 1)
                if not before(t, 2):
                    act.wait_ge(a_kv, t - 1)
                act.activation(vv[:, k, :, 0:DK], psQ[:, 2 * P:3 * P].rearrange("p (h d) -> p h d", h=H),
                               ACT.Copy).then_inc(a_v, 1)
                if not before(t, 1):
                    features(t - 1, 1 - k)
                    phT_copy(t - 1, 1 - k)

            tiles(act, PAIRS, 2, attention, head=6)
            mT_copy(PAIRS - 3, 1)
            features(PAIRS - 1, 1)
            phT_copy(PAIRS - 1, 1)
            mT_copy(PAIRS - 2, 0)
            mT_copy(PAIRS - 1, 1)

            act.wait_ge(pool_consts, POOL_CONSTS)
            act.wait_ge(ln_ag, 1)
            act.activation(rstd[:, :], mv[:, :, 1], ACT.Sqrt, bias=eps5[:, :]).then_inc(ln_sd, 1)

            def turned_x(p):
                act.wait_ge(b_XT, p + 1)
                act.activation(xnT[:, p], psO, ACT.Copy).then_inc(b_xnT, 1)

            def turned_ctx(p, u):
                for g in range(3):
                    act.wait_ge(b_T, 6 * p + g + 1)
                    if g == 0 and not before(p, 2):
                        act.wait_ge(b_S, NG * (p - 1))
                    act.activation(cxT[:, u, 0, g * W:(g + 1) * W], psC[:, g % 2], ACT.Copy).then_inc(b_evA, 1)

            def hq_turned(p):
                act.wait_ge(b_HT, p + 1)
                act.activation(hqT[:, p], psO, ACT.Copy).then_inc(b_hqT, 1)

            def cross(p, k, last=False):
                u = k % 2
                if not last:
                    turned_ctx(p + 1, 1 - u)
                if not before(p, 1):
                    hq_turned(p - 1)
                act.wait_ge(b_nm, p + 1)
                if not before(p, 2):
                    act.wait_ge(b_sum, p - 1)
                for g in range(NG):
                    if not before(p, 1):
                        act.wait_ge(b_ET, NG * (p - 1) + g + 1)
                    act.activation(ex[:, g * W:(g + 1) * W], psS[:, g], ACT.Exp, bias=nm[:, u],
                                   accum_out=s3[:, u, g:g + 1]).then_inc(b_exp, 1)
                if not last:
                    turned_x(p + 1)
                act.wait_ge(b_ET, NG * p + 2)
                if not before(p, 1):
                    act.wait_ge(b_pv, p)
                act.activation(etT[0:JP, 1], psE[0:JP, 1].rearrange("p (c i) -> p c i", c=CG),
                               ACT.Copy).then_inc(b_etA, 1)
                act.wait_ge(b_pv, p + 1)
                act.wait_ge(b_rz, p + 1)
                if not before(p, 1):
                    act.wait_ge(b_HT, p)
                act.activation(hq[:, :], psO, ACT.Copy, scale=rz[:, u]).then_inc(b_hq, 1)

            turned_x(0)
            turned_ctx(0, 0)
            cross(0, 0)
            for p in range(1, CR):
                cross(p, p)
            with act.Fori(CR, PAIRS - 2 * CR + 1, CR) as p0:
                for k in range(CR):
                    cross(p0 + k, k)
            for p in range(PAIRS - CR, PAIRS):
                cross(p, p % CR, last=(p == PAIRS - 1))
            hq_turned(PAIRS - 1)

            act.wait_ge(h_tr, 1)
            act.activation(rT[:, :, :], PS[0:PAIRS, 6, 0:P].rearrange("p (u i) -> p u i", u=2), ACT.Copy).then_inc(h_cp, 1)
            act.wait_ge(h_sub, 1)
            act.activation(ba[:, :, 0:T], rT[:, :, 0:T], ACT.Exp).then_inc(h_ex, 1)

            def z_rows(t, k):
                act.wait_ge(c_T, t + 1)
                act.activation(res[:, t], PS[:, 6 + k, 0:P], ACT.Copy).then_inc(c_cp, 1)

            tiles(act, PAIRS, 2, z_rows)
            act.wait_ge(ln_ag, 2)
            act.activation(rstd[:, :], mv[:, :, 1], ACT.Sqrt, bias=eps5[:, :]).then_inc(ln_sd, 1)

            def x2_turned(t, k):
                act.wait_ge(d_T, t + 1)
                if not before(t, 2):
                    act.wait_ge(d_h, t - 1)
                act.activation(x2s[:, k], PS[:, k, 0:P], ACT.Copy).then_inc(d_cp, 1)

            tiles(act, PAIRS, 2, x2_turned)

            act.wait_ge(r_hc, 1)
            act.activation(rt1, rt0, ACT.Square).then_inc(r_sq, 1)
            act.wait_ge(r_vs, 1)
            act.activation(rstat[:, 1], rstat[:, 1], ACT.Sqrt, bias=eps6[:, :], scale=1.0 / R1).then_inc(r_sd, 1)
            act.wait_ge(r_ln, 1)
            act.activation(rt1, rt0, ACT.Gelu_apprx_tanh).then_inc(r_ge, 1)
            act.wait_ge(r_T, 1)
            act.activation(hrT.rearrange("p (a q) n -> p a (q n)", a=2), PS[:, 4:6, :], ACT.Copy).then_inc(r_Tc, 1)
            act.wait_ge(r_dif, 1)
            act.activation(pw[:, 1], pw[:, 0], ACT.Exp).then_inc(r_exp, 1)

            def rows_turned(k, u):
                act.wait_ge(f_X, k + 1)
                if not before(k, 2):
                    act.wait_ge(f_H1, k - 1)
                act.activation(xgT[:, u], PS[:, 0, 0:P], ACT.Copy).then_inc(f_xT, 1)

            def hidden_turned(k, u):
                act.wait_ge(f_G, k + 1)
                if not before(k, 2):
                    act.wait_ge(f_Y, k - 1)
                act.activation(gT[:, u], psG, ACT.Copy).then_inc(f_gT, 1)

            def expert_tile(k, u, last=False):
                if not last:
                    rows_turned(k + 1, 1 - u)
                act.wait_ge(f_h2, k + 1)
                act.activation(h2[:, u], h2[:, u], ACT.Gelu_apprx_tanh).then_inc(f_ge, 1)
                if not before(k, 1):
                    hidden_turned(k - 1, 1 - u)

            rows_turned(0, 0)
            tiles(act, KT - 1, 2, expert_tile)
            expert_tile(KT - 1, (KT - 1) % 2, last=True)
            hidden_turned(KT - 1, (KT - 1) % 2)
            act.wait_ge(ln_ag, 3)
            act.activation(rstd[:, :], mv[:, :, 1], ACT.Sqrt, bias=eps5[:, :]).then_inc(ln_sd, 1)

        @block.tensor
        def _(pe):
            pe.wait_ge(consts_loaded, 16 * len(CONSTS))
            pe.wait_ge(dve_consts, 1)
            for i in range(2):
                pe.matmul(psF[:, i * HM:(i + 1) * HM], wqk[:, i, :], pblk[:, :, :].rearrange("p h m -> p (h m)"),
                          start=True, stop=True).then_inc(composite, 1)
            pe.wait_ge(composite_sb, 1)
            pe.wait_ge(pool_consts, 12)

            def kv_and_turn(t, k):
                pe.wait_ge(a_exp, t + 1)
                if not before(t, 1):
                    pe.wait_ge(a_phTs, t)
                for g in range(4):
                    last = pe.transpose(psT[:, g * P:(g + 1) * P], phi[:, k, g * P:(g + 1) * P], ident[:, :])
                last.then_inc(a_phT, 1)
                pe.wait_ge(a_v, t + 1)
                pe.wait_ge(a_phi, t + 1)
                if not before(t, 1):
                    pe.wait_ge(a_kvm, t)
                for g in range(4):
                    for b in range(2):
                        r = slice(b * HALF, b * HALF + T)
                        last = pe.matmul(psKV[:, b, g * 36:g * 36 + 36], phi[r, k, HM + g * P:HM + (g + 1) * P],
                                         vv[r, k, 4 * g:4 * g + 4, :].rearrange("p h c -> p (h c)"), start=True, stop=True)
                last.then_inc(a_kv, 1)

            def numerators(t, k):
                pe.wait_ge(a_phTs, t + 1)
                pe.wait_ge(a_kvm, t + 1)
                if not before(t, 1):
                    pe.wait_ge(a_mg, t)
                for g in range(4):
                    for b in range(2):
                        last = pe.matmul(psN[b * HALF:(b + 1) * HALF, g * 36:g * 36 + 36],
                                         phT[:, k, g * P + b * HALF:g * P + (b + 1) * HALF],
                                         kvs[:, k, b, g * 36:g * 36 + 36], start=True, stop=True)
                last.then_inc(a_num, 1)

            def turn_merged(t, k):
                pe.wait_ge(a_mg, t + 1)
                if not before(t, 1):
                    pe.wait_ge(a_res, t)
                pe.transpose(psW[:, 0:P], mg[:, k], ident[:, :]).then_inc(a_mT, 1)

            def out_projection(t, k):
                pe.wait_ge(a_mTs, t + 1)
                pe.matmul(psW[:, P:2 * P], mgT[:, k], woT[:, :], start=True, stop=True).then_inc(a_wo, 1)

            def attention(t, k):
                pe.wait_ge(xT_loaded[k], 8 * (t - k) + 16)
                if not before(t, 1):
                    pe.wait_ge(a_sq, t)
                    pe.wait_ge(a_v, t)
                pe.matmul(psQ[:, 0:3 * P], xT[:, k], wqkvT[:, :, :].rearrange("p a b -> p (a b)"),
                          start=True, stop=True).then_inc(a_qkv, 1)
                if not before(t, 3):
                    out_projection(t - 3, 1 - k)
                if not before(t, 1):
                    pe.wait_ge(a_sub, t)
                for i in range(2):
                    last = pe.matmul(psF[:, i * HM:(i + 1) * HM], xT[:, k], wfeat[:, i, :], start=True, stop=True)
                last.then_inc(a_feat, 1)
                if not before(t, 2):
                    numerators(t - 2, k)
                if not before(t, 1):
                    kv_and_turn(t - 1, 1 - k)
                if not before(t, 2):
                    turn_merged(t - 2, k)

            tiles(pe, PAIRS, 2, attention)
            out_projection(PAIRS - 3, 1)
            numerators(PAIRS - 2, 0)
            kv_and_turn(PAIRS - 1, 1)
            turn_merged(PAIRS - 2, 0)
            out_projection(PAIRS - 2, 0)
            numerators(PAIRS - 1, 1)
            turn_merged(PAIRS - 1, 1)
            out_projection(PAIRS - 1, 1)

            def turn_x(p, u):
                pe.wait_ge(b_xn, p + 1)
                if not before(p, 2):
                    pe.wait_ge(b_hqT, p - 1)
                pe.transpose(psO, xn[:, u], ident[:, :]).then_inc(b_XT, 1)

            def turn_ctx(p, k, g):
                if g == 0:
                    pe.wait_ge(ctx_loaded[k], 16 * (p - k) + 64)
                if g >= 2 or not before(p, 1):
                    q, n = (p, g - 2) if g >= 2 else (p - 1, g + 4)
                    pe.wait_ge(b_evA if n < 3 else b_evD, 3 * q + n % 3 + 1)
                for c in range(CG):
                    last = pe.transpose(psC[:, g % 2, c * JP:(c + 1) * JP], cx[0:JP, k, g // 3, (g % 3) * CG + c],
                                        ident[0:JP, 0:JP])
                last.then_inc(b_T, 1)

            def turn_exp(p, g):
                pe.wait_ge(b_exp, NG * p + g + 1)
                if g == 2:
                    pe.wait_ge(b_etD, 2 * p + 1)
                elif not before(p, 1):
                    pe.wait_ge(b_etD, 2 * p) if g == 0 else pe.wait_ge(b_etA, p)
                for c in range(CG):
                    j = g * W + c * JP
                    last = pe.transpose(psE[0:JP, g % 2, c * P:(c + 1) * P], ex[:, j:j + JP], ident[:, :])
                last.then_inc(b_ET, 1)

            def values(p, k, g):
                if g == 1:
                    pe.wait_ge(b_etA, p + 1)
                else:
                    pe.wait_ge(b_etD, 2 * p + 1 + g // 2)
                for c in range(CG):
                    for b in range(2):
                        last = pe.matmul(psO[b * HALF:(b + 1) * HALF], etT[0:JP, g, c, b * HALF:(b + 1) * HALF],
                                         cx[0:JP, k, b, g * CG + c], start=(g == 0 and c == 0),
                                         stop=(g == NG - 1 and c == CG - 1), skip_group_check=True)
                if g == NG - 1:
                    last.then_inc(b_pv, 1)

            def turn_hq(p):
                pe.wait_ge(b_hq, p + 1)
                pe.transpose(psO, hq[:, :], ident[:, :]).then_inc(b_HT, 1)

            def cross(p, k, last=False):
                u, n = k % 2, (k + 1) % CR
                pe.wait_ge(b_xw, p + 1)
                pe.wait_ge(b_evA, 3 * p + 3)
                pe.wait_ge(b_evD, 3 * p + 3)
                for g in range(NG):
                    if not before(p, 1):
                        pe.wait_ge(b_exp, NG * (p - 1) + g + 1)
                    for b in range(2):
                        mm = pe.matmul(psS[b * HALF:(b + 1) * HALF, g], xw[:, u, b * HALF:(b + 1) * HALF],
                                       cxT[:, u, b, g * W:(g + 1) * W], start=True, stop=True)
                    mm.then_inc(b_S, 1)
                    if not last:
                        turn_ctx(p + 1, n, g)
                if not before(p, 1):
                    turn_hq(p - 1)
                if not last:
                    for g in range(3, 6):
                        turn_ctx(p + 1, n, g)
                    turn_x(p + 1, 1 - u)
                turn_exp(p, 0)
                turn_exp(p, 1)
                if last:
                    pe.wait_ge(b_hqT, p)
                else:
                    pe.wait_ge(b_xnT, p + 2)
                values(p, k, 0)
                turn_exp(p, 2)
                values(p, k, 1)
                values(p, k, 2)

            pe.wait_ge(a_st, PAIRS)
            turn_x(0, 0)
            for g in range(6):
                turn_ctx(0, 0, g)
            for p in range(CR):
                cross(p, p)
            with pe.Fori(CR, PAIRS - 2 * CR + 1, CR) as p0:
                for k in range(CR):
                    cross(p0 + k, k)
            for p in range(PAIRS - CR, PAIRS):
                cross(p, p % CR, last=(p == PAIRS - 1))
            turn_hq(PAIRS - 1)

            pe.wait_ge(b_rm, PAIRS)
            pe.wait_ge(b_etA, PAIRS)
            pe.transpose(PS[0:PAIRS, 6, 0:P], rm_all[:, :], ident[:, :]).then_inc(h_tr, 1)
            pe.wait_ge(h_R, 1)
            for n in range(NT // 512):
                last = pe.matmul(PS[:, n, :], ones16[:, :],
                                 x4[0:PAIRS].rearrange("p t i -> p (t i)")[:, n * 512:(n + 1) * 512],
                                 start=True, stop=True)
            last.then_inc(h_bc, 1)

            def turn_z(t, k):
                pe.wait_ge(c_z, t + 1)
                if not before(t, 2):
                    pe.wait_ge(c_cp, t - 1)
                pe.transpose(PS[:, 6 + k, 0:P], zT[:, k], ident[:, :]).then_inc(c_T, 1)

            def project(t, k):
                if not before(t, 2):
                    pe.wait_ge(c_z, t - 1)
                for i, x in enumerate((xnT, hqT, x3, x4)):
                    last = pe.matmul(PS[:, 4 + k, 0:P], wqv[:, i], x[:, t], start=(i == 0), stop=(i == 3))
                last.then_inc(c_mm, 1)
                if not before(t, 1):
                    turn_z(t - 1, 1 - k)

            pe.wait_ge(b_hqT, PAIRS)
            pe.wait_ge(h_x4, 1)
            pe.wait_ge(h_x3, 1)
            tiles(pe, PAIRS, 2, project)
            turn_z(PAIRS - 1, 1)

            def router(t, k):
                pe.wait_ge(d_cp, t + 1)
                pe.matmul(PS[:, 2:4, :].rearrange("p a (t n) -> p (a t) n", n=R1)[:, t, :],
                          x2s[:, k], wr1[:, :], start=True, stop=True).then_inc(d_h, 1)

            def turn_x2(t, k):
                pe.wait_ge(d_xn, t + 1)
                if not before(t, 2):
                    pe.wait_ge(d_cp, t - 1)
                pe.transpose(PS[:, k, 0:P], xn[:, k], ident[:, :]).then_inc(d_T, 1)
                if not before(t, 1):
                    router(t - 1, 1 - k)

            tiles(pe, PAIRS, 2, turn_x2)
            router(PAIRS - 1, 1)

            pe.wait_ge(r_ge, 1)
            for q in range(PAIRS // 2):
                last = pe.transpose(PS[:, 4 + q // 4, (q % 4) * P:(q % 4 + 1) * P],
                                    rt1[:, 2 * q:2 * q + 2, :].rearrange("p a n -> p (a n)"), ident[:, :])
            last.then_inc(r_T, 1)
            pe.wait_ge(r_Tc, 1)
            for q in range(PAIRS // 2):
                last = pe.matmul(PS[:, 6, 2 * q * E:(2 * q + 2) * E], hrT[:, q], wr2[:, :, :].rearrange("p a e -> p (a e)"),
                                 start=True, stop=True)
            last.then_inc(r_lg, 1)
            pe.wait_ge(r_chosen, 1)
            flat = chosen[:, :, :].rearrange("p t e -> p (t e)")
            pe.matmul(PS[:, 0, 0:P], below[:, :], flat, start=True, stop=True)
            pe.matmul(PS[:, 0, P:2 * P], ones_bf[:, :], flat, start=True, stop=True).then_inc(r_rank, 1)
            pe.wait_ge(r_what, 1)
            for n in range(2 * PAIRS):
                last = pe.matmul(PS[:, 7, 0:3 * KT], which[:, n], what[:, n].rearrange("p c k -> p (c k)"),
                                 start=(n == 0), stop=(n == 2 * PAIRS - 1))
            last.then_inc(r_table, 1)

            def turn_rows(k, u):
                pe.wait_ge(gathered[u], 8 * (k - u) + 16)
                if not before(k, 1):
                    pe.wait_ge(f_xT, k)
                pe.transpose(PS[:, 0, 0:P], xg[:, u], ident[:, :]).then_inc(f_X, 1)

            def up(k, u, e):
                pe.wait_ge(f_xT, k + 1)
                for half, done, free in ((1, f_H2, f_h2), (0, f_H1, f_h1)):
                    if not before(k, 2):
                        pe.wait_ge(free, k - 1)
                    pe.matmul(PS[:, 1 + 2 * u + half, :], xgT[:, u],
                              w1s[:, :, :].rearrange("p e (h f) -> p e h f", h=2)[:, e, half, :],
                              start=True, stop=True).then_inc(done, 1)

            def turn_hidden(k, u):
                pe.wait_ge(f_g, k + 1)
                if not before(k, 1):
                    pe.wait_ge(f_gT, k)
                for f in range(FT):
                    last = pe.transpose(psG[:, f * P:(f + 1) * P], gg[:, u, f * P:(f + 1) * P], ident[:, :])
                last.then_inc(f_G, 1)

            def down(k, u, e):
                pe.wait_ge(f_gT, k + 1)
                if not before(k, 2):
                    pe.wait_ge(f_yb, k - 1)
                for f in range(FT):
                    last = pe.matmul(PS[:, 6 + u, 0:P], gT[:, u, f * P:(f + 1) * P], w2s[:, e, f, :],
                                     start=(f == 0), stop=(f == FT - 1))
                last.then_inc(f_Y, 1)

            def expert_of(k):
                return pe.value_load(eki[0:1, bass.ds(k, 1)], min_val=0, max_val=E - 1)

            def expert_tile(k, u, last=False):
                if not last:
                    turn_rows(k + 1, 1 - u)
                up(k, u, expert_of(k))
                if not before(k, 2):
                    down(k - 2, u, expert_of(k - 2))
                if not before(k, 1):
                    turn_hidden(k - 1, 1 - u)

            pe.wait_ge(r_experts, 1)
            pe.wait_ge(w1_loaded, 16 * E)
            pe.wait_ge(w2_loaded, 32 * E)
            turn_rows(0, 0)
            tiles(pe, KT - 1, 2, expert_tile)
            expert_tile(KT - 1, (KT - 1) % 2, last=True)
            down(KT - 2, KT % 2, expert_of(KT - 2))
            turn_hidden(KT - 1, (KT - 1) % 2)
            down(KT - 1, (KT - 1) % 2, expert_of(KT - 1))

        @block.vector
        def _(dve):
            steps = [0]

            def link(ins):
                steps[0] += 1
                ins.then_inc(chain, 1)
                dve.wait_ge(chain, steps[0])

            link(dve.memset(scan_t[:, :, :, :], 0.0))
            dve.wait_ge(pool_consts, 12)
            dve.wait_ge(consts_loaded, 16 * len(CONSTS))
            dve.tensor_tensor(pblk[:, :, :], projT[:, :].unsqueeze(1).broadcast_to([P, H, M]),
                              headmask[:, :].unsqueeze(2).broadcast_to([P, H, M]), ALU.mult).then_inc(dve_consts, 1)

            def keep_kv(t, k):
                dve.wait_ge(a_kv, t + 1)
                if not before(t, 2):
                    dve.wait_ge(a_num, t - 1)
                dve.tensor_tensor(kvs[:, k], psKV, kvmask[:, :, :, :].rearrange("p a b c -> p (a b c)").unsqueeze(1)
                                  .broadcast_to([P, 2, H * (DK + 1)]), ALU.mult).then_inc(a_kvm, 1)

            def merged(t, k):
                dve.wait_ge(a_num, t + 1)
                dve.tensor_scalar(den[:, k], num[:, :, DK], M * 1e-6, None, ALU.add).then_inc(a_dn, 1)
                dve.wait_ge(a_dn, t + 1)
                dve.reciprocal(rden[:, k], den[:, k]).then_inc(a_rc, 1)
                dve.wait_ge(a_rc, t + 1)
                if not before(t, 2):
                    dve.wait_ge(a_mT, t - 1)
                dve.tensor_tensor(mg[:, k].rearrange("p (h d) -> p h d", h=H), num[:, :, 0:DK],
                                  rden[:, k].unsqueeze(2).broadcast_to([P, H, DK]), ALU.mult).then_inc(a_mg, 1)

            def residual(t, k):
                dve.wait_ge(a_wo, t + 1)
                dve.wait_ge(a_xb, t + 1)
                dve.tensor_tensor(res[:, t], psW[:, P:2 * P], xb[:, k], ALU.add).then_inc(a_res, 1)
                dve.wait_ge(a_res, t + 1)
                dve.bn_stats(st[:, t], res[:, t]).then_inc(a_st, 1)

            def key_epsilon(t, k):
                dve.wait_ge(a_exp, t + 1)
                dve.tensor_scalar(phi[:, k, HM:2 * HM], phi[:, k, HM:2 * HM], 1e-6, None, ALU.add).then_inc(a_phi, 1)

            def attention(t, r):
                k = r % 2
                if not before(t, 3):
                    residual(t - 3, (r - 3) % 4)
                dve.wait_ge(a_sq, t + 1)
                if not before(t, 2):
                    dve.wait_ge(a_c, t - 1)
                dve.tensor_reduce(nr[:, k], sq[:, k].rearrange("p (h d) -> p h d", d=DK), AX.X, ALU.add).then_inc(a_nrm, 1)
                if not before(t, 1):
                    key_epsilon(t - 1, 1 - k)
                dve.wait_ge(a_feat, t + 1)
                dve.tensor_reduce(mx[:, k], psF.rearrange("p (h m) -> p h m", m=M), AX.X, ALU.max).then_inc(a_max, 1)
                if not before(t, 2):
                    merged(t - 2, k)
                dve.wait_ge(a_max, t + 1)
                dve.wait_ge(a_nrm, t + 1)
                dve.tensor_tensor(cc[:, k], mx[:, k], nr[:, k], ALU.add).then_inc(a_c, 1)
                dve.wait_ge(a_c, t + 1)
                if not before(t, 2):
                    dve.wait_ge(a_kv, t - 1)
                dve.tensor_tensor(phi[:, k].rearrange("p (h m) -> p h m", m=M), psF.rearrange("p (h m) -> p h m", m=M),
                                  cc[:, k].unsqueeze(2).broadcast_to([P, 2 * H, M]), ALU.subtract).then_inc(a_sub, 1)
                if not before(t, 1):
                    keep_kv(t - 1, 1 - k)

            tiles(dve, PAIRS, 4, attention)
            residual(PAIRS - 3, 1)
            key_epsilon(PAIRS - 1, 1)
            merged(PAIRS - 2, 0)
            keep_kv(PAIRS - 1, 1)
            residual(PAIRS - 2, 2)
            merged(PAIRS - 1, 1)
            residual(PAIRS - 1, 3)

            def norm_factors(n, stats, count):
                dve.wait_ge(stats, count)
                for t in range(PAIRS):
                    last = dve.bn_aggr(mv[:, t], st[:, t])
                last.then_inc(ln_ag, 1)
                dve.wait_ge(ln_sd, n)
                dve.reciprocal(rstd[:, :], rstd[:, :]).then_inc(ln_rs, 1)
                dve.wait_ge(ln_rs, n)

            norm_factors(1, a_st, PAIRS)
            dve.wait_ge(late_loaded, 16 * len(LATE))

            def norm1(p, u):
                if not before(p, 2):
                    dve.wait_ge(b_XT, p - 1)
                dve.tensor_scalar(xn[:, u], res[:, p], mv[:, p, 0:1], rstd[:, bass.ds(p, 1)], ALU.subtract,
                                  ALU.mult).then_inc(b_xn, 1)
                dve.wait_ge(b_xn, p + 1)
                if not before(p, 2):
                    dve.wait_ge(b_rm, p - 1)
                if not before(p, 1):
                    dve.wait_ge(b_rs, p)
                dve.scalar_tensor_tensor(out=tmpr[:, :], in0=xn[:, u], scalar=1.0, in1=w1_b[:, :], op0=ALU.mult,
                                         op1=ALU.mult, accum_out=rs[:, u]).then_inc(b_rs, 1)

            def similarity_weights(p, u):
                dve.wait_ge(b_xnT, p + 1)
                if not before(p, 2):
                    dve.wait_ge(b_S, NG * (p - 1))
                dve.tensor_scalar(xw[:, u], xnT[:, p], wsim[:, 2:3], wsim[:, 1:2], ALU.mult, ALU.add).then_inc(b_xw, 1)

            def turned_ctx(p, u):
                for g in range(3, 6):
                    dve.wait_ge(b_T, 6 * p + g + 1)
                    dve.tensor_copy(cxT[:, u, 1, (g - 3) * W:(g - 2) * W], psC[:, g % 2]).then_inc(b_evD, 1)

            def cross(p, k, last=False):
                u = k % 2
                for g in range(NG):
                    dve.wait_ge(b_S, NG * p + g + 1)
                    if g == 0 and not before(p, 1):
                        dve.wait_ge(b_nm, p)
                    dve.tensor_reduce(m3[:, g:g + 1], psS[:, g], AX.X, ALU.max).then_inc(b_mx, 1)
                dve.wait_ge(b_mx, NG * p + NG)
                if not before(p, 2):
                    dve.wait_ge(b_rm, p - 1)
                    dve.wait_ge(b_exp, NG * (p - 1))
                dve.tensor_reduce(nm[:, u], m3[:, :], AX.X, ALU.max, negate=True).then_inc(b_nm, 1)
                if not last:
                    norm1(p + 1, 1 - u)
                    turned_ctx(p + 1, 1 - u)
                dve.wait_ge(b_ET, NG * p + 1)
                if not before(p, 1):
                    dve.wait_ge(b_pv, p)
                dve.tensor_copy(etT[0:JP, 0], psE[0:JP, 0].rearrange("p (c i) -> p c i", c=CG)).then_inc(b_etD, 1)
                if not last:
                    similarity_weights(p + 1, 1 - u)
                dve.wait_ge(b_exp, NG * p + NG)
                if not before(p, 1):
                    dve.wait_ge(b_rz, p)
                dve.tensor_reduce(s1[:, :], s3[:, u], AX.X, ALU.add).then_inc(b_sum, 1)
                dve.wait_ge(b_ET, NG * p + NG)
                dve.tensor_copy(etT[0:JP, 2], psE[0:JP, 0].rearrange("p (c i) -> p c i", c=CG)).then_inc(b_etD, 1)
                dve.wait_ge(b_sum, p + 1)
                if not before(p, 2):
                    dve.wait_ge(b_hq, p - 1)
                dve.reciprocal(rz[:, u], s1[:, :]).then_inc(b_rz, 1)

            norm1(0, 0)
            similarity_weights(0, 0)
            turned_ctx(0, 0)
            for p in range(CR):
                cross(p, p)
            with dve.Fori(CR, PAIRS - 2 * CR + 1, CR) as p0:
                for k in range(CR):
                    cross(p0 + k, k)
            for p in range(PAIRS - CR, PAIRS):
                cross(p, p % CR, last=(p == PAIRS - 1))

            dve.wait_ge(h_cp, 1)
            rows = rT[:, :, 0:T]
            link(dve.tensor_scalar(rows, rows, bsim[:, :], None, ALU.add))
            link(dve.tensor_reduce(bmx[:, :, :], rows, AX.X, ALU.max))
            dve.tensor_tensor(rows, rows, bmx[:, :, :].broadcast_to([PAIRS, 2, T]), ALU.subtract).then_inc(h_sub, 1)
            dve.wait_ge(h_ex, 1)
            link(dve.tensor_reduce(bmx[:, :, :], ba[:, :, 0:T], AX.X, ALU.add))
            link(dve.reciprocal(bmx[:, :, :], bmx[:, :, :]))
            link(dve.tensor_tensor(ba[:, :, 0:T], ba[:, :, 0:T], bmx[:, :, :].broadcast_to([PAIRS, 2, T]), ALU.mult))
            dve.tensor_tensor(x4[0:PAIRS], ba[:, :, :].rearrange("p u i -> p (u i)").unsqueeze(1).broadcast_to([PAIRS, PAIRS, P]),
                              ident[0:PAIRS, 0:PAIRS].unsqueeze(2).broadcast_to([PAIRS, PAIRS, P]), ALU.mult).then_inc(h_R, 1)
            dve.wait_ge(h_bc, 1)
            link(dve.tensor_tensor(x4.rearrange("p t i -> p (t i)"), xnT[:, :, :].rearrange("p t i -> p (t i)"),
                                   PS[:, 0:4, :].rearrange("p a b -> p (a b)"), ALU.mult))
            link(dve.tensor_reduce(hcb[:, :], x4.rearrange("p t (u i) -> p (t u) i", u=2), AX.X, ALU.add))
            dve.tensor_tensor(x4.rearrange("p t (u i) -> p (t u) i", u=2),
                              xnT[:, :, :].rearrange("p t (u i) -> p (t u) i", u=2),
                              hcb[:, :].unsqueeze(2).broadcast_to([P, B, HALF]), ALU.mult).then_inc(h_x4, 1)

            def z_stats(t, k):
                dve.wait_ge(c_cp, t + 1)
                dve.bn_stats(st[:, t], res[:, t]).then_inc(c_st, 1)

            def z_sum(t, k):
                dve.wait_ge(c_mm, t + 1)
                if not before(t, 2):
                    dve.wait_ge(c_T, t - 1)
                dve.scalar_tensor_tensor(out=zT[:, k], in0=PS[:, 4 + k, 0:P], scalar=bqv[:, :], in1=xnT[:, t],
                                         op0=ALU.add, op1=ALU.add).then_inc(c_z, 1)
                if not before(t, 1):
                    z_stats(t - 1, 1 - k)

            tiles(dve, PAIRS, 2, z_sum)
            z_stats(PAIRS - 1, 1)
            norm_factors(2, c_st, PAIRS)

            def norm2(t, k):
                if not before(t, 2):
                    dve.wait_ge(d_T, t - 1)
                    dve.wait_ge(d_x2, t - 1)
                dve.tensor_scalar(xn[:, k], res[:, t], mv[:, t, 0:1], rstd[:, bass.ds(t, 1)], ALU.subtract,
                                  ALU.mult).then_inc(d_xn, 1)

            tiles(dve, PAIRS, 2, norm2)

            dve.wait_ge(d_h, PAIRS)
            hps = PS[:, 2:4, :].rearrange("p a (t n) -> p (a t) n", n=R1)

            def over_tiles(v):
                return v[:, :].unsqueeze(1).broadcast_to([P, PAIRS, R1])

            def over_units(v):
                return v.unsqueeze(2).broadcast_to([P, PAIRS, R1])

            link(dve.tensor_tensor(rt2, hps, over_tiles(br1_b), ALU.add))
            link(dve.tensor_reduce(rstat[:, 0], rt2, AX.X, ALU.add))
            link(dve.tensor_scalar(rstat[:, 0], rstat[:, 0], -1.0 / R1, None, ALU.mult))
            dve.tensor_tensor(rt0, rt2, over_units(rstat[:, 0]), ALU.add).then_inc(r_hc, 1)
            dve.wait_ge(r_sq, 1)
            dve.tensor_reduce(rstat[:, 1], rt1, AX.X, ALU.add).then_inc(r_vs, 1)
            dve.wait_ge(r_sd, 1)
            link(dve.reciprocal(rstat[:, 2], rstat[:, 1]))
            link(dve.tensor_tensor(rt0, rt0, over_units(rstat[:, 2]), ALU.mult))
            link(dve.tensor_tensor(rt0, rt0, over_tiles(lns_b), ALU.mult))
            dve.tensor_tensor(rt0, rt0, over_tiles(lnb_b), ALU.add).then_inc(r_ln, 1)
            id_real = ident[:, :].rearrange("p (b i) -> p b i", b=2)[:, :, 0:T]
            link(dve.tensor_reduce(real[:, :], id_real, AX.XY, ALU.add))
            dve.wait_ge(r_lg, 1)
            link(dve.tensor_tensor(lg[:, :, :], PS[:, 6, 0:P].rearrange("p (t e) -> p t e", e=E),
                                   br2_b[:, :].unsqueeze(1).broadcast_to([P, PAIRS, E]), ALU.add))
            for t in range(PAIRS):
                last = dve.max(top[:, t], lg[:, t])
            link(last)
            dve.tensor_tensor(pw[:, 0], top[:, :, 1], top[:, :, 0], ALU.subtract).then_inc(r_dif, 1)
            for t in range(PAIRS):
                last = dve.max_index(topi[:, t], top[:, t], lg[:, t])
            link(last)
            link(dve.tensor_copy(topf[:, :, :], topi[:, :, :]))
            for i in range(2):
                link(dve.tensor_tensor(oh[:, i], topf[:, :, i:i + 1].broadcast_to([P, PAIRS, E]),
                                       iota[:, 0:E].unsqueeze(1).broadcast_to([P, PAIRS, E]), ALU.is_equal))
            link(dve.tensor_scalar(oh[:, :, :, :], oh[:, :, :, :], real[:, :], None, ALU.mult))
            dve.tensor_tensor(chosen[:, :, :], oh[:, 0], oh[:, 1], ALU.add).then_inc(r_chosen, 1)
            dve.wait_ge(r_exp, 1)
            link(dve.tensor_scalar(pw[:, 3], pw[:, 1], 1.0, None, ALU.add))
            link(dve.reciprocal(pw[:, 2], pw[:, 3]))
            link(dve.tensor_tensor(pw[:, 3], pw[:, 1], pw[:, 2], ALU.mult))

            dve.wait_ge(r_rank, 1)
            link(dve.tensor_copy(scan_t[:, 0, 8:], PS[:, 0, P:2 * P].rearrange("p (t e) -> p t e", e=E)))
            for i, d in enumerate((1, 2, 4, 8)):
                old, new = scan_t[:, i % 2], scan_t[:, 1 - i % 2]
                link(dve.tensor_tensor(new[:, 8:], old[:, 8:], old[:, 8 - d:8 - d + PAIRS], ALU.add))
            counts = scan_t[:, 0, 8 + PAIRS - 1]
            link(dve.tensor_scalar(tmpk[:, 0:FULL], iota[:, 0:FULL], float(P), None, ALU.mult))
            link(dve.tensor_tensor(full, counts.unsqueeze(2).broadcast_to([P, E, FULL]),
                                   tmpk[:, 0:FULL].unsqueeze(1).broadcast_to([P, E, FULL]), ALU.is_gt))
            link(dve.tensor_reduce(scan_e[:, 0, 4:], full, AX.X, ALU.add))
            for i, d in enumerate((1, 2, 4)):
                old, new = scan_e[:, i % 2], scan_e[:, 1 - i % 2]
                link(dve.tensor_tensor(new[:, 4:], old[:, 4:], old[:, 4 - d:4 - d + E], ALU.add))
            last_tile, first_tile = scan_e[:, 1, 4:], scan_e[:, 1, 3:3 + E]
            link(dve.tensor_tensor(late_tile, iota[:, 0:KT].unsqueeze(2).broadcast_to([P, KT, E]),
                                   last_tile.unsqueeze(1).broadcast_to([P, KT, E]), ALU.is_ge))
            link(dve.tensor_reduce(ekf[:, :], late_tile, AX.X, ALU.add))
            link(dve.tensor_scalar(ekf[:, :], ekf[:, :], float(E - 1), None, ALU.min))
            dve.tensor_copy(eki[:, :], ekf[:, :]).then_inc(r_experts, 1)
            link(dve.tensor_scalar(scan_e[:, 0, 4:], first_tile, float(P), None, ALU.mult))
            link(dve.tensor_tensor(slot[:, :, :], PS[:, 0, 0:P].rearrange("p (t e) -> p t e", e=E),
                                   scan_t[:, 0, 7:7 + PAIRS], ALU.add))
            link(dve.tensor_tensor(slot[:, :, :], slot[:, :, :], scan_e[:, 0, 4:].unsqueeze(1).broadcast_to([P, PAIRS, E]),
                                   ALU.add))
            link(dve.tensor_tensor(sel[:, :, :, :], oh[:, :, :, :], slot[:, :, :].unsqueeze(1).broadcast_to([P, 2, PAIRS, E]),
                                   ALU.mult))
            link(dve.tensor_reduce(slf[:, :], sel[:, :, :, :].rearrange("p a t e -> p (a t) e"), AX.X, ALU.add))
            link(dve.tensor_copy(slu[:, 0], slf[:, :]))
            link(dve.tensor_scalar(slu[:, 1], slu[:, 0], P - 1, None, ALU.bitwise_and))
            link(dve.tensor_scalar(slu[:, 2], slu[:, 0], 7, None, ALU.logical_shift_right))
            link(dve.tensor_copy(slh[:, :, :], slu[:, 1:3]))
            N2 = 2 * PAIRS
            link(dve.tensor_tensor(what[:, :, 0], slh[:, 1].unsqueeze(2).broadcast_to([P, N2, KT]),
                                   iota[:, 0:KT].unsqueeze(1).broadcast_to([P, N2, KT]), ALU.is_equal))
            link(dve.tensor_scalar(what[:, :, 0], what[:, :, 0], real[:, :], None, ALU.mult))
            for i in range(2):
                part = what[:, i * PAIRS:(i + 1) * PAIRS]
                for c, v in ((1, token_id[:, :]), (2, pw[:, 2 + i])):
                    link(dve.tensor_tensor(part[:, :, c], part[:, :, 0], v.unsqueeze(2).broadcast_to([P, PAIRS, KT]), ALU.mult))
            dve.tensor_tensor(which, slh[:, 0].unsqueeze(2).broadcast_to([P, N2, P]),
                              iota[:, :].unsqueeze(1).broadcast_to([P, N2, P]), ALU.is_equal).then_inc(r_what, 1)
            dve.wait_ge(r_table, 1)
            table = PS[:, 7, 0:3 * KT].rearrange("p (c k) -> p c k", c=3)
            link(dve.tensor_scalar(tmpk[:, :], table[:, 0], float(-2 * NT), float(2 * NT), ALU.mult, ALU.add))
            link(dve.tensor_tensor(tmpk[:, :], table[:, 1], tmpk[:, :], ALU.add))
            link(dve.tensor_copy(sidx[:, :], tmpk[:, :]))
            link(dve.tensor_copy(wk[:, :], table[:, 2]))
            dve.tensor_copy(gidx[:, :], table[:, 1]).then_inc(r_index, 1)

            def hidden(k, u, e):
                for half, ready, done, h, free in ((1, f_H2, f_h2, h2, f_g), (0, f_H1, f_h1, h1, f_g)):
                    dve.wait_ge(ready, k + 1)
                    if not before(k, 2):
                        dve.wait_ge(free, k - 1)
                    dve.tensor_tensor(h[:, u], PS[:, 1 + 2 * u + half, :],
                                      b1b.rearrange("p e (h f) -> p e h f", h=2)[:, e, half, :], ALU.add).then_inc(done, 1)

            def result(k, u, e):
                dve.wait_ge(f_Y, k + 1)
                if not before(k, 2):
                    dve.wait_ge(f_ys, k - 1)
                dve.tensor_tensor(yb[:, u], PS[:, 6 + u, 0:P], b2b[:, e, :], ALU.add).then_inc(f_yb, 1)
                dve.wait_ge(f_yb, k + 1)
                if not before(k, 2):
                    dve.wait_ge(added[u], 8 * (k - u))
                dve.tensor_scalar(ys[:, u], yb[:, u], wk[:, bass.ds(k, 1)], None, ALU.mult).then_inc(f_ys, 1)

            def expert_of(k):
                return dve.value_load(eki[0:1, bass.ds(k, 1)], min_val=0, max_val=E - 1)

            def expert_tile(k, u):
                hidden(k, u, expert_of(k))
                if not before(k, 2):
                    result(k - 2, u, expert_of(k - 2))
                dve.wait_ge(f_ge, k + 1)
                dve.wait_ge(f_h1, k + 1)
                if not before(k, 2):
                    dve.wait_ge(f_G, k - 1)
                dve.tensor_tensor(gg[:, u], h1[:, u], h2[:, u], ALU.mult).then_inc(f_g, 1)

            dve.wait_ge(r_experts, 1)
            dve.wait_ge(w2_loaded, 32 * E)
            tiles(dve, KT, 2, expert_tile)
            for k in range(KT - 2, KT):
                result(k, k % 2, expert_of(k))

            dve.wait_ge(o_in, 32)
            dve.tensor_tensor(x2[:, :, :], wide[:, 0], wide[:, 1], ALU.add).then_inc(o_sum, 1)
            dve.wait_ge(o_sum, 1)
            with dve.Fori(0, PAIRS, 1) as t:
                dve.bn_stats(st[:, t], x2[:, t]).then_inc(o_st, 1)
            norm_factors(3, o_st, PAIRS)
            for i, (src, v, op) in enumerate(((x2[:, :, :], mv[:, :, 0:1], ALU.subtract),
                                              (wide[:, 0], rstd[:, :].unsqueeze(2), ALU.mult))):
                dve.tensor_tensor(wide[:, 0], src, v.broadcast_to([P, PAIRS, P]), op).then_inc(o_y, 1)
                dve.wait_ge(o_y, i + 1)


def kernel(**inputs):
    import numpy as np
    import concourse.bacc as bacc
    from concourse.bass_utils import run_bass_kernel_spmd

    given = {n: np.ascontiguousarray(v) for n, v in inputs.items()}
    B, T, D = given["x"].shape
    given["xT"] = given["x"].reshape(B // 2, 2, T, D).transpose(3, 0, 1, 2)
    given["wqT"] = given["L0_attn_Wq"].T
    given["wkT"] = given["L0_attn_Wk"].T
    given["wvT"] = given["L0_attn_Wv"].T
    given["woT"] = given["L0_attn_Wo"].T
    given["projT"] = given["L0_attn_proj"].transpose(0, 2, 1).reshape(D, -1)
    given["wsimT"] = given["L0_xattn_w_sim"].reshape(3, D).T
    for n in ("L0_attn_Wv", "L0_attn_Wo", "L0_attn_proj"):
        del given[n]
    nc = bacc.Bacc("TRN2", target_bir_lowering=False, num_devices=1)
    arrays, aps = {}, {}
    for n, v in given.items():
        v = np.ascontiguousarray(v)
        arrays["in_" + n] = v
        aps[n] = nc.dram_tensor("in_" + n, v.shape, mybir.dt.from_np(v.dtype), kind="ExternalInput").ap()
    out = nc.dram_tensor("out_0", (B, T, D), mybir.dt.float32, kind="ExternalOutput").ap()
    build(nc, aps, out)
    return run_bass_kernel_spmd(nc, [arrays], core_ids=[0]).results[0]["out_0"]
```

```python
from contextlib import ExitStack

import concourse.bass as bass
from concourse import mybir

F32 = mybir.dt.float32
BF16 = mybir.dt.bfloat16
I32 = mybir.dt.int32
U32 = mybir.dt.uint32
ALU = mybir.AluOpType
ACT = mybir.ActivationFunctionType
AX = mybir.AxisListType

P = 128
HALF = 64


def tiles(eng, count, ring, body, head=4):
    turns = (count - head - ring) // ring
    for t in range(head):
        body(t, t % ring)
    if turns > 0:
        with eng.Fori(head, head + ring * (turns - 1) + 1, ring) as t0:
            for k in range(ring):
                body(t0 + k, (head + k) % ring)
    for t in range(head + ring * max(turns, 0), count):
        body(t, t % ring)


def before(t, n):
    return isinstance(t, int) and t < n


def after(t, n, count):
    return isinstance(t, int) and t + n >= count


def build(nc, a, out):
    B, T, D = a["x"].shape
    J = a["ctx_1024"].shape[1]
    H, DK, M = 16, 8, 32
    HM = H * M
    PAIRS = B // 2
    CH = 12
    JP = J // CH
    CG = 4
    NG = CH // CG
    W = CG * JP
    QT = 4
    QW = QT * P
    CR = 4
    E = a["L0_ffn_W1"].shape[0]
    R1 = D // 2
    F = a["L0_ffn_W2"].shape[1]
    FT = F // P
    NT = PAIRS * P
    FULL = B * T // P
    NC = 2 * PAIRS // 4
    KT = 2 * B * T // P + E - 1
    assert (D, T, J, JP * CH) == (P, 56, 1500, J) and JP <= P and B * T % P == 0

    accd = [nc.dram_tensor(f"accumulated{i}", (NT, D), F32, kind="Internal").ap() for i in range(2)]
    x2d = nc.dram_tensor("x2_rows", (NT, D + E), F32, kind="Internal").ap()

    with ExitStack() as ctx:
        def sb(name, shape, dt=F32):
            return ctx.enter_context(nc.sbuf_tensor(name, shape, dt))

        def sem(name):
            return ctx.enter_context(nc.semaphore(name))

        PS = ctx.enter_context(nc.psum_tensor("PS", [P, 8, 512], F32))

        ident = sb("ident", [P, P])
        ones_bf = sb("ones_bf", [P, P], BF16)
        below = sb("below", [P, P], BF16)
        headmask = sb("headmask", [P, H])
        kvmask = sb("kvmask", [P, 4, 2, 4, DK + 1])
        iota = sb("iota", [P, P])
        iota1 = sb("iota1", [P, KT])
        one = sb("one", [P, 1])
        line1 = sb("line1", [P, 1])
        real = sb("real", [P, 1])
        eps5 = sb("eps5", [P, 1])
        eps6 = sb("eps6", [P, 1])
        zero = sb("zero", [P, P])
        wqkvT = sb("wqkvT", [P, 3, P])
        wqk = sb("wqk", [P, 2, P])
        woT = sb("woT", [P, P])
        projT = sb("projT", [P, M])
        pblk = sb("pblk", [P, H, M])
        wfeat = sb("wfeat", [P, 2, HM])
        bo_b = sb("bo_b", [P, D])
        wsim = sb("wsim", [P, 3])
        w1_b = sb("w1_b", [P, D])
        bsim = sb("bsim", [PAIRS, 1])
        wqv = sb("wqv", [P, 4, P])
        bqv = sb("bqv", [P, 1])
        wr1 = sb("wr1", [P, R1])
        wr2 = sb("wr2", [P, 2, E])
        br1_b = sb("br1_b", [P, R1])
        lns_b = sb("lns_b", [P, R1])
        lnb_b = sb("lnb_b", [P, R1])
        br2_b = sb("br2_b", [P, E])
        b2b = sb("b2b", [P, E, D])
        w1s = sb("w1s", [P, E, 2 * F])
        b1c = sb("b1c", [P, E * 2 * FT])

        xT = sb("xT", [P, 2, P])
        xn_in = sb("xn_in", [P, 2, P])
        sq = sb("sq", [P, 2, 2 * P])
        mx = sb("mx", [P, 2, 2 * H])
        nr = sb("nr", [P, 2, 2 * H])
        cc = sb("cc", [P, 2, 2 * H])
        phi = sb("phi", [P, 2, 2 * HM])
        vv = sb("vv", [P, 2, 4, 2, 4, DK + 1])
        phT = sb("phT", [P, 2, HM])
        kvs = sb("kvs", [P, 2, 4, 2, 36])
        den = sb("den", [P, 2, H])
        rden = sb("rden", [P, 2, H])
        mg = sb("mg", [P, 2, P])
        mgT = sb("mgT", [P, 2, P])
        xb = sb("xb", [P, 4, P])
        wide = sb("wide", [P, 2, PAIRS, P])
        res, hqT = wide[:, 0], wide[:, 1]
        st = sb("st", [P, PAIRS, 6])
        mv = sb("mv", [P, PAIRS, 2])
        rstd = sb("rstd", [P, PAIRS])
        shift = sb("shift", [P, PAIRS])
        xn = sb("xn", [P, 2, P])
        rows = phi[:, :, :].rearrange("p k f -> p (k f)").rearrange("p (t i) -> p t i", i=P)
        term_products = sb("term_products", [P, P])

        arena = sb("arena", [P, CR * 2 * CH * P])
        cx = arena[:, :].rearrange("p (r b c d) -> p r b c d", r=CR, b=2, c=CH)
        turned = sb("turned", [P, 2 * 2 * J])
        cxT = turned[:, :].rearrange("p (u b j) -> p u b j", u=2, b=2)
        mid = sb("mid", [P, J + NG * 4 * P])
        ex = mid[:, 0:J]
        etT = mid[:, J:].rearrange("p (g c i) -> p g c i", g=NG, c=CG)
        xnT = sb("xnT", [P, PAIRS, P])
        xw = sb("xw", [P, 2, P])
        rs = sb("rs", [P, 2, 1])
        m3 = sb("m3", [P, NG])
        nm = sb("nm", [P, 2, 1])
        s3 = sb("s3", [P, 2, NG])
        s1 = sb("s1", [P, 1])
        rz = sb("rz", [P, 2, 1])
        hq = sb("hq", [P, P])
        rm_all = sb("rm_all", [P, PAIRS])
        rT = sb("rT", [PAIRS, 2, HALF])
        ba = sb("ba", [PAIRS, 2, HALF])
        bmx = sb("bmx", [PAIRS, 2, 1])
        hcb = sb("hcb", [P, B])
        halves = sb("halves", [P, 2])
        wcol = sb("wcol", [P, PAIRS, 2])
        x3 = res
        x4 = turned[:, 3 * PAIRS * R1:3 * PAIRS * R1 + NT].rearrange("p (t i) -> p t i", t=PAIRS)
        zT = mid[:, J:J + 2 * QW].rearrange("p (k i) -> p k i", k=2)

        x2 = xnT
        x2s = mid[:, 0:2 * QW].rearrange("p (k i) -> p k i", k=2)
        rt0, rt1, rt2 = (turned[:, i * PAIRS * R1:(i + 1) * PAIRS * R1].rearrange("p (t n) -> p t n", t=PAIRS)
                         for i in range(3))
        rstat = sb("rstat", [P, 3, PAIRS])
        hrT = mid[:, J:J + PAIRS // 2 * P].rearrange("p (q n) -> p q n", q=PAIRS // 2)
        lg = sb("lg", [P, PAIRS, E])
        top = sb("top", [P, PAIRS, 8])
        topi = sb("topi", [P, PAIRS, 8], U32)
        pad = sb("pad", [P, 1])
        pw = sb("pw", [P, 4, PAIRS])
        oh = sb("oh", [P, 2, PAIRS, E])
        scan = sb("scan", [P, 2, 8 + PAIRS, E], BF16)
        in_row = sb("in_row", [P, E], BF16)
        several = sb("several", [P, FULL])
        earlier = sb("earlier", [P, E, E])
        tiles_e = sb("tiles_e", [P, E])
        base = sb("base", [P, 2, E])
        parts_e = sb("parts_e", [P, E, E])
        last_tile = sb("last_tile", [P, E])
        full = mid[:, KT * E:KT * E + E * FULL].rearrange("p (e n) -> p e n", e=E)
        slot = sb("slot", [P, PAIRS, E])
        sel = sb("sel", [P, 2, PAIRS, E])
        slu = sb("slu", [P, 3, 2 * PAIRS], U32)
        late_tile = mid[:, 0:KT * E].rearrange("p (k e) -> p k e", k=KT)
        ekf = sb("ekf", [P, KT])
        eki = sb("eki", [P, KT], I32)
        which = wide[:, 0].rearrange("p t i -> p (t i)").bitcast(BF16).rearrange("p (n i) -> p n i", i=P)
        what = turned[:, 0:2 * PAIRS * KT].bitcast(BF16).rearrange("p (n c k) -> p n c k", n=2 * PAIRS, c=2)
        hits = mid[:, KT * E + E * FULL:KT * (E + 2 * PAIRS) + E * FULL].rearrange("p (n k) -> p n k", k=KT)
        hi1 = sb("hi1", [P, 2 * PAIRS])
        minus_lo = sb("minus_lo", [P, NC])
        apart = mid[:, J + 512:J + 512 + NC * P].rearrange("p (n i) -> p n i", i=P)
        gates = sb("gates", [P, 2, PAIRS, E])

        w2s = arena[:, 0:E * FT * D].rearrange("p (e f d) -> p e f d", e=E, f=FT)
        w1t = arena[:, E * FT * D:E * FT * D + 4 * F].rearrange("p (u f) -> p u f", u=2)
        gidx = sb("gidx", [P, KT], U32)
        sidx = sb("sidx", [P, KT], U32)
        beyond = sb("beyond", [P, KT])
        slot_token = sb("slot_token", [P, KT])
        gs = sb("gs", [P, 2, 1], U32)
        ss = sb("ss", [P, 2, 1], U32)
        spare = sb("spare", [P, 1])
        xg = sb("xg", [P, 2, D + E])
        gk = sb("gk", [P, KT * E])
        xgT = sb("xgT", [P, 2, P])
        g2, gg = (turned[:, i * 2 * F:(i + 1) * 2 * F].rearrange("p (u f) -> p u f", u=2) for i in range(2))
        yb = sb("yb", [P, 2, P])
        ys = sb("ys", [P, 2, P])

        proj_loaded = sem("proj_loaded")
        headmask_made = sem("headmask_made")
        qk_weights_loaded = sem("qk_weights_loaded")
        consts_loaded = sem("consts_loaded")
        late_loaded = sem("late_loaded")
        pool_consts = sem("pool_consts")
        dve_consts = sem("dve_consts")
        xT_loaded = [sem(f"xT_loaded{i}") for i in range(2)]
        x_loaded = [sem(f"x_loaded{i}") for i in range(2)]
        ctx_loaded = [sem(f"ctx_loaded{i}") for i in range(CR)]
        a_projected = sem("a_projected")
        a_query_feat = sem("a_query_feat")
        a_key_feat = sem("a_key_feat")
        a_squared = sem("a_squared")
        a_v_kept = sem("a_v_kept")
        a_norms = sem("a_norms")
        a_max = sem("a_max")
        a_offset = sem("a_offset")
        a_shifted = sem("a_shifted")
        a_exp = sem("a_exp")
        a_key_eps = sem("a_key_eps")
        a_phi_turned = sem("a_phi_turned")
        a_phi_copied = sem("a_phi_copied")
        a_kv = sem("a_kv")
        a_kv_kept = sem("a_kv_kept")
        a_num = sem("a_num")
        a_den = sem("a_den")
        a_rden = sem("a_rden")
        a_merged = sem("a_merged")
        a_merged_turned = sem("a_merged_turned")
        a_merged_copied = sem("a_merged_copied")
        a_out = sem("a_out")
        a_xb = sem("a_xb")
        a_res = sem("a_res")
        a_stats = sem("a_stats")
        b_ctx_turned = sem("b_ctx_turned")
        b_ctx_even = sem("b_ctx_even")
        b_ctx_odd = sem("b_ctx_odd")
        b_xn = sem("b_xn")
        b_rows_kept = sem("b_rows_kept")
        b_x_turned = sem("b_x_turned")
        b_xnT = sem("b_xnT")
        b_xw = sem("b_xw")
        b_row_term = sem("b_row_term")
        b_sim = sem("b_sim")
        b_group_max = sem("b_group_max")
        b_neg_max = sem("b_neg_max")
        b_row_max = sem("b_row_max")
        b_exp = sem("b_exp")
        b_exp_turned = sem("b_exp_turned")
        b_exp_evenD = sem("b_exp_evenD")
        b_exp_oddA = sem("b_exp_oddA")
        b_sum = sem("b_sum")
        b_inv_sum = sem("b_inv_sum")
        b_values = sem("b_values")
        b_hq = sem("b_hq")
        b_hq_turned = sem("b_hq_turned")
        b_hqT = sem("b_hqT")
        h_turned = sem("h_turned")
        h_copied = sem("h_copied")
        h_shifted = sem("h_shifted")
        h_exp = sem("h_exp")
        h_weights = sem("h_weights")
        h_weights_turned = sem("h_weights_turned")
        h_weight_cols = sem("h_weight_cols")
        h_heads = sem("h_heads")
        h_heads_kept = sem("h_heads_kept")
        h_x3 = sem("h_x3")
        h_x4 = sem("h_x4")
        c_query = sem("c_query")
        c_z = sem("c_z")
        c_z_turned = sem("c_z_turned")
        d_rows_normed = sem("d_rows_normed")
        d_rows_turned = sem("d_rows_turned")
        d_rows_copied = sem("d_rows_copied")
        d_hidden = sem("d_hidden")
        d_rows_stored = sem("d_rows_stored")
        d_zeroed = sem("d_zeroed")
        d_gates_stored = sem("d_gates_stored")
        r_centred = sem("r_centred")
        r_squared = sem("r_squared")
        r_var_sum = sem("r_var_sum")
        r_deviation = sem("r_deviation")
        r_normed = sem("r_normed")
        r_scaled = sem("r_scaled")
        r_biased = sem("r_biased")
        r_biased_last = sem("r_biased_last")
        r_gelu = sem("r_gelu")
        r_hidden_turned = sem("r_hidden_turned")
        r_hidden_copied = sem("r_hidden_copied")
        r_logits = sem("r_logits")
        r_difference = sem("r_difference")
        r_exp = sem("r_exp")
        r_chosen = sem("r_chosen")
        r_first_weight = sem("r_first_weight")
        r_gate = sem("r_gate")
        r_gates = sem("r_gates")
        r_rank = sem("r_rank")
        r_hits = sem("r_hits")
        r_minus_place = sem("r_minus_place")
        r_apart = sem("r_apart")
        r_which_last = sem("r_which_last")
        r_which = sem("r_which")
        r_what = sem("r_what")
        r_table = sem("r_table")
        r_index = sem("r_index")
        r_experts = sem("r_experts")
        f_gather_index = sem("f_gather_index")
        f_add_index = sem("f_add_index")
        f_rows_turned = sem("f_rows_turned")
        f_rows_copied = sem("f_rows_copied")
        f_gates_kept = sem("f_gates_kept")
        f_gate_weights = sem("f_gate_weights")
        f_lin_weights = sem("f_lin_weights")
        f_gate_units = sem("f_gate_units")
        f_lin_units = sem("f_lin_units")
        f_gelu = sem("f_gelu")
        f_gated = sem("f_gated")
        f_result = sem("f_result")
        f_biased = sem("f_biased")
        f_scaled = sem("f_scaled")
        o_sum = sem("o_sum")
        o_rows_act = sem("o_rows_act")
        o_rows_dve = sem("o_rows_dve")
        o_stored = sem("o_stored")
        ln_moments = sem("ln_moments")
        ln_deviation = sem("ln_deviation")
        ln_shift = sem("ln_shift")
        composite = sem("composite")
        composite_kept = sem("composite_kept")
        w1_loaded, w2_loaded = sem("w1_loaded"), sem("w2_loaded")
        gathered = [sem(f"gathered{i}") for i in range(2)]
        added = [sem(f"added{i}") for i in range(2)]
        sums_loaded = [sem(f"sums_loaded{q}") for q in range(PAIRS // QT)]
        chain = sem("chain")

        def over_tiles(v):
            return v[:, :].unsqueeze(1).broadcast_to([P, QT, R1])

        def rows_here(q):
            return 1 if q < PAIRS // QT - 2 else 2

        block = ctx.enter_context(nc.Block())

        psF = PS[:, 0:2, :].rearrange("p a b -> p (a b)")
        feat = psF.rearrange("p (h m) -> p h m", m=M)
        psQ = PS[:, 2, :]
        psT = PS[:, 3, :]
        psKV = PS[:, 4, 0:2 * H * (DK + 1)].rearrange("p (g b c) -> p g b c", g=4, b=2)
        psN = PS[:, 6, :]
        psW = PS[:, 7, :]
        num = psN[:, 0:H * (DK + 1)].rearrange("p (h c) -> p h c", h=H)
        psC = PS[:, 0:2, 0:W]
        psS = PS[:, 2:5, 0:W]
        psE = PS[:, 5:7, :]
        psO = PS[:, 7, 0:P]
        psX = PS[:, 0:6:5, 0:P]

        def experts(eng, first, count=1):
            return nc.values_load_multi_w_load_instructions(
                eki[0:1, bass.ds(first, count)], engines=[eng.engine], min_val=0, max_val=E - 1,
                skip_runtime_bounds_check_because="they are counted from 0 up and cut off at E - 1 when computed")[1]

        CONSTS = [
            (wqkvT[:, 0, :], a["wqT"]), (wqkvT[:, 1, :], a["wkT"]), (wqkvT[:, 2, :], a["wvT"]),
            (woT[:, :], a["woT"]), (bo_b[:, :], a["L0_attn_bo"].partition_broadcast(P)),
        ]
        LATE = [
            (wsim[:, :], a["wsimT"]), (w1_b[:, :], a["L0_xattn_w_sim"][0:D].partition_broadcast(P)),
            (bsim[:, :], a["L0_xattn_b_sim"].partition_broadcast(PAIRS)),
            (wqv[:, :, :], a["L0_xattn_W_qv"].rearrange("(k p) n -> p k n", p=P)),
            (bqv[:, :], a["L0_xattn_b_qv"].rearrange("(p a) -> p a", a=1)),
            (wr1[:, :], a["L0_ffn_Wr1"]),
            (wr2[0:R1, 0, :], a["L0_ffn_Wr2"]), (wr2[R1:P, 1, :], a["L0_ffn_Wr2"]),
            (br1_b[:, :], a["L0_ffn_br1"].partition_broadcast(P)),
            (lns_b[:, :], a["L0_ffn_ln_scale"].partition_broadcast(P)),
            (lnb_b[:, :], a["L0_ffn_ln_bias"].partition_broadcast(P)),
            (br2_b[:, :], a["L0_ffn_br2"].partition_broadcast(P)),
            (b2b[:, :, :], a["L0_ffn_b2"].partition_broadcast(P)), (b1c[:, :], a["b1T"]),
        ]
        ATTENTION_CONSTS = 9
        POOL_CONSTS = 20

        @block.sync
        def _(sp):
            sp.dma_start(projT[:, :], a["projT"]).then_inc(proj_loaded, 16)
            for i, n in enumerate(("Wq", "Wk")):
                sp.dma_start(wqk[:, i, :], a["L0_attn_" + n]).then_inc(qk_weights_loaded, 16)
            for dst, src in CONSTS:
                sp.dma_start(dst, src).then_inc(consts_loaded, 16)

            def load_x(t, k):
                if not before(t, 2):
                    sp.wait_ge(a_key_feat, t - 1)
                    sp.wait_ge(a_xb, t - 1)
                sp.dma_start(xT[:, k, :].rearrange("p (b i) -> p b i", b=2)[:, :, 0:T],
                             a["xT"][:, t, :, :]).then_inc(xT_loaded[k], 16)
                for b in range(2):
                    sp.dma_start(xn_in[b * HALF:b * HALF + T, k, :], a["x"][2 * t + b]).then_inc(x_loaded[k], 16)

            def load_ctx(p, k):
                if not before(p, CR):
                    sp.wait_ge(b_values, p - CR + 1)
                cut = JP // 16 * 16
                for b in range(2):
                    src = a["ctx_1024"][2 * p + b].rearrange("(p c) d -> p c d", c=CH)
                    sp.dma_start(cx[0:cut, k, b], src[0:cut]).then_inc(ctx_loaded[k], 16)
                    sp.dma_start(cx[cut:JP, k, b], src[cut:JP]).then_inc(ctx_loaded[k], 16)

            sp.wait_ge(pool_consts, 2)
            for p in range(CR):
                load_x(2 * p, 0)
                load_x(2 * p + 1, 1)
                load_ctx(p, p)
            sp.wait_ge(pool_consts, POOL_CONSTS)
            for dst, src in LATE:
                sp.dma_start(dst, src).then_inc(late_loaded, 16)
            with sp.Fori(2 * CR, PAIRS - 1, 2) as t0:
                for k in range(2):
                    load_x(t0 + k, k)
            for e in range(E):
                sp.dma_start(w1s[:, e, :], a["L0_ffn_W1"][e]).then_inc(w1_loaded, 16)
            sp.dma_start(accd[1].rearrange("(p t) d -> p t d", t=PAIRS),
                         zero[:, :].unsqueeze(1).broadcast_to([P, PAIRS, D])).then_inc(d_zeroed, 16)
            with sp.Fori(CR, PAIRS - CR + 1, CR) as p0:
                for k in range(CR):
                    load_ctx(p0 + k, k)
            sp.wait_ge(b_values, PAIRS)
            for e in range(E):
                sp.dma_start(w2s[:, e], a["L0_ffn_W2"][e].rearrange("(f p) n -> p f n", p=P)).then_inc(w2_loaded, 16)
            sp.wait_ge(d_rows_normed, PAIRS // QT)
            for dst in (x2d[:, 0:D], accd[0]):
                sp.dma_start(dst.rearrange("(p t) d -> p t d", t=PAIRS), x2[:, :, :]).then_inc(d_rows_stored, 16)
            sp.wait_ge(r_gates, 1)
            sp.dma_start(x2d[:, D:].rearrange("(p t) e -> p t e", t=PAIRS), gates[:, 0]).then_inc(d_gates_stored, 16)

            def load_sum(i, q):
                part = slice(q * QT, (q + 1) * QT)
                sp.dma_start(wide[:, i, part],
                             accd[i].rearrange("(p t) d -> p t d", t=PAIRS)[:, part]).then_inc(sums_loaded[q], 16)

            first, then = KT % 2, 1 - KT % 2
            sp.wait_ge(added[first], 16 * ((KT + 1 - first) // 2))
            for q in range(2):
                load_sum(first, q)
            sp.wait_ge(added[then], 16 * ((KT + 1 - then) // 2))
            for q in range(2):
                load_sum(then, q)
            for q in range(2, PAIRS // QT):
                for i in range(2):
                    load_sum(i, q)
            for q in range(PAIRS // QT):
                part = slice(q * QT, (q + 1) * QT)
                sp.wait_ge(o_rows_act, q + 1)
                sp.wait_ge(o_rows_dve, q + 1)
                for b in range(2):
                    sp.dma_start(out.rearrange("(t b) i d -> b i t d", b=2)[b][:, part],
                                 wide[b * HALF:b * HALF + T, 0, part]).then_inc(o_stored, 16)
            sp.wait_ge(o_stored, 32 * (PAIRS // QT))

        @block.gpsimd
        def _(pool):
            pool.memset(headmask[:, :], 1.0).then_inc(headmask_made, 1)
            pool.memset(xT[:, :, :], 0.0).then_inc(pool_consts, 1)
            pool.memset(xn_in[:, :, :], 0.0).then_inc(pool_consts, 1)
            pool.wait_ge(headmask_made, 1)
            pool.affine_select(out=headmask[:, :], in_=headmask[:, :], compare_op=ALU.is_ge, fill=0.0, base=0,
                               pattern=[[-DK, H]], channel_multiplier=1).then_inc(headmask_made, 1)
            pool.wait_ge(headmask_made, 2)
            pool.affine_select(out=headmask[:, :], in_=headmask[:, :], compare_op=ALU.is_ge, fill=0.0, base=DK - 1,
                               pattern=[[DK, H]], channel_multiplier=-1).then_inc(headmask_made, 1)
            pool.memset(ident[:, :], 0.0).then_inc(pool_consts, 1)
            kvmask_heads = kvmask[:, :, :, :, :].rearrange("p a b h c -> p (a b) h c")
            pool.memset(kvmask_heads, 1.0).then_inc(pool_consts, 1)
            pool.memset(vv[:, :, :, :, :, :], 0.0).then_inc(pool_consts, 1)
            pool.memset(eps6[:, :], 1e-6).then_inc(pool_consts, 1)
            pool.wait_ge(pool_consts, 6)
            pool.affine_select(out=ident[:, :], in_=ident[:, :], compare_op=ALU.not_equal, fill=1.0, base=0,
                               pattern=[[-1, P]], channel_multiplier=1).then_inc(pool_consts, 1)
            pool.affine_select(out=kvmask_heads, in_=kvmask_heads, compare_op=ALU.is_ge, fill=0.0, base=0,
                               pattern=[[0, 8], [-M, 4], [0, DK + 1]], channel_multiplier=1).then_inc(pool_consts, 1)
            pool.wait_ge(pool_consts, 8)
            pool.affine_select(out=kvmask_heads, in_=kvmask_heads, compare_op=ALU.is_ge, fill=0.0,
                               base=M - 1, pattern=[[0, 8], [M, 4], [0, DK + 1]],
                               channel_multiplier=-1).then_inc(pool_consts, 1)
            pool.memset(wr2[:, :, :], 0.0).then_inc(pool_consts, 1)
            pool.memset(eps5[:, :], 1e-5).then_inc(pool_consts, 1)
            pool.memset(one[:, :], 1.0).then_inc(pool_consts, 1)
            pool.memset(ba[:, :, :], 0.0).then_inc(pool_consts, 1)
            pool.memset(ones_bf[:, :], 1.0).then_inc(pool_consts, 1)
            pool.memset(below[:, :], 1.0).then_inc(pool_consts, 1)
            pool.memset(zero[:, :], 0.0).then_inc(pool_consts, 1)
            pool.iota(iota[:, :], [[1, P]], base=0, channel_multiplier=0,
                      allow_small_or_imprecise_dtypes=True).then_inc(pool_consts, 1)
            pool.iota(iota1[:, :], [[1, KT]], base=1, channel_multiplier=0,
                      allow_small_or_imprecise_dtypes=True).then_inc(pool_consts, 1)
            pool.iota(line1[:, :], [[0, 1]], base=1, channel_multiplier=1,
                      allow_small_or_imprecise_dtypes=True).then_inc(pool_consts, 1)
            pool.wait_ge(pool_consts, 19)
            pool.affine_select(out=below[:, :], in_=below[:, :], compare_op=ALU.is_ge, fill=0.0, base=-1,
                               pattern=[[1, P]], channel_multiplier=-1).then_inc(pool_consts, 1)
            pool.wait_ge(consts_loaded, 16 * len(CONSTS))

            def attention(t, k):
                x = k % 2
                pool.wait_ge(x_loaded[x], 16 * (t - x) + 32)
                if not before(t, 4):
                    pool.wait_ge(a_res, t - 3)
                pool.tensor_tensor(xb[:, k], xn_in[:, x], bo_b[:, :], ALU.add).then_inc(a_xb, 1)
                if not before(t, 1):
                    key_epsilon(t - 1, 1 - x)

            def key_epsilon(t, x):
                pool.wait_ge(a_exp, t + 1)
                pool.tensor_tensor(phi[:, x, HM:2 * HM], phi[:, x, HM:2 * HM], eps6[:, :].broadcast_to([P, HM]),
                                   ALU.add).then_inc(a_key_eps, 1)

            tiles(pool, PAIRS, 4, attention)
            key_epsilon(PAIRS - 1, 1)

            def products(p):
                pool.wait_ge(b_hqT, p + 1)
                pool.tensor_tensor(x3[:, p], xnT[:, p], hqT[:, p], ALU.mult).then_inc(h_x3, 1)

            def cross(p, k):
                pool.wait_ge(b_xn, p + 1)
                pool.tensor_copy(rows[:, p], xn[:, k % 2]).then_inc(b_rows_kept, 1)
                pool.wait_ge(b_neg_max, p + 1)
                pool.wait_ge(b_row_term, p + 1)
                pool.tensor_tensor(rm_all[:, bass.ds(p, 1)], rs[:, k % 2], nm[:, k % 2], ALU.subtract).then_inc(b_row_max, 1)
                if not before(p, 1):
                    products(p - 1)

            pool.wait_ge(a_kv, PAIRS)
            tiles(pool, PAIRS, CR, cross)
            products(PAIRS - 1)

            for q in range(PAIRS // QT):
                pool.wait_ge(h_heads_kept, q + 1)
                part = slice(q * QT, (q + 1) * QT)
                pool.tensor_tensor(x4[:, part].rearrange("p t (u i) -> p (t u) i", u=2),
                                   xnT[:, part].rearrange("p t (u i) -> p (t u) i", u=2),
                                   hcb[:, 2 * q * QT:2 * (q + 1) * QT].unsqueeze(2).broadcast_to([P, 2 * QT, HALF]),
                                   ALU.mult).then_inc(h_x4, 1)
            for q in range(PAIRS // QT - 1):
                part = rt0[:, q * QT:(q + 1) * QT]
                pool.wait_ge(r_normed, q + 1)
                pool.tensor_tensor(part, part, over_tiles(lns_b), ALU.mult).then_inc(r_scaled, 1)
                pool.wait_ge(r_scaled, q + 1)
                pool.tensor_tensor(part, part, over_tiles(lnb_b), ALU.add).then_inc(r_biased, 1)

            pool.wait_ge(r_first_weight, 1)
            pool.tensor_tensor(pw[:, 3], pw[:, 1], pw[:, 2], ALU.mult).then_inc(r_gate, 1)
            pool.wait_ge(r_gate, 1)
            for i in range(2):
                pool.tensor_tensor(gates[:, i], oh[:, i], pw[:, 2 + i].unsqueeze(2).broadcast_to([P, PAIRS, E]),
                                   ALU.mult).then_inc(r_gate, 1)
            pool.wait_ge(r_gate, 3)
            pool.tensor_tensor(gates[:, 0], gates[:, 0], gates[:, 1], ALU.add).then_inc(r_gates, 1)

            for c in range(4):
                part, n = slice(c * NC, (c + 1) * NC), c % 2 * NC
                pool.wait_ge(r_hits, c + 1)
                for w, v in enumerate((line1[:, :].broadcast_to([P, NC]), iota[:, n:n + NC])):
                    pool.tensor_tensor(what[:, part, w], hits[:, part], v.unsqueeze(2).broadcast_to([P, NC, KT]),
                                       ALU.mult).then_inc(r_what, 1)

            top_row = pool.to_reg(NT - 1)

            def copy_gather_index(k, u):
                if not before(k, 2):
                    pool.wait_ge(gathered[u], 8 * (k - u))
                pool.tensor_copy(gs[:, u], gidx[:, bass.ds(k, 1)]).then_inc(f_gather_index, 1)

            def copy_scatter_index(k, u):
                if before(k, 1):
                    pool.wait_ge(r_index, 2)
                if not before(k, 2):
                    pool.wait_ge(added[u], 8 * (k - u))
                pool.tensor_copy(ss[:, u], sidx[:, bass.ds(k, 1)]).then_inc(f_add_index, 1)

            LAG = 5

            def gather(k, u):
                pool.wait_ge(f_gather_index, k + 1)
                if not before(k, 2):
                    pool.wait_ge(f_rows_turned, k - 1)
                    pool.wait_ge(f_gates_kept, k - 1)
                if not before(k, LAG):
                    copy_scatter_index(k - LAG, (u - LAG) % 2)
                pool.indirect_dma_start(xg[:, u], None, x2d, bass.IndirectOffsetOnAxis(ap=gs[:, u], axis=0),
                                        bounds_check=top_row, oob_is_err=False).then_inc(gathered[u], 16)

            def scatter(k, u, last=False):
                pool.wait_ge(f_scaled, k + 1)
                pool.wait_ge(f_add_index, k + 1)
                if not last:
                    copy_gather_index(k + LAG + 1, (u + LAG + 1) % 2)
                pool.indirect_dma_start(accd[u], bass.IndirectOffsetOnAxis(ap=ss[:, u], axis=0), ys[:, u], None,
                                        bounds_check=top_row, oob_is_err=False, compute_op=ALU.add).then_inc(added[u], 16)

            def expert_tile(k, u, last=False):
                gather(k, u)
                if before(k, LAG):
                    copy_gather_index(k + 1, 1 - u)
                else:
                    scatter(k - LAG, (u - LAG) % 2, last)

            pool.wait_ge(r_index, 1)
            pool.wait_ge(d_rows_stored, 32)
            pool.wait_ge(d_gates_stored, 16)
            pool.wait_ge(d_zeroed, 16)
            copy_gather_index(0, 0)
            tiles(pool, KT - 1, 2, expert_tile, head=LAG + 3)
            expert_tile(KT - 1, (KT - 1) % 2, last=True)
            for k in range(KT - LAG, KT):
                copy_scatter_index(k, k % 2)
                scatter(k, k % 2, last=True)
            for q in range(PAIRS // QT):
                part = slice(q * QT, (q + 1) * QT)
                pool.wait_ge(sums_loaded[q], 32)
                pool.tensor_tensor(x2[:, part], wide[:, 0, part], wide[:, 1, part], ALU.add).then_inc(o_sum, 1)

        @block.scalar
        def _(act):
            for i in range(2):
                act.wait_ge(composite, i + 1)
                act.activation(wfeat[:, i], psF[:, i * HM:(i + 1) * HM], ACT.Copy,
                               scale=float(DK) ** -0.5).then_inc(composite_kept, 1)
            act.wait_ge(pool_consts, ATTENTION_CONSTS)

            def features(t, k):
                act.wait_ge(a_shifted, 2 * t + 2)
                act.activation(phi[:, k], phi[:, k], ACT.Exp).then_inc(a_exp, 1)

            def phT_copy(t, k):
                act.wait_ge(a_phi_turned, t + 1)
                if not before(t, 2):
                    act.wait_ge(a_num, t - 1)
                act.activation(phT[:, k], psT, ACT.Identity, bias=eps6[:, :]).then_inc(a_phi_copied, 1)

            def mT_copy(t, k):
                act.wait_ge(a_merged_turned, t + 1)
                if not before(t, 2):
                    act.wait_ge(a_out, t - 1)
                act.activation(mgT[:, k], psW[:, 0:P], ACT.Copy).then_inc(a_merged_copied, 1)

            def attention(t, k):
                if not before(t, 3):
                    mT_copy(t - 3, 1 - k)
                act.wait_ge(a_projected, t + 1)
                if not before(t, 2):
                    act.wait_ge(a_norms, t - 1)
                act.activation(sq[:, k], psQ[:, 0:2 * P], ACT.Square, scale=float(2 * DK) ** -0.5).then_inc(a_squared, 1)
                if not before(t, 2):
                    act.wait_ge(a_kv, t - 1)
                for b in range(2):
                    rows = slice(b * HALF, (b + 1) * HALF)
                    act.activation(vv[rows, k, :, b, :, 0:DK],
                                   psQ[rows, 2 * P:3 * P].rearrange("p (g h d) -> p g h d", g=4, h=4),
                                   ACT.Copy).then_inc(a_v_kept, 1)
                if not before(t, 1):
                    features(t - 1, 1 - k)
                    phT_copy(t - 1, 1 - k)

            tiles(act, PAIRS, 2, attention, head=6)
            mT_copy(PAIRS - 3, 1)
            features(PAIRS - 1, 1)
            phT_copy(PAIRS - 1, 1)

            def ready_table(function):
                act.activation(spare[:, :], eps6[:, :], function)

            def deviations(n, first, end):
                act.wait_ge(ln_moments, n)
                act.activation(rstd[:, first:end], mv[:, first:end, 1], ACT.Sqrt, bias=eps5[:, :]).then_inc(ln_deviation, 1)

            def turned_x(p):
                act.wait_ge(b_x_turned, p + 1)
                act.activation(xnT[:, p], psO, ACT.Copy).then_inc(b_xnT, 1)

            def turned_ctx(p, u, g):
                act.wait_ge(b_ctx_turned, 6 * p + g + 1)
                if g == 0 and not before(p, 2):
                    act.wait_ge(b_sim, NG * (p - 1))
                act.activation(cxT[:, u, g // 3, g % 3 * W:(g % 3 + 1) * W], psC[:, 0], ACT.Copy).then_inc(b_ctx_even, 1)

            def hq_turned(p):
                act.wait_ge(b_hq_turned, p + 1)
                act.activation(hqT[:, p], psO, ACT.Copy).then_inc(b_hqT, 1)

            def exponentials(p, u, g):
                if g == 0:
                    act.wait_ge(b_neg_max, p + 1)
                    if not before(p, 2):
                        act.wait_ge(b_sum, p - 1)
                if not before(p, 1):
                    act.wait_ge(b_exp_turned, NG * (p - 1) + g + 1)
                act.activation(ex[:, g * W:(g + 1) * W], psS[:, g], ACT.Exp, bias=nm[:, u],
                               accum_out=s3[:, u, g:g + 1]).then_inc(b_exp, 1)

            def cross(p, k):
                u = k % 2
                exponentials(p, u, 1)
                if not before(p, 1):
                    hq_turned(p - 1)
                if not after(p, 2, PAIRS):
                    turned_ctx(p + 2, u, 0)
                if not after(p, 1, PAIRS):
                    turned_x(p + 1)
                exponentials(p, u, 2)
                act.wait_ge(b_exp_turned, NG * p + 2)
                if not before(p, 1):
                    act.wait_ge(b_values, p)
                act.activation(etT[0:JP, 1], psE[0:JP, 1].rearrange("p (c i) -> p c i", c=CG),
                               ACT.Copy).then_inc(b_exp_oddA, 1)
                if not after(p, 2, PAIRS):
                    turned_ctx(p + 2, u, 2)
                    turned_ctx(p + 2, u, 4)
                if not after(p, 1, PAIRS):
                    exponentials(p + 1, 1 - u, 0)
                act.wait_ge(b_values, p + 1)
                act.wait_ge(b_inv_sum, p + 1)
                if not before(p, 1):
                    act.wait_ge(b_hq_turned, p)
                act.activation(hq[:, :], psO, ACT.Copy, scale=rz[:, u]).then_inc(b_hq, 1)

            mT_copy(PAIRS - 2, 0)
            act.wait_ge(pool_consts, POOL_CONSTS)
            turned_ctx(0, 0, 0)
            turned_ctx(0, 0, 2)
            mT_copy(PAIRS - 1, 1)
            turned_ctx(0, 0, 4)
            deviations(1, 0, PAIRS)
            turned_ctx(1, 1, 0)
            turned_x(0)
            ready_table(ACT.Exp)
            turned_ctx(1, 1, 2)
            turned_ctx(1, 1, 4)
            exponentials(0, 0, 0)
            for p in range(CR):
                cross(p, p)
            with act.Fori(CR, PAIRS - 2 * CR + 1, CR) as p0:
                for k in range(CR):
                    cross(p0 + k, k)
            for p in range(PAIRS - CR, PAIRS):
                cross(p, p % CR)
            hq_turned(PAIRS - 1)

            act.wait_ge(h_turned, 1)
            act.activation(rT[:, :, :], PS[0:PAIRS, 6, 0:P].rearrange("p (u i) -> p u i", u=2), ACT.Copy).then_inc(h_copied, 1)
            act.wait_ge(h_shifted, 1)
            act.activation(ba[:, :, 0:T], rT[:, :, 0:T], ACT.Exp).then_inc(h_exp, 1)

            def deviations_z(q):
                part = slice(q * QT, (q + 1) * QT)
                act.wait_ge(ln_moments, q + 2)
                act.activation(rstd[:, part], mv[:, part, 1], ACT.Sqrt, bias=eps5[:, :]).then_inc(ln_deviation, 1)

            def x2_rows(q):
                act.wait_ge(ln_shift, q + 1)
                for t in range(q * QT, (q + 1) * QT):
                    last = act.activation(x2[:, t], PS[:, 4 + q, t % QT * P:(t % QT + 1) * P], ACT.Identity,
                                          bias=shift[:, t:t + 1], scale=rstd[:, t:t + 1])
                last.then_inc(d_rows_normed, 1)

            def x2_turned(q):
                act.wait_ge(d_rows_turned, q + 1)
                if q >= 2:
                    act.wait_ge(d_hidden, q - 1)
                act.activation(x2s[:, q % 2], PS[:, q, :], ACT.Copy).then_inc(d_rows_copied, 1)

            def squares(q):
                part = slice(q * QT, (q + 1) * QT)
                act.wait_ge(r_centred, q + 1)
                act.activation(rt1[:, part], rt0[:, part], ACT.Square).then_inc(r_squared, 1)

            def deviations_h(q):
                part = slice(q * QT, (q + 1) * QT)
                act.wait_ge(r_var_sum, q + 1)
                act.activation(rstat[:, 1, part], rstat[:, 1, part], ACT.Sqrt, bias=eps6[:, :],
                               scale=1.0 / R1).then_inc(r_deviation, 1)

            deviations_z(0)
            x2_rows(0)
            deviations_z(1)
            x2_turned(0)
            x2_rows(1)
            x2_turned(1)
            squares(0)
            deviations_z(2)
            x2_rows(2)
            deviations_h(0)
            x2_turned(2)
            squares(1)
            deviations_z(3)
            x2_rows(3)
            deviations_h(1)
            x2_turned(3)
            squares(2)
            deviations_h(2)
            squares(3)
            deviations_h(3)
            for i in range(2):
                part = slice(i * PAIRS // 2, (i + 1) * PAIRS // 2)
                act.wait_ge(r_biased, 2 + i)
                if i == 1:
                    act.wait_ge(r_biased_last, 1)
                act.activation(rt1[:, part], rt0[:, part], ACT.Gelu_apprx_tanh).then_inc(r_gelu, 1)
            for i in range(2):
                act.wait_ge(r_hidden_turned, i + 1)
                act.activation(hrT[:, i * QT:(i + 1) * QT].rearrange("p q n -> p (q n)"), PS[:, i, :],
                               ACT.Copy).then_inc(r_hidden_copied, 1)
            act.wait_ge(r_difference, 1)
            act.activation(pw[:, 1], pw[:, 0], ACT.Exp).then_inc(r_exp, 1)
            ready_table(ACT.Gelu_apprx_tanh)
            act.wait_ge(r_minus_place, 1)
            for n in range(NC):
                last = act.activation(apart[:, n], iota[:, :], ACT.Abs, bias=minus_lo[:, n:n + 1])
            last.then_inc(r_apart, 1)
            act.wait_ge(r_apart, 1)
            act.activation(which[:, 3 * NC:4 * NC], apart, ACT.Relu, bias=one[:, :], scale=-1.0).then_inc(r_which_last, 1)

            def rows_turned(k, u):
                act.wait_ge(f_rows_turned, k + 1)
                if not before(k, 2):
                    act.wait_ge(f_lin_units, k - 1)
                act.activation(xgT[:, u], psX[:, u], ACT.Copy).then_inc(f_rows_copied, 1)

            def gate_weights(k, u, e):
                if not before(k, 2):
                    act.wait_ge(f_gate_units, k - 1)
                act.activation(w1t[:, u, F:2 * F], w1s[:, e, F:2 * F], ACT.Copy).then_inc(f_gate_weights, 1)

            def gelus(k, u, e):
                act.wait_ge(f_gate_units, k + 1)
                if not before(k, 2):
                    act.wait_ge(f_gated, k - 1)
                for c in range(FT):
                    last = act.activation(g2[:, u, c * P:(c + 1) * P], PS[:, 2 + 2 * u, c * P:(c + 1) * P],
                                          ACT.Gelu_apprx_tanh, bias=b1c[:, bass.ds(e * 2 * FT + FT + c, 1)])
                last.then_inc(f_gelu, 1)

            def expert_tile(k, u, last=False):
                if last:
                    gelus(k, u, *experts(act, k))
                    return
                this, following = experts(act, k, 2)
                rows_turned(k + 1, 1 - u)
                gate_weights(k + 1, 1 - u, following)
                gelus(k, u, this)

            act.wait_ge(r_experts, 1)
            act.wait_ge(w1_loaded, 16 * E)
            act.wait_ge(b_values, PAIRS)
            gate_weights(0, 0, *experts(act, 0))
            rows_turned(0, 0)
            tiles(act, KT - 1, 2, expert_tile)
            expert_tile(KT - 1, (KT - 1) % 2, last=True)

            def last_rows(q):
                act.wait_ge(ln_shift, q + 5)
                for t in range(q * QT + rows_here(q), (q + 1) * QT):
                    last = act.activation(wide[:, 0, t], x2[:, t], ACT.Identity, bias=shift[:, t:t + 1], scale=rstd[:, t:t + 1])
                last.then_inc(o_rows_act, 1)

            deviations(6, 0, QT)
            for q in range(1, PAIRS // QT):
                deviations(q + 6, q * QT, (q + 1) * QT)
                last_rows(q - 1)
            last_rows(PAIRS // QT - 1)

        @block.tensor
        def _(pe):
            pe.wait_ge(dve_consts, 1)
            pe.wait_ge(qk_weights_loaded, 32)
            for i in range(2):
                pe.matmul(psF[:, i * HM:(i + 1) * HM], wqk[:, i, :], pblk[:, :, :].rearrange("p h m -> p (h m)"),
                          start=True, stop=True).then_inc(composite, 1)
            pe.wait_ge(consts_loaded, 16 * len(CONSTS))
            pe.wait_ge(pool_consts, ATTENTION_CONSTS)
            pe.wait_ge(dve_consts, 5)

            def kv_and_turn(t, k):
                pe.wait_ge(a_exp, t + 1)
                if not before(t, 1):
                    pe.wait_ge(a_phi_copied, t)
                for g in range(4):
                    last = pe.transpose(psT[:, g * P:(g + 1) * P], phi[:, k, g * P:(g + 1) * P], ident[:, :])
                last.then_inc(a_phi_turned, 1)
                pe.wait_ge(a_v_kept, 2 * t + 2)
                pe.wait_ge(a_key_eps, t + 1)
                if not before(t, 1):
                    pe.wait_ge(a_kv_kept, t)
                for g in range(4):
                    last = pe.matmul(psKV[:, g].rearrange("p b c -> p (b c)"), phi[:, k, HM + g * P:HM + (g + 1) * P],
                                     vv[:, k, g].rearrange("p b h c -> p (b h c)"), start=True, stop=True)
                last.then_inc(a_kv, 1)

            def numerators(t, k):
                pe.wait_ge(a_phi_copied, t + 1)
                pe.wait_ge(a_kv_kept, t + 1)
                if not before(t, 1):
                    pe.wait_ge(a_merged, t)
                for g in range(4):
                    for b in range(2):
                        last = pe.matmul(psN[b * HALF:(b + 1) * HALF, g * 36:g * 36 + 36],
                                         phT[:, k, g * P + b * HALF:g * P + (b + 1) * HALF],
                                         kvs[:, k, g, b], start=True, stop=True)
                last.then_inc(a_num, 1)

            def turn_merged(t, k):
                pe.wait_ge(a_merged, t + 1)
                if not before(t, 1):
                    pe.wait_ge(a_res, t)
                pe.transpose(psW[:, 0:P], mg[:, k], ident[:, :]).then_inc(a_merged_turned, 1)

            def out_projection(t, k):
                pe.wait_ge(a_merged_copied, t + 1)
                pe.matmul(psW[:, P:2 * P], mgT[:, k], woT[:, :], start=True, stop=True).then_inc(a_out, 1)

            def attention(t, k):
                pe.wait_ge(xT_loaded[k], 8 * (t - k) + 16)
                if not before(t, 1):
                    pe.wait_ge(a_squared, t)
                    pe.wait_ge(a_v_kept, 2 * t)
                pe.matmul(psQ[:, 0:3 * P], xT[:, k], wqkvT[:, :, :].rearrange("p a b -> p (a b)"),
                          start=True, stop=True).then_inc(a_projected, 1)
                if not before(t, 3):
                    out_projection(t - 3, 1 - k)
                for i, done in enumerate((a_query_feat, a_key_feat)):
                    if before(t, 1):
                        pe.wait_ge(composite_kept, i + 1)
                    else:
                        pe.wait_ge(a_shifted, 2 * t - 1 + i)
                    pe.matmul(psF[:, i * HM:(i + 1) * HM], xT[:, k], wfeat[:, i, :], start=True,
                              stop=True).then_inc(done, 1)
                if not before(t, 2):
                    numerators(t - 2, k)
                if not before(t, 1):
                    kv_and_turn(t - 1, 1 - k)
                if not before(t, 2):
                    turn_merged(t - 2, k)

            def turn_x(p, u):
                pe.wait_ge(b_xn, p + 1)
                if not before(p, 2):
                    pe.wait_ge(b_hqT, p - 1)
                elif p == 1:
                    pe.wait_ge(b_xnT, 1)
                pe.transpose(psO, xn[:, u], ident[:, :]).then_inc(b_x_turned, 1)

            def turn_ctx(p, k, g):
                if g == 0:
                    pe.wait_ge(ctx_loaded[k], 16 * (p - k) + 64)
                if g >= 2 or not before(p, 1):
                    pe.wait_ge(b_ctx_odd if g % 2 else b_ctx_even, 3 * p + g // 2)
                for c in range(CG):
                    last = pe.transpose(psC[:, g % 2, c * JP:(c + 1) * JP], cx[0:JP, k, g // 3, (g % 3) * CG + c],
                                        ident[0:JP, 0:JP])
                last.then_inc(b_ctx_turned, 1)

            def turn_exp(p, g):
                pe.wait_ge(b_exp, NG * p + g + 1)
                if g == 2:
                    pe.wait_ge(b_exp_evenD, 2 * p + 1)
                elif not before(p, 1):
                    pe.wait_ge(b_exp_evenD, 2 * p) if g == 0 else pe.wait_ge(b_exp_oddA, p)
                for c in range(CG):
                    j = g * W + c * JP
                    last = pe.transpose(psE[0:JP, g % 2, c * P:(c + 1) * P], ex[:, j:j + JP], ident[:, :])
                last.then_inc(b_exp_turned, 1)

            def values(p, k, g):
                if g == 1:
                    pe.wait_ge(b_exp_oddA, p + 1)
                else:
                    pe.wait_ge(b_exp_evenD, 2 * p + 1 + g // 2)
                for c in range(CG):
                    for b in range(2):
                        last = pe.matmul(psO[b * HALF:(b + 1) * HALF], etT[0:JP, g, c, b * HALF:(b + 1) * HALF],
                                         cx[0:JP, k, b, g * CG + c], start=(g == 0 and c == 0),
                                         stop=(g == NG - 1 and c == CG - 1), skip_group_check=True)
                if g == NG - 1:
                    last.then_inc(b_values, 1)

            def turn_hq(p):
                pe.wait_ge(b_hq, p + 1)
                pe.transpose(psO, hq[:, :], ident[:, :]).then_inc(b_hq_turned, 1)

            def similarities(p, u, g):
                if g == 0:
                    pe.wait_ge(b_xw, p + 1)
                    pe.wait_ge(b_ctx_even, 3 * p + 3)
                    pe.wait_ge(b_ctx_odd, 3 * p + 3)
                if not before(p, 1):
                    pe.wait_ge(b_exp, NG * (p - 1) + g + 1)
                for b in range(2):
                    last = pe.matmul(psS[b * HALF:(b + 1) * HALF, g], xw[:, u, b * HALF:(b + 1) * HALF],
                                     cxT[:, u, b, g * W:(g + 1) * W], start=True, stop=True)
                last.then_inc(b_sim, 1)

            def cross(p, k):
                u = k % 2

                def next_ctx(g):
                    if not after(p, 2, PAIRS):
                        turn_ctx(p + 2, (k + 2) % CR, g)

                def next_similarities(g):
                    if not after(p, 1, PAIRS):
                        similarities(p + 1, 1 - u, g)

                turn_exp(p, 0)
                if not before(p, 1):
                    turn_hq(p - 1)
                next_ctx(0)
                if not after(p, 1, PAIRS):
                    turn_x(p + 1, 1 - u)
                turn_exp(p, 1)
                next_ctx(1)
                if after(p, 1, PAIRS):
                    pe.wait_ge(b_hqT, p)
                else:
                    pe.wait_ge(b_xnT, p + 2)
                values(p, k, 0)
                next_similarities(0)
                turn_exp(p, 2)
                next_ctx(2)
                next_similarities(1)
                values(p, k, 1)
                next_ctx(3)
                next_similarities(2)
                next_ctx(4)
                values(p, k, 2)
                next_ctx(5)

            tiles(pe, PAIRS, 2, attention)
            out_projection(PAIRS - 3, 1)
            numerators(PAIRS - 2, 0)
            kv_and_turn(PAIRS - 1, 1)
            pe.wait_ge(a_shifted, 2 * PAIRS)
            turn_ctx(0, 0, 0)
            turn_merged(PAIRS - 2, 0)
            turn_ctx(0, 0, 1)
            out_projection(PAIRS - 2, 0)
            turn_ctx(0, 0, 2)
            numerators(PAIRS - 1, 1)
            turn_ctx(0, 0, 3)
            turn_merged(PAIRS - 1, 1)
            turn_ctx(0, 0, 4)
            out_projection(PAIRS - 1, 1)
            turn_ctx(0, 0, 5)
            for g in range(2):
                turn_ctx(1, 1, g)
            pe.wait_ge(a_res, PAIRS)
            pe.wait_ge(a_squared, PAIRS)
            turn_x(0, 0)
            for g in range(NG):
                similarities(0, 0, g)
                turn_ctx(1, 1, g + 2)
            turn_ctx(1, 1, 5)
            for p in range(CR):
                cross(p, p)
            with pe.Fori(CR, PAIRS - 2 * CR + 1, CR) as p0:
                for k in range(CR):
                    cross(p0 + k, k)
            for p in range(PAIRS - CR, PAIRS):
                cross(p, p % CR)
            turn_hq(PAIRS - 1)

            pe.wait_ge(b_row_max, PAIRS)
            pe.wait_ge(b_exp_oddA, PAIRS)
            pe.transpose(PS[0:PAIRS, 6, 0:P], rm_all[:, :], ident[:, :]).then_inc(h_turned, 1)

            def product(q, parts):
                part = slice(q * QT, (q + 1) * QT)
                for i, x in parts:
                    last = pe.matmul(PS[:, q, :], wqv[:, i], x[:, part].rearrange("p t i -> p (t i)"), start=(i == 0),
                                     stop=(i == 3))
                return last

            def heads(q):
                for t in range(q * QT, (q + 1) * QT):
                    last = pe.matmul(PS[:, 4 + q, t % QT * 2:t % QT * 2 + 2], rows[:, t], wcol[:, t], start=True, stop=True)
                last.then_inc(h_heads, 1)

            def with_heads(q):
                pe.wait_ge(h_x4, q + 1)
                product(q, [(3, x4)]).then_inc(c_query, 1)

            def turn_z(q):
                pe.wait_ge(c_z, q + 1)
                for k in range(QT):
                    last = pe.transpose(PS[:, 4 + q, k * P:(k + 1) * P], zT[:, q % 2, k * P:(k + 1) * P], ident[:, :])
                last.then_inc(c_z_turned, 1)

            def turn_x2(q):
                pe.wait_ge(d_rows_normed, q + 1)
                for k in range(QT):
                    last = pe.transpose(PS[:, q, k * P:(k + 1) * P], x2[:, q * QT + k], ident[:, :])
                last.then_inc(d_rows_turned, 1)

            def router(q):
                pe.wait_ge(d_rows_copied, q + 1)
                for k in range(QT):
                    last = pe.matmul(PS[:, 4 + q, k * R1:(k + 1) * R1], x2s[:, q % 2, k * P:(k + 1) * P], wr1[:, :],
                                     start=True, stop=True)
                last.then_inc(d_hidden, 1)

            pe.wait_ge(h_x3, PAIRS)
            product(0, [(0, xnT), (1, hqT), (2, x3)])
            pe.wait_ge(h_weights, 1)
            pe.transpose(PS[:, 6, 0:PAIRS], ba[:, :, :].rearrange("p u i -> p (u i)"),
                         ident[0:PAIRS, 0:PAIRS]).then_inc(h_weights_turned, 1)
            product(1, [(0, xnT)])
            pe.wait_ge(h_weight_cols, 1)
            heads(0)
            product(1, [(1, hqT)])
            heads(1)
            product(1, [(2, x3)])
            with_heads(0)
            heads(2)
            with_heads(1)
            turn_z(0)
            product(2, [(0, xnT)])
            heads(3)
            product(2, [(1, hqT), (2, x3)])
            turn_z(1)
            with_heads(2)
            turn_x2(0)
            product(3, [(0, xnT)])
            turn_z(2)
            router(0)
            product(3, [(1, hqT)])
            turn_x2(1)
            product(3, [(2, x3)])
            with_heads(3)
            router(1)
            turn_z(3)
            turn_x2(2)
            router(2)
            turn_x2(3)
            router(3)

            for i in range(2):
                pe.wait_ge(r_gelu, i + 1)
                for q in range(QT):
                    t = 2 * (i * QT + q)
                    last = pe.transpose(PS[:, i, q * P:(q + 1) * P], rt1[:, t:t + 2, :].rearrange("p a n -> p (a n)"),
                                        ident[:, :])
                last.then_inc(r_hidden_turned, 1)
            for q in range(PAIRS // 2):
                if q % QT == 0:
                    pe.wait_ge(r_hidden_copied, q // QT + 1)
                last = pe.matmul(PS[:, 6 + q // QT, 2 * q * E:(2 * q + 2) * E], hrT[:, q],
                                 wr2[:, :, :].rearrange("p a e -> p (a e)"), start=True, stop=True)
                if q % QT == QT - 1:
                    last.then_inc(r_logits, 1)
            pe.wait_ge(r_chosen, 1)
            pe.matmul(PS[:, 0, 0:E], below[:, :], in_row[:, :], start=True, stop=True)
            pe.matmul(PS[:, 0, E:2 * E], ones_bf[:, :], in_row[:, :], start=True, stop=True).then_inc(r_rank, 1)
            for n in range(2 * PAIRS):
                if n % NC == 0:
                    pe.wait_ge(r_what, 2 * (n // NC + 1))
                    if n < 3 * NC:
                        pe.wait_ge(r_which, n // NC + 1)
                    else:
                        pe.wait_ge(r_which_last, 1)
                last = pe.matmul(PS[:, 7, 0:2 * KT], which[:, n], what[:, n].rearrange("p c k -> p (c k)"),
                                 start=(n == 0), stop=(n == 2 * PAIRS - 1))
            last.then_inc(r_table, 1)

            def turn_rows(k, u):
                pe.wait_ge(gathered[u], 8 * (k - u) + 16)
                if not before(k, 2):
                    pe.wait_ge(f_rows_copied, k - 1)
                pe.transpose(psX[:, u], xg[:, u, 0:D], ident[:, :]).then_inc(f_rows_turned, 1)

            def up(k, u):
                pe.wait_ge(f_rows_copied, k + 1)
                for half, weights, done, free in ((1, f_gate_weights, f_gate_units, f_gelu), (0, f_lin_weights, f_lin_units, f_gated)):
                    pe.wait_ge(weights, k + 1)
                    if not before(k, 2):
                        pe.wait_ge(free, k - 1)
                    for c in range(FT):
                        last = pe.matmul(PS[:, 1 + 2 * u + half, c * P:(c + 1) * P],
                                         w1t[:, u, half * F + c * P:half * F + (c + 1) * P], xgT[:, u],
                                         start=True, stop=True)
                    last.then_inc(done, 1)

            def down(k, u, e):
                pe.wait_ge(f_gated, k + 1)
                if not before(k, 2):
                    pe.wait_ge(f_biased, k - 1)
                for f in range(FT):
                    last = pe.matmul(PS[:, 6 + u, 0:P], gg[:, u, f * P:(f + 1) * P], w2s[:, e, f, :],
                                     start=(f == 0), stop=(f == FT - 1))
                last.then_inc(f_result, 1)

            def expert_tile(k, u, last=False):
                if not last:
                    turn_rows(k + 1, 1 - u)
                up(k, u)
                if not before(k, 1):
                    down(k - 1, 1 - u, *experts(pe, k - 1))

            pe.wait_ge(r_experts, 1)
            pe.wait_ge(w2_loaded, 16 * E)
            turn_rows(0, 0)
            tiles(pe, KT - 1, 2, expert_tile)
            expert_tile(KT - 1, (KT - 1) % 2, last=True)
            down(KT - 1, (KT - 1) % 2, *experts(pe, KT - 1))

        @block.vector
        def _(dve):
            steps = [0]

            def link(ins):
                steps[0] += 1
                ins.then_inc(chain, 1)
                dve.wait_ge(chain, steps[0])

            link(dve.memset(scan[:, :, :, :], 0.0))
            dve.wait_ge(proj_loaded, 16)
            dve.wait_ge(headmask_made, 3)
            dve.tensor_tensor(pblk[:, :, :], projT[:, :].unsqueeze(1).broadcast_to([P, H, M]),
                              headmask[:, :].unsqueeze(2).broadcast_to([P, H, M]), ALU.mult).then_inc(dve_consts, 1)
            dve.wait_ge(pool_consts, ATTENTION_CONSTS)
            for b in range(2):
                for k in range(2):
                    dve.memset(vv[b * HALF:b * HALF + T, k, :, b, :, DK], 1.0).then_inc(dve_consts, 1)

            def keep_kv(t, k):
                dve.wait_ge(a_kv, t + 1)
                if not before(t, 2):
                    dve.wait_ge(a_num, t - 1)
                dve.tensor_tensor(kvs[:, k].rearrange("p g b c -> p (g b c)"), PS[:, 4, 0:2 * H * (DK + 1)],
                                  kvmask[:, :, :, :, :].rearrange("p g b h c -> p (g b h c)"), ALU.mult).then_inc(a_kv_kept, 1)

            def merged(t, k):
                dve.wait_ge(a_num, t + 1)
                dve.tensor_scalar(den[:, k], num[:, :, DK], M * 1e-6, None, ALU.add).then_inc(a_den, 1)
                dve.wait_ge(a_den, t + 1)
                dve.reciprocal(rden[:, k], den[:, k]).then_inc(a_rden, 1)
                dve.wait_ge(a_rden, t + 1)
                if not before(t, 2):
                    dve.wait_ge(a_merged_turned, t - 1)
                dve.tensor_tensor(mg[:, k].rearrange("p (h d) -> p h d", h=H), num[:, :, 0:DK],
                                  rden[:, k].unsqueeze(2).broadcast_to([P, H, DK]), ALU.mult).then_inc(a_merged, 1)

            def residual(t, k):
                dve.wait_ge(a_out, t + 1)
                dve.wait_ge(a_xb, t + 1)
                dve.tensor_tensor(res[:, t], psW[:, P:2 * P], xb[:, k], ALU.add).then_inc(a_res, 1)
                dve.wait_ge(a_res, t + 1)
                dve.bn_stats(st[:, t], res[:, t]).then_inc(a_stats, 1)

            def attention(t, r):
                k = r % 2
                if not before(t, 3):
                    residual(t - 3, (r - 3) % 4)
                dve.wait_ge(a_squared, t + 1)
                if not before(t, 2):
                    dve.wait_ge(a_offset, t - 1)
                dve.tensor_reduce(nr[:, k], sq[:, k].rearrange("p (h d) -> p h d", d=DK), AX.X, ALU.add).then_inc(a_norms, 1)
                for i, ready in enumerate((a_query_feat, a_key_feat)):
                    dve.wait_ge(ready, t + 1)
                    dve.tensor_reduce(mx[:, k, i * H:(i + 1) * H], feat[:, i * H:(i + 1) * H], AX.X,
                                      ALU.max).then_inc(a_max, 1)
                if not before(t, 2):
                    merged(t - 2, k)
                dve.wait_ge(a_max, 2 * t + 2)
                dve.wait_ge(a_norms, t + 1)
                dve.tensor_tensor(cc[:, k], mx[:, k], nr[:, k], ALU.add).then_inc(a_offset, 1)
                dve.wait_ge(a_offset, t + 1)
                if not before(t, 2):
                    dve.wait_ge(a_kv, t - 1)
                for i in range(2):
                    dve.tensor_tensor(phi[:, k].rearrange("p (h m) -> p h m", m=M)[:, i * H:(i + 1) * H],
                                      feat[:, i * H:(i + 1) * H],
                                      cc[:, k, i * H:(i + 1) * H].unsqueeze(2).broadcast_to([P, H, M]),
                                      ALU.subtract).then_inc(a_shifted, 1)
                if not before(t, 1):
                    keep_kv(t - 1, 1 - k)

            def moments(first, end):
                for t in range(first, end):
                    last = dve.bn_aggr(mv[:, t], st[:, t])
                return last

            def inverse_deviations(n, first, end):
                dve.wait_ge(ln_deviation, n)
                link(dve.reciprocal(rstd[:, first:end], rstd[:, first:end]))

            def norm1(p, u):
                if not before(p, 2):
                    dve.wait_ge(b_x_turned, p - 1)
                    dve.wait_ge(b_rows_kept, p - 1)
                dve.tensor_scalar(xn[:, u], res[:, p], mv[:, p, 0:1], rstd[:, bass.ds(p, 1)], ALU.subtract,
                                  ALU.mult).then_inc(b_xn, 1)

            def row_term(p, u):
                dve.wait_ge(b_xn, p + 1)
                if not before(p, 2):
                    dve.wait_ge(b_row_max, p - 1)
                if not before(p, 1):
                    dve.wait_ge(b_row_term, p)
                dve.scalar_tensor_tensor(out=term_products[:, :], in0=xn[:, u], scalar=1.0, in1=w1_b[:, :], op0=ALU.mult,
                                         op1=ALU.mult, accum_out=rs[:, u]).then_inc(b_row_term, 1)

            def similarity_weights(p, u):
                dve.wait_ge(b_xnT, p + 1)
                if not before(p, 2):
                    dve.wait_ge(b_sim, NG * (p - 1))
                dve.tensor_scalar(xw[:, u], xnT[:, p], wsim[:, 2:3], wsim[:, 1:2], ALU.mult, ALU.add).then_inc(b_xw, 1)

            def turned_ctx(p, u, g):
                dve.wait_ge(b_ctx_turned, 6 * p + g + 1)
                if g == 1 and not before(p, 2):
                    dve.wait_ge(b_sim, NG * (p - 1))
                dve.tensor_copy(cxT[:, u, g // 3, g % 3 * W:(g % 3 + 1) * W], psC[:, 1]).then_inc(b_ctx_odd, 1)

            def maxima(p, g):
                dve.wait_ge(b_sim, NG * p + g + 1)
                if g == 0 and not before(p, 1):
                    dve.wait_ge(b_neg_max, p)
                dve.tensor_reduce(m3[:, g:g + 1], psS[:, g], AX.X, ALU.max).then_inc(b_group_max, 1)

            def row_maxima(p, u):
                dve.wait_ge(b_group_max, NG * p + NG)
                if not before(p, 2):
                    dve.wait_ge(b_row_max, p - 1)
                    dve.wait_ge(b_exp, NG * (p - 1))
                dve.tensor_reduce(nm[:, u], m3[:, :], AX.X, ALU.max, negate=True).then_inc(b_neg_max, 1)

            def turned_exp(p, g):
                dve.wait_ge(b_exp_turned, NG * p + g + 1)
                if g == 0 and not before(p, 1):
                    dve.wait_ge(b_values, p)
                dve.tensor_copy(etT[0:JP, g], psE[0:JP, 0].rearrange("p (c i) -> p c i", c=CG)).then_inc(b_exp_evenD, 1)

            def cross(p, k):
                u = k % 2
                turned_exp(p, 0)
                if not after(p, 1, PAIRS):
                    similarity_weights(p + 1, 1 - u)
                if not after(p, 2, PAIRS):
                    norm1(p + 2, u)
                    row_term(p + 2, u)
                    turned_ctx(p + 2, u, 1)
                if not after(p, 1, PAIRS):
                    maxima(p + 1, 0)
                dve.wait_ge(b_exp, NG * p + NG)
                if not before(p, 1):
                    dve.wait_ge(b_inv_sum, p)
                dve.tensor_reduce(s1[:, :], s3[:, u], AX.X, ALU.add).then_inc(b_sum, 1)
                turned_exp(p, 2)
                dve.wait_ge(b_sum, p + 1)
                if not before(p, 2):
                    dve.wait_ge(b_hq, p - 1)
                dve.reciprocal(rz[:, u], s1[:, :]).then_inc(b_inv_sum, 1)
                if not after(p, 1, PAIRS):
                    maxima(p + 1, 1)
                if not after(p, 2, PAIRS):
                    turned_ctx(p + 2, u, 3)
                if not after(p, 1, PAIRS):
                    maxima(p + 1, 2)
                    row_maxima(p + 1, 1 - u)
                if not after(p, 2, PAIRS):
                    turned_ctx(p + 2, u, 5)

            tiles(dve, PAIRS, 4, attention)
            residual(PAIRS - 3, 1)
            merged(PAIRS - 2, 0)
            keep_kv(PAIRS - 1, 1)
            dve.wait_ge(a_stats, PAIRS - 2)
            moments(0, PAIRS - 2)
            residual(PAIRS - 2, 2)
            turned_ctx(0, 0, 1)
            merged(PAIRS - 1, 1)
            turned_ctx(0, 0, 3)
            residual(PAIRS - 1, 3)
            dve.wait_ge(a_stats, PAIRS)
            moments(PAIRS - 2, PAIRS).then_inc(ln_moments, 1)
            turned_ctx(0, 0, 5)
            inverse_deviations(1, 0, PAIRS)
            norm1(0, 0)
            dve.wait_ge(late_loaded, 16 * len(LATE))
            similarity_weights(0, 0)
            turned_ctx(1, 1, 1)
            row_term(0, 0)
            maxima(0, 0)
            maxima(0, 1)
            norm1(1, 1)
            row_term(1, 1)
            maxima(0, 2)
            row_maxima(0, 0)
            turned_ctx(1, 1, 3)
            turned_ctx(1, 1, 5)
            for p in range(CR):
                cross(p, p)
            with dve.Fori(CR, PAIRS - 2 * CR + 1, CR) as p0:
                for k in range(CR):
                    cross(p0 + k, k)
            for p in range(PAIRS - CR, PAIRS):
                cross(p, p % CR)

            link(dve.tensor_reduce(halves[:, :], ident[:, :].rearrange("p (b i) -> p b i", b=2), AX.X, ALU.add))
            dve.wait_ge(h_copied, 1)
            rows = rT[:, :, 0:T]
            link(dve.tensor_scalar(rows, rows, bsim[:, :], None, ALU.add))
            link(dve.tensor_reduce(bmx[:, :, :], rows, AX.X, ALU.max))
            dve.tensor_tensor(rows, rows, bmx[:, :, :].broadcast_to([PAIRS, 2, T]), ALU.subtract).then_inc(h_shifted, 1)
            dve.wait_ge(h_exp, 1)
            link(dve.tensor_reduce(bmx[:, :, :], ba[:, :, 0:T], AX.X, ALU.add))
            link(dve.reciprocal(bmx[:, :, :], bmx[:, :, :]))
            dve.tensor_tensor(ba[:, :, 0:T], ba[:, :, 0:T], bmx[:, :, :].broadcast_to([PAIRS, 2, T]),
                              ALU.mult).then_inc(h_weights, 1)
            dve.wait_ge(h_weights_turned, 1)
            dve.tensor_tensor(wcol[:, :, :], PS[:, 6, 0:PAIRS].unsqueeze(2).broadcast_to([P, PAIRS, 2]),
                              halves[:, :].unsqueeze(1).broadcast_to([P, PAIRS, 2]), ALU.mult).then_inc(h_weight_cols, 1)

            def keep_heads(q):
                dve.wait_ge(h_heads, q + 1)
                dve.tensor_copy(hcb[:, 2 * q * QT:2 * (q + 1) * QT], PS[:, 4 + q, 0:2 * QT]).then_inc(h_heads_kept, 1)

            def z_sum(q):
                dve.wait_ge(c_query, q + 1)
                if q >= 2:
                    dve.wait_ge(c_z_turned, q - 1)
                dve.scalar_tensor_tensor(out=zT[:, q % 2], in0=PS[:, q, :], scalar=bqv[:, :],
                                         in1=xnT[:, q * QT:(q + 1) * QT].rearrange("p t i -> p (t i)"),
                                         op0=ALU.add, op1=ALU.add).then_inc(c_z, 1)

            def z_stats(q):
                dve.wait_ge(c_z_turned, q + 1)
                for t in range(q * QT, (q + 1) * QT):
                    last = dve.bn_stats(st[:, t], PS[:, 4 + q, t % QT * P:(t % QT + 1) * P])
                link(last)
                moments(q * QT, (q + 1) * QT).then_inc(ln_moments, 1)

            def norm2(q):
                part = slice(q * QT, (q + 1) * QT)
                inverse_deviations(q + 2, q * QT, (q + 1) * QT)
                dve.scalar_tensor_tensor(out=shift[:, part], in0=mv[:, part, 0], scalar=-1.0, in1=rstd[:, part],
                                         op0=ALU.mult, op1=ALU.mult).then_inc(ln_shift, 1)

            def over_units(v):
                return v.unsqueeze(2).broadcast_to([P, QT, R1])

            def centred(q):
                part = slice(q * QT, (q + 1) * QT)
                dve.wait_ge(d_hidden, q + 1)
                raw = rt2[:, part]
                link(dve.tensor_tensor(raw, PS[:, 4 + q, 0:QT * R1].rearrange("p (t n) -> p t n", n=R1),
                                       over_tiles(br1_b), ALU.add))
                link(dve.tensor_reduce(rstat[:, 0, part], raw, AX.X, ALU.add))
                link(dve.tensor_scalar(rstat[:, 0, part], rstat[:, 0, part], -1.0 / R1, None, ALU.mult))
                dve.tensor_tensor(rt0[:, part], raw, over_units(rstat[:, 0, part]), ALU.add).then_inc(r_centred, 1)

            def variance(q):
                part = slice(q * QT, (q + 1) * QT)
                dve.wait_ge(r_squared, q + 1)
                dve.tensor_reduce(rstat[:, 1, part], rt1[:, part], AX.X, ALU.add).then_inc(r_var_sum, 1)

            def normed(q):
                part = slice(q * QT, (q + 1) * QT)
                dve.wait_ge(r_deviation, q + 1)
                link(dve.reciprocal(rstat[:, 2, part], rstat[:, 1, part]))
                dve.tensor_tensor(rt0[:, part], rt0[:, part], over_units(rstat[:, 2, part]), ALU.mult).then_inc(r_normed, 1)

            keep_heads(0)
            keep_heads(1)
            z_sum(0)
            keep_heads(2)
            z_sum(1)
            z_stats(0)
            keep_heads(3)
            norm2(0)
            z_stats(1)
            norm2(1)
            z_sum(2)
            centred(0)
            z_stats(2)
            norm2(2)
            variance(0)
            z_sum(3)
            centred(1)
            normed(0)
            z_stats(3)
            variance(1)
            norm2(3)
            centred(2)
            normed(1)
            variance(2)
            centred(3)
            normed(2)
            variance(3)
            normed(3)
            part = rt0[:, PAIRS - QT:PAIRS]
            dve.wait_ge(r_normed, PAIRS // QT)
            link(dve.tensor_tensor(part, part, over_tiles(lns_b), ALU.mult))
            dve.tensor_tensor(part, part, over_tiles(lnb_b), ALU.add).then_inc(r_biased_last, 1)
            id_real = ident[:, :].rearrange("p (b i) -> p b i", b=2)[:, :, 0:T]
            link(dve.tensor_reduce(real[:, :], id_real, AX.XY, ALU.add))
            link(dve.tensor_scalar(pad[:, :], real[:, :], -float(P), float(P), ALU.mult, ALU.add))
            link(dve.tensor_scalar(several[:, :], iota[:, 0:FULL], float(P), None, ALU.mult))
            link(dve.tensor_tensor(earlier[:, :, :], iota[:, 0:E].unsqueeze(2).broadcast_to([P, E, E]),
                                   iota1[:, 0:E].unsqueeze(1).broadcast_to([P, E, E]), ALU.is_ge))
            link(dve.tensor_scalar(earlier[:, :, :], earlier[:, :, :], float(P), None, ALU.mult))

            def logits(i):
                part = slice(i * PAIRS // 2, (i + 1) * PAIRS // 2)
                dve.wait_ge(r_logits, i + 1)
                link(dve.tensor_tensor(lg[:, part], PS[:, 6 + i, i * P // 2:(i + 1) * P // 2].rearrange("p (t e) -> p t e", e=E),
                                       br2_b[:, :].unsqueeze(1).broadcast_to([P, PAIRS // 2, E]), ALU.add))
                for t in range(i * PAIRS // 2, (i + 1) * PAIRS // 2):
                    last = dve.max(top[:, t], lg[:, t])
                link(last)

            def places(i):
                for t in range(i * PAIRS // 2, (i + 1) * PAIRS // 2):
                    last = dve.max_index(topi[:, t], top[:, t], lg[:, t])
                return last

            logits(0)
            places(0)
            logits(1)
            dve.tensor_tensor(pw[:, 0], top[:, :, 1], top[:, :, 0], ALU.subtract).then_inc(r_difference, 1)
            link(places(1))
            for i in range(2):
                last = dve.scalar_tensor_tensor(out=oh[:, i], in0=topi[:, :, i:i + 1].broadcast_to([P, PAIRS, E]),
                                                scalar=pad[:, :], in1=iota[:, 0:E].unsqueeze(1).broadcast_to([P, PAIRS, E]),
                                                op0=ALU.add, op1=ALU.is_equal)
            link(last)
            link(dve.tensor_tensor(scan[:, 0, 8:], oh[:, 0], oh[:, 1], ALU.add))
            with nc.allow_low_precision(reason="counts up to the number of tiles are exact"):
                dve.tensor_reduce(in_row[:, :], scan[:, 0, 8:].rearrange("p t e -> p e t"), AX.X,
                                  ALU.add).then_inc(r_chosen, 1)
            dve.wait_ge(r_exp, 1)
            link(dve.tensor_scalar(pw[:, 3], pw[:, 1], 1.0, None, ALU.add))
            dve.reciprocal(pw[:, 2], pw[:, 3]).then_inc(r_first_weight, 1)
            dve.wait_ge(r_chosen, 1)
            for i, d in enumerate((1, 2, 4, 8)):
                old, new = scan[:, i % 2], scan[:, 1 - i % 2]
                link(dve.tensor_tensor(new[:, 8:], old[:, 8:], old[:, 8 - d:8 - d + PAIRS], ALU.add))
            dve.wait_ge(r_rank, 1)
            counts = PS[:, 0, E:2 * E]
            link(dve.tensor_tensor(full, counts.unsqueeze(2).broadcast_to([P, E, FULL]),
                                   several[:, :].unsqueeze(1).broadcast_to([P, E, FULL]), ALU.is_gt))
            link(dve.tensor_reduce(tiles_e[:, :], full, AX.X, ALU.add))
            link(dve.tensor_tensor(parts_e[:, :, :], earlier[:, :, :], tiles_e[:, :].unsqueeze(1).broadcast_to([P, E, E]),
                                   ALU.mult))
            link(dve.tensor_reduce(base[:, 0], parts_e[:, :, :], AX.X, ALU.add))
            link(dve.tensor_tensor(base[:, 1], PS[:, 0, 0:E], base[:, 0], ALU.add))
            link(dve.tensor_tensor(slot[:, :, :], scan[:, 0, 7:7 + PAIRS],
                                   base[:, 1].unsqueeze(1).broadcast_to([P, PAIRS, E]), ALU.add))
            link(dve.tensor_tensor(sel[:, :, :, :], oh[:, :, :, :], slot[:, :, :].unsqueeze(1).broadcast_to([P, 2, PAIRS, E]),
                                   ALU.mult))
            with nc.allow_low_precision(reason="one whole number and zeros"):
                link(dve.tensor_reduce(slu[:, 0], sel[:, :, :, :].rearrange("p a t e -> p (a t) e"), AX.X, ALU.add))
            dve.tensor_scalar(slu[:, 1], slu[:, 0], P - 1, None, ALU.bitwise_and)
            link(dve.tensor_scalar(slu[:, 2], slu[:, 0], 7, None, ALU.logical_shift_right))
            dve.tensor_scalar(minus_lo[:, :], slu[:, 1, 3 * NC:4 * NC], -1.0, None, ALU.mult).then_inc(r_minus_place, 1)
            link(dve.tensor_scalar(hi1[:, :], slu[:, 2], 1.0, real[:, :], ALU.add, ALU.mult))
            for c in range(4):
                part = slice(c * NC, (c + 1) * NC)
                dve.tensor_tensor(hits[:, part], hi1[:, part].unsqueeze(2).broadcast_to([P, NC, KT]),
                                  iota1[:, :].unsqueeze(1).broadcast_to([P, NC, KT]), ALU.is_equal).then_inc(r_hits, 1)
            for c in range(3):
                part = slice(c * NC, (c + 1) * NC)
                dve.tensor_tensor(which[:, part], slu[:, 1, part].unsqueeze(2).broadcast_to([P, NC, P]),
                                  iota[:, :].unsqueeze(1).broadcast_to([P, NC, P]), ALU.is_equal).then_inc(r_which, 1)
            link(dve.scalar_tensor_tensor(out=last_tile[:, :], in0=base[:, 0], scalar=1.0 / P, in1=tiles_e[:, :],
                                          op0=ALU.mult, op1=ALU.add))
            link(dve.tensor_tensor(late_tile, iota[:, 0:KT].unsqueeze(2).broadcast_to([P, KT, E]),
                                   last_tile[:, :].unsqueeze(1).broadcast_to([P, KT, E]), ALU.is_ge))
            dve.wait_ge(r_table, 1)
            table = PS[:, 7, 0:2 * KT].rearrange("p (c k) -> p c k", c=2)
            link(dve.tensor_scalar(slot_token[:, :], table[:, 0], -1.0, float(PAIRS), ALU.add, ALU.mult))
            link(dve.tensor_tensor(slot_token[:, :], slot_token[:, :], table[:, 1], ALU.add))
            dve.tensor_scalar(gidx[:, :], slot_token[:, :], 0.0, None, ALU.max).then_inc(r_index, 1)
            link(dve.tensor_reduce(ekf[:, :], late_tile, AX.X, ALU.add))
            dve.tensor_scalar(eki[:, :], ekf[:, :], float(E - 1), None, ALU.min).then_inc(r_experts, 1)
            link(dve.tensor_scalar(beyond[:, :], table[:, 0], 0.0, float(2 * NT), ALU.is_equal, ALU.mult))
            dve.tensor_tensor(sidx[:, :], slot_token[:, :], beyond[:, :], ALU.add).then_inc(r_index, 1)

            def weights(k, u, e):
                if not before(k, 2):
                    dve.wait_ge(f_lin_units, k - 1)
                dve.tensor_copy(w1t[:, u, 0:F], w1s[:, e, 0:F]).then_inc(f_lin_weights, 1)

            def gated(k, u, e):
                dve.wait_ge(f_lin_units, k + 1)
                dve.wait_ge(f_gelu, k + 1)
                if not before(k, 2):
                    dve.wait_ge(f_result, k - 1)
                for c in range(FT):
                    part = slice(c * P, (c + 1) * P)
                    last = dve.scalar_tensor_tensor(out=gg[:, u, part], in0=PS[:, 1 + 2 * u, part],
                                                    scalar=b1c[:, bass.ds(e * 2 * FT + c, 1)], in1=g2[:, u, part],
                                                    op0=ALU.add, op1=ALU.mult)
                last.then_inc(f_gated, 1)

            def result(k, u, e):
                dve.wait_ge(f_result, k + 1)
                if not before(k, 2):
                    dve.wait_ge(f_scaled, k - 1)
                dve.tensor_tensor(yb[:, u], PS[:, 6 + u, 0:P], b2b[:, e, :], ALU.add).then_inc(f_biased, 1)
                dve.wait_ge(f_biased, k + 1)
                if not before(k, 2):
                    dve.wait_ge(added[u], 8 * (k - u))
                dve.tensor_scalar(ys[:, u], yb[:, u], gk[:, bass.ds(k * E + e, 1)], None, ALU.mult).then_inc(f_scaled, 1)

            def keep_gates(k, u):
                dve.wait_ge(gathered[u], 8 * (k - u) + 16)
                dve.tensor_copy(gk[:, bass.ds(k * E, E)], xg[:, u, D:]).then_inc(f_gates_kept, 1)

            def expert_tile(k, u, last=False):
                back = 0 if before(k, 2) else 2
                e = experts(dve, k - back, back + (1 if last else 2))
                if not last:
                    weights(k + 1, 1 - u, e[-1])
                    keep_gates(k + 1, 1 - u)
                if not before(k, 2):
                    result(k - 2, u, e[0])
                gated(k, u, e[-1] if last else e[-2])

            dve.wait_ge(r_experts, 1)
            dve.wait_ge(w2_loaded, 16 * E)
            dve.wait_ge(w1_loaded, 16 * E)
            weights(0, 0, *experts(dve, 0))
            keep_gates(0, 0)
            tiles(dve, KT - 1, 2, expert_tile)
            expert_tile(KT - 1, (KT - 1) % 2, last=True)
            dve.wait_ge(f_gates_kept, KT)
            for k in range(KT - 2, KT):
                result(k, k % 2, *experts(dve, k))

            def last_stats(q):
                dve.wait_ge(o_sum, q + 1)
                for t in range(q * QT, (q + 1) * QT):
                    last = dve.bn_stats(st[:, t], x2[:, t])
                link(last)
                moments(q * QT, (q + 1) * QT).then_inc(ln_moments, 1)

            def last_norm(q):
                part = slice(q * QT, (q + 1) * QT)
                inverse_deviations(q + 6, q * QT, (q + 1) * QT)
                dve.scalar_tensor_tensor(out=shift[:, part], in0=mv[:, part, 0], scalar=-1.0, in1=rstd[:, part],
                                         op0=ALU.mult, op1=ALU.mult).then_inc(ln_shift, 1)
                for t in range(q * QT, q * QT + rows_here(q)):
                    last = dve.tensor_scalar(wide[:, 0, t], x2[:, t], mv[:, t, 0:1], rstd[:, t:t + 1], ALU.subtract,
                                             ALU.mult)
                last.then_inc(o_rows_dve, 1)

            last_stats(0)
            for q in range(1, PAIRS // QT):
                last_stats(q)
                last_norm(q - 1)
            last_norm(PAIRS // QT - 1)


def kernel(**inputs):
    import numpy as np
    import concourse.bacc as bacc
    from concourse.bass_utils import run_bass_kernel_spmd

    given = {n: np.ascontiguousarray(v) for n, v in inputs.items()}
    B, T, D = given["x"].shape
    given["xT"] = given["x"].reshape(B // 2, 2, T, D).transpose(3, 0, 1, 2)
    given["wqT"] = given["L0_attn_Wq"].T
    given["wkT"] = given["L0_attn_Wk"].T
    given["wvT"] = given["L0_attn_Wv"].T
    given["woT"] = given["L0_attn_Wo"].T
    given["projT"] = given["L0_attn_proj"].transpose(0, 2, 1).reshape(D, -1)
    given["wsimT"] = given["L0_xattn_w_sim"].reshape(3, D).T
    given["b1T"] = given["L0_ffn_b1"].reshape(-1, D).T
    for n in ("L0_ffn_b1", "L0_attn_Wv", "L0_attn_Wo", "L0_attn_proj"):
        del given[n]
    nc = bacc.Bacc("TRN2", target_bir_lowering=False, num_devices=1)
    arrays, aps = {}, {}
    for n, v in given.items():
        v = np.ascontiguousarray(v)
        arrays["in_" + n] = v
        aps[n] = nc.dram_tensor("in_" + n, v.shape, mybir.dt.from_np(v.dtype), kind="ExternalInput").ap()
    out = nc.dram_tensor("out_0", (B, T, D), mybir.dt.float32, kind="ExternalOutput").ap()
    build(nc, aps, out)
    return run_bass_kernel_spmd(nc, [arrays], core_ids=[0]).results[0]["out_0"]
```
